# Optimizing a Trainium2 kernel written in Bass

```python
import numpy as np
import jax
import jax.numpy as jnp

def _softmax(x, axis=-1):
    return jax.nn.softmax(x, axis=axis)

def _gelu(x):
    return jax.nn.gelu(x, approximate=True)

def _silu(x):
    return jax.nn.silu(x)

def _sigmoid(x):
    return jax.nn.sigmoid(x)

def _layernorm(x, axis=-1, eps=1e-05):
    m = jnp.mean(x, axis=axis, keepdims=True)
    v = jnp.var(x, axis=axis, keepdims=True)
    return (x - m) / jnp.sqrt(v + eps)

def _scatter_add(tgt, idx, src, axis=0):
    return tgt.at[idx].add(src)

def _segment_sum(src, seg, n):
    return jax.ops.segment_sum(src, seg, n)
kernel_name = 'mk_early_fusion_embed_d1_tok_img256_r4_35f27a'

def setup_inputs(seed: int=0):
    np.random.seed(seed)
    _w = jnp.asarray

    def _rec_inputs():
        import jax
        import jax.numpy as jnp
        _rk = jax.random.key(seed)
        x = -0.000596345 + 1.00056 * jax.random.normal(jax.random.fold_in(_rk, 1), (8, 64, 64, 3), jnp.float32)
        x_txt = jax.random.randint(jax.random.fold_in(_rk, 51), (8, 512), 0, 64, jnp.int32)
        fside_BS_continuous_positions = jax.random.uniform(jax.random.fold_in(_rk, 71), (8, 512), jnp.float32, 0.0, 0.999927)
        return (x, x_txt, fside_BS_continuous_positions)
    x, x_txt, fside_BS_continuous_positions = _rec_inputs()

    def _L0_tok_setup():
        import jax, jax.numpy as jnp
        import numpy as np
        M1, M2, WIDTH, LAYERS = (16, 16, 64, 4)
        B, H, W = (16, 64, 64)
        EPS = 1e-05

        def _spectral_conv(h, w1, w2):
            xf = jnp.fft.rfft2(h)
            top = jnp.einsum('bixy,ioxy->boxy', xf[:, :, :M1, :M2], w1)
            bot = jnp.einsum('bixy,ioxy->boxy', xf[:, :, -M1:, :M2], w2)
            of = jnp.zeros(xf.shape, dtype=xf.dtype)
            of = of.at[:, :, :M1, :M2].set(top)
            of = of.at[:, :, -M1:, :M2].set(bot)
            return jnp.fft.irfft2(of, s=(h.shape[-2], h.shape[-1]))
        key = jax.random.key(seed)
        ks = jax.random.split(key, 16)
        scale = 1.0 / (WIDTH * WIDTH)
        inp = {'x': jax.random.normal(ks[0], (B, H, W, 3), dtype=jnp.float32), 'fc0_w': jax.random.normal(ks[1], (3, WIDTH), dtype=jnp.float32) * 0.3, 'fc0_b': jnp.zeros((WIDTH,), jnp.float32), 'w1r': jax.random.normal(ks[2], (LAYERS, WIDTH, WIDTH, M1, M2), dtype=jnp.float32) * scale, 'w1i': jax.random.normal(ks[3], (LAYERS, WIDTH, WIDTH, M1, M2), dtype=jnp.float32) * scale, 'w2r': jax.random.normal(ks[4], (LAYERS, WIDTH, WIDTH, M1, M2), dtype=jnp.float32) * scale, 'w2i': jax.random.normal(ks[5], (LAYERS, WIDTH, WIDTH, M1, M2), dtype=jnp.float32) * scale, 'pw_w': jax.random.normal(ks[6], (LAYERS, WIDTH, WIDTH), dtype=jnp.float32) * (1.0 / np.sqrt(WIDTH)), 'pw_b': jnp.zeros((LAYERS, WIDTH), jnp.float32), 'gamma': jnp.ones((LAYERS, WIDTH), jnp.float32), 'beta': jnp.zeros((LAYERS, WIDTH), jnp.float32), 'fc1_w': jax.random.normal(ks[7], (WIDTH, 128), dtype=jnp.float32) * (1.0 / np.sqrt(WIDTH)), 'fc1_b': jnp.zeros((128,), jnp.float32), 'fc2_w': jax.random.normal(ks[8], (128, 1), dtype=jnp.float32) * (1.0 / np.sqrt(128.0)), 'fc2_b': jnp.zeros((1,), jnp.float32)}
        return inp
    _L0_tok_all = _L0_tok_setup()
    _L0_tok_in = {k: v for k, v in _L0_tok_all.items() if k in ('fc0_w', 'fc0_b', 'w1r', 'w1i', 'w2r', 'w2i', 'pw_w', 'pw_b', 'gamma', 'beta', 'fc1_w', 'fc1_b', 'fc2_w', 'fc2_b')}
    del _L0_tok_all

    def _L0_txt_setup():
        import jax, jax.numpy as jnp
        import numpy as np
        N_SCALES = 4

        def _conv1d(x, w, b, pad):
            y = jax.lax.conv_general_dilated(x, w, window_strides=(1,), padding=[(pad, pad)], dimension_numbers=('NCH', 'OIH', 'NCH'))
            return y + b[None, :, None]
        key = jax.random.key(seed)
        ks = jax.random.split(key, 12)
        B, S, P, D = (8, 512, 512, 64)
        byte_sequence = jax.random.randint(ks[0], (B, S), 0, 64, dtype=jnp.int64)
        continuous_positions = jax.random.uniform(ks[1], (B, P), dtype=jnp.float32)
        emb = jax.random.normal(ks[2], (64, D), dtype=jnp.float32)
        locality_shapes = jax.random.normal(ks[3], (64, 4), dtype=jnp.float32)
        w1 = jax.random.normal(ks[4], (128, 64, 7), dtype=jnp.float32) * 0.02
        b1 = jnp.zeros((128,), dtype=jnp.float32)
        w2 = jax.random.normal(ks[5], (64, 128, 5), dtype=jnp.float32) * 0.02
        b2 = jnp.zeros((64,), dtype=jnp.float32)
        w3 = jax.random.normal(ks[6], (1, 64, 3), dtype=jnp.float32) * 0.02
        b3 = jnp.zeros((1,), dtype=jnp.float32)
        multiscale_widths = jnp.array([0.01, 0.02, 0.05, 0.1], dtype=jnp.float32)
        scale_weights = jnp.ones((4,), dtype=jnp.float32)
        return {'byte_sequence': byte_sequence, 'continuous_positions': continuous_positions, 'emb': emb, 'locality_shapes': locality_shapes, 'w1': w1, 'b1': b1, 'w2': w2, 'b2': b2, 'w3': w3, 'b3': b3, 'multiscale_widths': multiscale_widths, 'scale_weights': scale_weights}
    _L0_txt_all = _L0_txt_setup()
    _L0_txt_in = {k: v for k, v in _L0_txt_all.items() if k in ('emb', 'locality_shapes', 'w1', 'b1', 'w2', 'b2', 'w3', 'b3', 'multiscale_widths', 'scale_weights')}
    del _L0_txt_all

    def _L0_attn_setup():
        import jax, jax.numpy as jnp
        import numpy as np
        P = 64
        H = 64
        BATCH = 8
        L = 1024

        def _binary_operator(q_i, q_j):
            (iA, iB, iC, iD), (ib1, ib2) = q_i
            (jA, jB, jC, jD), (jb1, jb2) = q_j
            A_new = jA * iA + jB * iC
            B_new = jA * iB + jB * iD
            C_new = jC * iA + jD * iC
            D_new = jC * iB + jD * iD
            nb1 = jA * ib1 + jB * ib2 + jb1
            nb2 = jC * ib1 + jD * ib2 + jb2
            return ((A_new, B_new, C_new, D_new), (nb1, nb2))
        key = jax.random.key(seed)
        ks = jax.random.split(key, 7)
        std_B = 1.0 / np.sqrt(H)
        std_C = 1.0 / np.sqrt(P)
        return {'input_sequence': jax.random.normal(ks[0], (BATCH, L, H), dtype=jnp.float32), 'A_diag': jax.random.uniform(ks[1], (P,), dtype=jnp.float32), 'G_diag': jax.random.uniform(ks[2], (P,), dtype=jnp.float32), 'dt': jax.random.normal(ks[3], (P,), dtype=jnp.float32) * 0.5, 'Bmat': jax.random.uniform(ks[4], (P, H, 2), dtype=jnp.float32, minval=-std_B, maxval=std_B), 'Cmat': jax.random.uniform(ks[5], (H, P, 2), dtype=jnp.float32, minval=-std_C, maxval=std_C), 'D': jax.random.normal(ks[6], (H,), dtype=jnp.float32)}
    _L0_attn_all = _L0_attn_setup()
    _L0_attn_in = {k: v for k, v in _L0_attn_all.items() if k in ('A_diag', 'G_diag', 'dt', 'Bmat', 'Cmat', 'D')}
    del _L0_attn_all

    def _L0_ffn_setup():
        import jax, jax.numpy as jnp
        import numpy as np
        E, D, H, TOP_K = (6, 64, 64, 2)
        ROUTER_H = D // 2
        key = jax.random.key(seed)
        ks = jax.random.split(key, 12)
        s = 1.0 / np.sqrt(D)
        sh = 1.0 / np.sqrt(H)
        sr = 1.0 / np.sqrt(ROUTER_H)
        return {'features': jax.random.normal(ks[0], (8, 1024, D), dtype=jnp.float32), 'router_w1': jax.random.uniform(ks[1], (D, ROUTER_H), jnp.float32, -s, s), 'router_b1': jnp.zeros((ROUTER_H,), jnp.float32), 'router_w2': jax.random.uniform(ks[2], (ROUTER_H, E), jnp.float32, -sr, sr), 'router_b2': jnp.zeros((E,), jnp.float32), 'expert_w1': jax.random.uniform(ks[3], (E, D, H), jnp.float32, -s, s), 'expert_b1': jnp.zeros((E, H), jnp.float32), 'expert_w2': jax.random.uniform(ks[4], (E, H, H), jnp.float32, -sh, sh), 'expert_b2': jnp.zeros((E, H), jnp.float32), 'expert_w3': jax.random.uniform(ks[5], (E, H, D), jnp.float32, -sh, sh), 'expert_b3': jnp.zeros((E, D), jnp.float32)}
    _L0_ffn_all = _L0_ffn_setup()
    _L0_ffn_in = {k: v for k, v in _L0_ffn_all.items() if k in ('router_w1', 'router_b1', 'router_w2', 'router_b2', 'expert_w1', 'expert_b1', 'expert_w2', 'expert_b2', 'expert_w3', 'expert_b3')}
    del _L0_ffn_all
    return {'x': x, 'x_txt': x_txt, 'fside_BS_continuous_positions': fside_BS_continuous_positions, 'L0_tok_fc0_w': _L0_tok_in['fc0_w'], 'L0_tok_fc0_b': _L0_tok_in['fc0_b'], 'L0_tok_w1r': _L0_tok_in['w1r'], 'L0_tok_w1i': _L0_tok_in['w1i'], 'L0_tok_w2r': _L0_tok_in['w2r'], 'L0_tok_w2i': _L0_tok_in['w2i'], 'L0_tok_pw_w': _L0_tok_in['pw_w'], 'L0_tok_pw_b': _L0_tok_in['pw_b'], 'L0_tok_gamma': _L0_tok_in['gamma'], 'L0_tok_beta': _L0_tok_in['beta'], 'L0_tok_fc1_w': _L0_tok_in['fc1_w'], 'L0_tok_fc1_b': _L0_tok_in['fc1_b'], 'L0_tok_fc2_w': _L0_tok_in['fc2_w'], 'L0_tok_fc2_b': _L0_tok_in['fc2_b'], 'L0_txt_emb': _L0_txt_in['emb'], 'L0_txt_locality_shapes': _L0_txt_in['locality_shapes'], 'L0_txt_w1': _L0_txt_in['w1'], 'L0_txt_b1': _L0_txt_in['b1'], 'L0_txt_w2': _L0_txt_in['w2'], 'L0_txt_b2': _L0_txt_in['b2'], 'L0_txt_w3': _L0_txt_in['w3'], 'L0_txt_b3': _L0_txt_in['b3'], 'L0_txt_multiscale_widths': _L0_txt_in['multiscale_widths'], 'L0_txt_scale_weights': _L0_txt_in['scale_weights'], 'L0_attn_A_diag': _L0_attn_in['A_diag'], 'L0_attn_G_diag': _L0_attn_in['G_diag'], 'L0_attn_dt': _L0_attn_in['dt'], 'L0_attn_Bmat': _L0_attn_in['Bmat'], 'L0_attn_Cmat': _L0_attn_in['Cmat'], 'L0_attn_D': _L0_attn_in['D'], 'L0_ffn_router_w1': _L0_ffn_in['router_w1'], 'L0_ffn_router_b1': _L0_ffn_in['router_b1'], 'L0_ffn_router_w2': _L0_ffn_in['router_w2'], 'L0_ffn_router_b2': _L0_ffn_in['router_b2'], 'L0_ffn_expert_w1': _L0_ffn_in['expert_w1'], 'L0_ffn_expert_b1': _L0_ffn_in['expert_b1'], 'L0_ffn_expert_w2': _L0_ffn_in['expert_w2'], 'L0_ffn_expert_b2': _L0_ffn_in['expert_b2'], 'L0_ffn_expert_w3': _L0_ffn_in['expert_w3'], 'L0_ffn_expert_b3': _L0_ffn_in['expert_b3']}

def reference(x, x_txt, fside_BS_continuous_positions, L0_tok_fc0_w, L0_tok_fc0_b, L0_tok_w1r, L0_tok_w1i, L0_tok_w2r, L0_tok_w2i, L0_tok_pw_w, L0_tok_pw_b, L0_tok_gamma, L0_tok_beta, L0_tok_fc1_w, L0_tok_fc1_b, L0_tok_fc2_w, L0_tok_fc2_b, L0_txt_emb, L0_txt_locality_shapes, L0_txt_w1, L0_txt_b1, L0_txt_w2, L0_txt_b2, L0_txt_w3, L0_txt_b3, L0_txt_multiscale_widths, L0_txt_scale_weights, L0_attn_A_diag, L0_attn_G_diag, L0_attn_dt, L0_attn_Bmat, L0_attn_Cmat, L0_attn_D, L0_ffn_router_w1, L0_ffn_router_b1, L0_ffn_router_w2, L0_ffn_router_b2, L0_ffn_expert_w1, L0_ffn_expert_b1, L0_ffn_expert_w2, L0_ffn_expert_b2, L0_ffn_expert_w3, L0_ffn_expert_b3):
    import jax
    import jax.numpy as jnp

    def _L0_tok_ref(x, fc0_w, fc0_b, w1r, w1i, w2r, w2i, pw_w, pw_b, gamma, beta, fc1_w, fc1_b, fc2_w, fc2_b):
        import jax, jax.numpy as jnp
        import numpy as np
        M1, M2, WIDTH, LAYERS = (16, 16, 64, 4)
        B, H, W = (16, 64, 64)
        EPS = 1e-05

        def _spectral_conv(h, w1, w2):
            xf = jnp.fft.rfft2(h)
            top = jnp.einsum('bixy,ioxy->boxy', xf[:, :, :M1, :M2], w1)
            bot = jnp.einsum('bixy,ioxy->boxy', xf[:, :, -M1:, :M2], w2)
            of = jnp.zeros(xf.shape, dtype=xf.dtype)
            of = of.at[:, :, :M1, :M2].set(top)
            of = of.at[:, :, -M1:, :M2].set(bot)
            return jnp.fft.irfft2(of, s=(h.shape[-2], h.shape[-1]))
        h = jnp.einsum('bhwi,ic->bhwc', x, fc0_w) + fc0_b
        h = h.transpose(0, 3, 1, 2)
        for l in range(LAYERS):
            sc = _spectral_conv(h, w1r[l] + 1j * w1i[l], w2r[l] + 1j * w2i[l])
            pw = jnp.einsum('bihw,oi->bohw', h, pw_w[l]) + pw_b[l][None, :, None, None]
            y = sc + pw
            mean = y.mean(axis=(0, 2, 3), keepdims=True)
            var = y.var(axis=(0, 2, 3), keepdims=True)
            y = (y - mean) * jax.lax.rsqrt(var + EPS)
            y = y * gamma[l][None, :, None, None] + beta[l][None, :, None, None]
            h = jax.nn.gelu(y, approximate=False)
        h = h.transpose(0, 2, 3, 1)
        h = jax.nn.gelu(h @ fc1_w + fc1_b, approximate=False)
        out = (h @ fc2_w + fc2_b).squeeze(-1)
        return out

    def _L0_txt_ref(byte_sequence, continuous_positions, emb, locality_shapes, w1, b1, w2, b2, w3, b3, multiscale_widths, scale_weights):
        import jax, jax.numpy as jnp
        import numpy as np
        N_SCALES = 4

        def _conv1d(x, w, b, pad):
            y = jax.lax.conv_general_dilated(x, w, window_strides=(1,), padding=[(pad, pad)], dimension_numbers=('NCH', 'OIH', 'NCH'))
            return y + b[None, :, None]
        B, S = byte_sequence.shape
        P = continuous_positions.shape[1]
        amps = emb[byte_sequence]
        onehot = jax.nn.one_hot(byte_sequence, 64, dtype=jnp.float32)
        onehot = jnp.transpose(onehot, (0, 2, 1))
        h = jax.nn.gelu(_conv1d(onehot, w1, b1, 3), approximate=False)
        h = jax.nn.gelu(_conv1d(h, w2, b2, 2), approximate=False)
        ctx = jax.nn.sigmoid(_conv1d(h, w3, b3, 1))[:, 0, :]
        amps = amps * ctx[:, :, None]
        lp = locality_shapes[byte_sequence]
        byte_pos = jnp.linspace(0.0, 1.0, S, dtype=jnp.float32)
        center = byte_pos[None, :] + lp[..., 0] * 0.05
        xd = continuous_positions[:, None, :] - center[..., None]
        amp_scale = jax.nn.sigmoid(lp[..., 2])
        phase = lp[..., 3] * jnp.pi
        abs_w = jnp.abs(lp[..., 1])
        TWO_PI = 2.0 * jnp.pi
        basis_total = jnp.zeros((B, S, P), dtype=jnp.float32)
        for s in range(N_SCALES):
            width = abs_w * multiscale_widths[s] + 1e-05
            z = xd / width[..., None]
            basis = jnp.exp(-0.5 * z * z) * jnp.cos(phase[..., None] + TWO_PI * z)
            basis_total = basis_total + basis * (amp_scale[..., None] * scale_weights[s] ** 2)
        semantic_field = jnp.einsum('bsp,bsd->bpd', basis_total, amps)
        return semantic_field

    def _L0_attn_ref(input_sequence, A_diag, G_diag, dt, Bmat, Cmat, D):
        import jax, jax.numpy as jnp
        import numpy as np
        P = 64
        H = 64
        BATCH = 8
        L = 1024

        def _binary_operator(q_i, q_j):
            (iA, iB, iC, iD), (ib1, ib2) = q_i
            (jA, jB, jC, jD), (jb1, jb2) = q_j
            A_new = jA * iA + jB * iC
            B_new = jA * iB + jB * iD
            C_new = jC * iA + jD * iC
            D_new = jC * iB + jD * iD
            nb1 = jA * ib1 + jB * ib2 + jb1
            nb2 = jC * ib1 + jD * ib2 + jb2
            return ((A_new, B_new, C_new, D_new), (nb1, nb2))
        dt_s = jax.nn.sigmoid(dt)
        G_low = dt_s * A_diag
        G = G_low + jax.nn.relu(G_diag - G_low)
        A_low = 0.25 * G ** 2
        A = A_low + jax.nn.relu(A_diag - A_low)
        B_c = Bmat[..., 0] + 1j * Bmat[..., 1]
        C_c = Cmat[..., 0] + 1j * Cmat[..., 1]
        Bu = jnp.einsum('blh,ph->blp', input_sequence.astype(B_c.dtype), B_c)
        bshape = Bu.shape
        m11 = jnp.broadcast_to(1.0 - dt_s * G, bshape).astype(jnp.float32)
        m12 = jnp.broadcast_to(-dt_s * A, bshape).astype(jnp.float32)
        m21 = jnp.broadcast_to(dt_s * jnp.ones_like(A), bshape).astype(jnp.float32)
        m22 = jnp.broadcast_to(jnp.ones_like(A), bshape).astype(jnp.float32)
        f1 = dt_s * Bu
        f2 = jnp.zeros_like(f1)
        elems = ((m11, m12, m21, m22), (f1, f2))
        _, (_, xs2) = jax.lax.associative_scan(_binary_operator, elems, axis=1)
        ys = xs2
        out = jnp.einsum('blp,hp->blh', ys, C_c).real + D * input_sequence
        return out.astype(jnp.float32)

    def _L0_ffn_ref(features, router_w1, router_b1, router_w2, router_b2, expert_w1, expert_b1, expert_w2, expert_b2, expert_w3, expert_b3):
        import jax, jax.numpy as jnp
        import numpy as np
        E, D, H, TOP_K = (6, 64, 64, 2)
        ROUTER_H = D // 2
        rh = jax.nn.relu(features @ router_w1 + router_b1)
        expert_logits = jax.nn.softmax(rh @ router_w2 + router_b2, axis=-1)
        top_w, top_i = jax.lax.top_k(expert_logits, TOP_K)
        routing_weights = jax.nn.softmax(top_w, axis=-1)
        h1 = jax.nn.relu(jnp.einsum('bsd,edh->bseh', features, expert_w1) + expert_b1)
        h2 = jax.nn.relu(jnp.einsum('bseh,ehf->bsef', h1, expert_w2) + expert_b2)
        expert_out = jnp.einsum('bsef,efo->bseo', h2, expert_w3) + expert_b3
        sel = jnp.take_along_axis(expert_out, top_i[:, :, :, None], axis=2)
        combined = jnp.sum(sel * routing_weights[..., None], axis=2)
        return combined
    h = _L0_tok_ref(x, L0_tok_fc0_w, L0_tok_fc0_b, L0_tok_w1r, L0_tok_w1i, L0_tok_w2r, L0_tok_w2i, L0_tok_pw_w, L0_tok_pw_b, L0_tok_gamma, L0_tok_beta, L0_tok_fc1_w, L0_tok_fc1_b, L0_tok_fc2_w, L0_tok_fc2_b)
    h = jnp.concatenate([h, _L0_txt_ref(x_txt, fside_BS_continuous_positions, L0_txt_emb, L0_txt_locality_shapes, L0_txt_w1, L0_txt_b1, L0_txt_w2, L0_txt_b2, L0_txt_w3, L0_txt_b3, L0_txt_multiscale_widths, L0_txt_scale_weights)], axis=1)
    h = h + _L0_attn_ref(_layernorm(h, axis=-1), L0_attn_A_diag, L0_attn_G_diag, L0_attn_dt, L0_attn_Bmat, L0_attn_Cmat, L0_attn_D)
    h = h + _L0_ffn_ref(_layernorm(h, axis=-1), L0_ffn_router_w1, L0_ffn_router_b1, L0_ffn_router_w2, L0_ffn_router_b2, L0_ffn_expert_w1, L0_ffn_expert_b1, L0_ffn_expert_w2, L0_ffn_expert_b2, L0_ffn_expert_w3, L0_ffn_expert_b3)
    return h

_drawn_inputs = setup_inputs


def setup_inputs(seed=0):
    import zlib

    import numpy as np

    out = dict(_drawn_inputs(seed))
    spreads = {'L0_tok_fc0_b': (0.0, 2.0),
     'L0_tok_pw_b': (0.0, 2.0),
     'L0_tok_gamma': (1.0, 0.2),
     'L0_tok_beta': (0.0, 0.1),
     'L0_tok_fc1_b': (0.0, 0.368),
     'L0_txt_b1': (0.0, 0.8),
     'L0_txt_b2': (0.0, 0.8),
     'L0_txt_scale_weights': (1.0, 0.2),
     'L0_ffn_router_b1': (0.0, 0.607),
     'L0_ffn_router_b2': (0.0, 0.411),
     'L0_ffn_expert_b1': (0.0, 0.8),
     'L0_ffn_expert_b2': (0.0, 0.8),
     'L0_ffn_expert_b3': (0.0, 0.392)}
    factors = {'L0_tok_w1r': 44.486,
     'L0_tok_w1i': 42.815,
     'L0_tok_w2r': 58.871,
     'L0_tok_w2i': 43.565,
     'L0_txt_w1': 8.0,
     'L0_txt_w2': 8.0,
     'L0_txt_w3': 8.0,
     'L0_ffn_expert_w1': 3.476,
     'L0_ffn_expert_w2': 2.985}
    for name, (base, spread) in spreads.items():
        noise = np.random.default_rng([zlib.crc32(name.encode()), seed]).standard_normal(out[name].shape)
        drawn = base * np.exp(spread * noise) if base else spread * noise
        out[name] = jnp.asarray(drawn.astype(out[name].dtype))
    for name, factor in factors.items():
        out[name] = (out[name] * factor).astype(out[name].dtype)
    return out
```

```python
from contextlib import ExitStack

import concourse.bass as bass
from concourse import mybir
import numpy as np

F32 = mybir.dt.float32
I32 = mybir.dt.int32
ALU = mybir.AluOpType
ACT = mybir.ActivationFunctionType
AX_X = mybir.AxisListType.X

P = 128
B, BP = 8, 4
X = Y = 64
C = D = 64
LAYERS = 4
KX, KY = 32, 16
PX = X * Y
NPAIR = X // 2
S = 512
ST = S // P
SCALES = 4
L = X + S
TILES = B * L // P
TT = B * ST
T = 32
CH = L // T
E, EP = 6, 3
EPS = 1e-5
TWO_PI_IN = 2 * np.pi * (1 - 2.0 ** -21)
NW = 4


COLS = [("ident", 128), ("dft_y", 64), ("dft_x", 128), ("idft_x", 128), ("idft_y", 256), ("swap", 128),
        ("fc0", 128), ("fc0_b", 1), ("fc1", 128), ("fc1_b", 1), ("fc2", 15), ("fc2_b", 1),
        ("cw1", 512), ("cb1", 1), ("cw2", 320), ("cb2", 1), ("cw3", 3), ("cb3", 1), ("emb", 68),
        ("vocab", 1), ("bytepos", ST), ("widths", SCALES), ("swts", SCALES), ("agd", 3), ("eye2", 64),
        ("bmat", 256), ("cmat", 128), ("dvec", 64), ("rw1", 32), ("rb1", 1), ("rw2", 6),
        ("ew1", 384), ("eb1", 3), ("ew2", 384), ("eb2", 3), ("ew3", 192), ("eb3", 64), ("sel", 384)]
AT, _n = {}, 0
for _name, _w in COLS:
    AT[_name] = (_n, _n + _w)
    _n += _w
CW = _n


def build_program(nc, xs, toks, pos, consts, lconst, wspec, out):
    nc.disable_value_cache = True
    with ExitStack() as ctx:
        def sb(name, shape, dt=F32):
            return ctx.enter_context(nc.sbuf_tensor(name, shape, dt))

        def sem(name):
            return ctx.enter_context(nc.semaphore(name))

        hbuf = sb("hbuf", [P, BP, PX])
        abuf = sb("abuf", [P, 16, B * C])
        spec = sb("spec", [P, KY, 2 * KX, B])
        wring = sb("wring", [P, NW, KX * C])
        stage = sb("stage", [P, 10 * 512])
        tok = sb("tok", [P, TILES, D])
        cst = sb("cst", [P, CW])
        lcst = sb("lcst", [P, 131])
        stats = sb("stats", [P, 32, 6])
        bn = sb("bn", [P, 16])
        banks = [ctx.enter_context(nc.psum_tensor(f"bank{i}", [P, 512], F32)) for i in range(8)]
        zdram = nc.dram_tensor("zdram", (4, 8, 4, 16, 64), F32).ap()

        xt = [stage[:, 512 * i:512 * (i + 1)] for i in range(2)]
        af = [stage[:, 512 * (2 + i):512 * (3 + i)] for i in range(4)]
        zs = [stage[:, 512 * i:512 * (i + 1)] for i in range(2)]
        z2 = [stage[0:64, 512 * (2 + i):512 * (3 + i)] for i in range(4)]
        ys = [stage[:, 512 * (6 + i):512 * (7 + i)] for i in range(4)]

        def c(name, rows=slice(0, P), lo=0, n=None):
            a, b = AT[name]
            return cst[rows, a + lo:(b if n is None else a + lo + n)]

        const_in = sem("const_in")
        toks_in = sem("toks_in"); onehot = sem("onehot"); pad0 = sem("pad0")
        conv1_mm = sem("conv1_mm"); conv1_act = sem("conv1_act"); conv2_mm = sem("conv2_mm")
        conv2_act = sem("conv2_act"); ctx_mm = sem("ctx_mm"); emb_mm = sem("emb_mm"); emb_out = sem("emb_out")
        tvec = sem("tvec"); tact = sem("tact")
        pos_in = sem("pos_in"); zk = sem("zk"); zsq = sem("zsq"); expd = sem("expd"); sind = sem("sind")
        basis = sem("basis"); field_mm = sem("field_mm"); field_out = sem("field_out"); vch = sem("vch")
        x_in = sem("x_in"); fc0_mm = sem("fc0_mm"); h_ready = sem("h_ready"); lc_in = sem("lc_in")
        w_in = [sem(f"w_in{i}") for i in range(NW)]
        t_mm = sem("t_mm"); xt_ready = sem("xt_ready"); f1_mm = sem("f1_mm"); af_ready = sem("af_ready")
        a_in = [sem(f"a_in{i}") for i in range(4)]
        f2_mm = sem("f2_mm"); s_act = sem("s_act"); s_dve = sem("s_dve"); mix_mm = sem("mix_mm")
        zs_ready = sem("zs_ready"); z_out = [sem(f"z_out{i}") for i in range(4)]
        z_in = [sem(f"z_in{i}") for i in range(4)]
        i1_mm = sem("i1_mm"); ys_ready = sem("ys_ready"); y_in = [sem(f"y_in{i}") for i in range(4)]
        o_mm = sem("o_mm"); o_stats = sem("o_stats"); o_act = sem("o_act"); bn_dve = sem("bn_dve")
        bn_mm = sem("bn_mm"); bn_act = sem("bn_act")
        fc1_mm = sem("fc1_mm"); fc1_act = sem("fc1_act"); fc2_mm = sem("fc2_mm"); fc0_act = sem("fc0_act"); bn_rs = sem("bn_rs"); ft_ready = sem("ft_ready")
        img_in = sem("img_in")
        ln_dve = sem("ln_dve"); ln_act = sem("ln_act"); tp_mm = sem("tp_mm"); tp_out = sem("tp_out")
        pw_mm = sem("pw_mm"); pw_out = sem("pw_out"); bu_mm = sem("bu_mm"); bu_out = sem("bu_out")
        st_mm = sem("st_mm"); st_out = sem("st_out"); cy_mm = sem("cy_mm"); cy_out = sem("cy_out")
        fx_mm = sem("fx_mm"); fx_out = sem("fx_out"); ao_mm = sem("ao_mm"); ao_out = sem("ao_out")
        tp2_mm = sem("tp2_mm"); tp2_out = sem("tp2_out")
        rh_mm = sem("rh_mm"); rh_act = sem("rh_act"); lg_mm = sem("lg_mm"); gate = sem("gate")
        gate_act = sem("gate_act"); gt_mm = sem("gt_mm"); gt_out = sem("gt_out")
        e1_mm = sem("e1_mm"); e1_act = sem("e1_act"); e2_mm = sem("e2_mm"); e2_act = sem("e2_act")
        gb_mm = sem("gb_mm"); gb_out = sem("gb_out"); e3_mm = sem("e3_mm"); res = sem("res")
        stored = sem("stored")

        ab1 = abuf[:, :, :].rearrange("p a n -> p (a n)")
        toki = ab1[:, 0:1024].bitcast(I32)
        oh = [ab1[:, 1024 + 520 * i:1024 + 520 * (i + 1)] for i in range(2)]
        g1 = [ab1[:, 2064 + 516 * i:2064 + 516 * (i + 1)] for i in range(2)]
        g2 = [ab1[0:64, 3096 + 516 * i:3096 + 516 * (i + 1)] for i in range(2)]
        sp1 = spec[:, :, :, :].rearrange("p a b c -> p (a b c)")
        embt = sp1[:, 0:TT * 68].rearrange("p (t e) -> p t e", e=68)
        amps = sp1[:, TT * 68:TT * 132].rearrange("p (t e) -> p t e", e=64)
        tv = sp1[:, TT * 132:TT * 132 + 24 * TT].rearrange("p (k t) -> p k t", t=TT)
        hb1 = hbuf[:, :, :].rearrange("p a n -> p (a n)")
        posb = hb1[:, 0:1024]
        xd = [hb1[:, 1024 + 512 * i:1536 + 512 * i] for i in range(2)]
        zz = [hb1[:, 2048 + 2048 * i:4096 + 2048 * i] for i in range(2)]
        kk = [hb1[:, 10240 + 2048 * i:12288 + 2048 * i].bitcast(I32) for i in range(2)]
        rr = [hb1[:, 6144 + 2048 * i:8192 + 2048 * i] for i in range(2)]
        ex = [hb1[:, 10240 + 2048 * i:12288 + 2048 * i] for i in range(2)]
        bas = [hb1[:, 14336 + 512 * i:14848 + 512 * i] for i in range(2)]
        xin = wring[0:6, 0:2, :].rearrange("p a n -> p (a n)")

        ut = ab1[0:64, 0:B * L]
        utb = ut.rearrange("p (b t) -> p b t", b=B)
        sx = hb1[:, 0:2 * B * L]
        sx4 = sx.rearrange("p (g c j) -> p g c j", c=CH, j=T)
        mp = hb1[:, 2 * B * L:2 * B * L + (T + 1) * P].rearrange("p (k n) -> p k n", n=P)
        cy = hb1[:, 14336:14336 + 16 * CH].rearrange("p (g c) -> p g c", c=CH)
        mrow = hb1[:, 14700:14828]
        co = hb1[:, 14832:14860]
        un = sp1[:, 0:TILES * D].rearrange("p (t d) -> p t d", d=D)
        w1 = sp1[:, 2304:4608].rearrange("p (t d) -> p t d", d=D)
        h2 = sp1[:, 4608:6912].rearrange("p (t d) -> p t d", d=D)
        lnv = sp1[:, 6912:6912 + 8 * TILES].rearrange("p (k t) -> p k t", t=TILES)
        u2t = ab1[0:64, 0:B * L]
        gtt = ab1[64:70, 0:B * L]
        wr1 = wring[:, :, :].rearrange("p a n -> p (a n)")
        lg = wr1[:, 0:216].rearrange("p (t e) -> p t e", e=E)
        pr = wr1[:, 216:432].rearrange("p (t e) -> p t e", e=E)
        gv = wr1[:, 432:432 + 216 * 6].rearrange("p (k t e) -> p k t e", k=6, e=E)
        gs = wr1[:, 1728:1728 + 12 * TILES].rearrange("p (k t) -> p k t", t=TILES)
        gates = wr1[:, 2200:2416].rearrange("p (t e) -> p t e", e=E)
        rh = [wr1[0:33, 2560 + 512 * i:3072 + 512 * i] for i in range(2)]
        hb0 = [hb1[:, 1536 * i:1536 * (i + 1)] for i in range(2)]
        hb2 = [hb1[:, 3072 + 1536 * i:3072 + 1536 * (i + 1)] for i in range(2)]
        hb3 = [hb1[:, 6144 + 1536 * i:6144 + 1536 * (i + 1)] for i in range(2)]
        w1t = wr1[:, 4096:4096 + 2304].rearrange("p (t d) -> p t d", d=D)

        def bc(v, n):
            return v.unsqueeze(2).to_broadcast([P, v.shape[1], n])

        def spectrum_parts(ky):
            src = banks[4 + ky % 2][:, :].rearrange("p (b k) -> p b k", b=BP)
            for part in range(2):
                for b2 in range(2):
                    yield (spec[64 * part:64 * part + 64, ky, :, b2::2].rearrange("p k b -> p b k"),
                           src[64 * b2:64 * b2 + 64, :, 64 * part:64 * part + 64])

        def spectrum_done(eng, l, n):
            eng.wait_ge(s_dve, 8 * l + (n + 1) // 2)
            if n > 1:
                eng.wait_ge(s_act, 8 * l + n // 2)

        block = ctx.enter_context(nc.Block())

        @block.sync
        def _(sp):
            sp.dma_start(cst[:, :], consts).then_inc(const_in, 16)
            for b in range(B):
                if b >= 2:
                    sp.wait_ge(onehot, b - 1)
                sp.dma_start(toki[:, 512 * (b % 2):512 * (b % 2 + 1)],
                             toks[b:b + 1, :].to_broadcast([P, S])).then_inc(toks_in, 16)
                if b < 7:
                    sp.wait_ge(toks_in, 16 * (b + 1))
            for b in range(B):
                if b >= 2:
                    sp.wait_ge(zk, ST * (b - 1))
                sp.dma_start(posb[:, 512 * (b % 2):512 * (b % 2 + 1)], pos[b:b + 1, :].to_broadcast([P, S])
                             ).then_inc(pos_in, 16)
                sp.wait_ge(pos_in, 16 * (b + 1))
            for bp in range(BP):
                if bp:
                    sp.wait_ge(fc0_mm, 8 * bp)
                sp.dma_start(xin, xs[bp]).then_inc(x_in, 16)
            with sp.Fori(0, LAYERS) as l:
                for g in range(16):
                    sp.wait_ge(af_ready, 16 * l + g + 1)
                    sp.dma_start(abuf[g::16, :, :].rearrange("p a n -> p (a n)"), af[g % 4]).then_inc(a_in[g % 4], 16)

                def z_read(ky):
                    sp.wait_ge(z_out[ky % 4], 64 * (4 * l + ky // 4 + 1))
                    sp.dma_start(z2[ky % 4], zdram[ky % 4].rearrange("k q (r b) o -> (k q r) (b o)", r=2)
                                 ).then_inc(z_in[ky % 4], 16)

                for ky in range(KY):
                    filled = sp.snap(16 * l + ky + 1)
                    if ky >= 4:
                        used = sp.snap(16 * l + ky - 3)
                        sp.wait_ge(i1_mm, used)
                    sp.wait_ge(zs_ready, filled)
                    for q in range(4):
                        sp.dma_start(zdram[ky % 4, :, q].rearrange("k m o -> m k o"),
                                     zs[ky % 2][32 * q:32 * q + 16, :].rearrange("m (k o) -> m k o", k=8)
                                     ).then_inc(z_out[ky % 4], 16)
                    if ky:
                        z_read(ky - 1)
                z_read(KY - 1)
            for b in range(B):
                sp.wait_ge(ft_ready, b + 1)
                sp.dma_start(tok[64 * (b % 2):64 * (b % 2) + 64, TT + b // 2, :],
                             stage[0:8, 512 * (4 + b % 2):512 * (5 + b % 2)]).then_inc(img_in, 16)
                sp.wait_ge(img_in, 16 * (b + 1))
            sp.wait_ge(res, 9)
            for b in range(B):
                sp.dma_start(out[b, X:L, :].rearrange("(t p) d -> p t d", p=P),
                             w1t[:, ST * b:ST * (b + 1), :]).then_inc(stored, 16)
                sp.dma_start(out[b, 0:X, :], w1t[64 * (b % 2):64 * (b % 2) + 64, TT + b // 2, :]).then_inc(stored, 16)
            sp.wait_ge(stored, 32 * B)

        @block.gpsimd
        def _(pool):
            for i in range(2):
                nc.gpsimd.memset(oh[i], 0.0)
                nc.gpsimd.memset(g1[i], 0.0)
                nc.gpsimd.memset(g2[i], 0.0).then_inc(pad0, 1)
            with pool.Fori(0, TT, 2) as i:
                for j in range(2):
                    pool.wait_ge(zk, i + j + 1)
                    nc.gpsimd.tensor_tensor(zz[j], zz[j], zz[j], ALU.mult).then_inc(zsq, 1)
            with pool.Fori(0, LAYERS) as l:
                for ky in range(KY):
                    if ky == NW:
                        pool.wait_ge(h_ready, 16 * l + 16)
                        pool.dma_start(lcst[:, :], lconst[bass.ds(l, 1)].rearrange("l p n -> (l p) n")).then_inc(lc_in, 16)
                    pool.wait_ge(mix_mm, 16 * l + ky + 1)
                    pool.dma_start(wring[:, ky % NW, :], wspec[bass.ds(KY * l + ky, 1)].rearrange("l p n -> (l p) n")
                                   ).then_inc(w_in[ky % NW], 16)

        @block.vector
        def _(dve):
            links = [0]

            def link(ins):
                links[0] += 1
                ins.then_inc(vch, 1)
                dve.wait_ge(vch, links[0])

            V = nc.vector
            dve.wait_ge(const_in, 16)
            dve.wait_ge(pad0, 2)
            im = c("cmat", slice(64, 128), lo=64, n=64)
            link(V.tensor_scalar(im, im, -1.0, None, ALU.mult))
            for b in range(B):
                i = b % 2
                dve.wait_ge(toks_in, 16 * (b + 1))
                if b >= 2:
                    dve.wait_ge(conv1_mm, b - 1)
                    dve.wait_ge(emb_mm, b - 1)
                t = toki[:, 512 * i:512 * (i + 1)]
                V.tensor_scalar(oh[i][0:64, 3:3 + S], t[0:64, :], c("vocab", slice(0, 64)), None, ALU.is_equal)
                V.tensor_scalar(oh[i][64:128, 2:2 + S], t[64:128, :], c("vocab", slice(64, 128)), None,
                                ALU.is_equal).then_inc(onehot, 1)
                if b >= 1:
                    dve.wait_ge(emb_mm, b)
                    V.tensor_copy(embt[:, ST * (b - 1):ST * b, :],
                                  banks[6][:, 0:ST * 68].rearrange("p (t e) -> p t e", e=68)).then_inc(emb_out, 1)
            dve.wait_ge(emb_mm, B)
            V.tensor_copy(embt[:, ST * (B - 1):ST * B, :],
                          banks[6][:, 0:ST * 68].rearrange("p (t e) -> p t e", e=68)).then_inc(emb_out, 1)
            dve.wait_ge(emb_out, B)
            lp = [embt[:, :, 64 + k] for k in range(4)]
            cen, ph, absw, amp, cxs = tv[:, 0], tv[:, 1], tv[:, 2], tv[:, 3], tv[:, 4]
            rw = [tv[:, 5 + s] for s in range(SCALES)]
            sw2 = tv[:, 10, 0:SCALES]
            link(V.tensor_scalar(tv[:, 9], lp[0], 0.05, None, ALU.mult))
            link(V.tensor_tensor(cen.rearrange("p (b t) -> p b t", t=ST), tv[:, 9].rearrange("p (b t) -> p b t", t=ST),
                                 c("bytepos").unsqueeze(1).to_broadcast([P, B, ST]), ALU.add))
            link(V.tensor_scalar(ph, lp[3], 0.5, 0.25, ALU.mult, ALU.add))
            link(V.tensor_scalar(tv[:, 11], lp[1], -1.0, None, ALU.mult))
            link(V.tensor_tensor(absw, lp[1], tv[:, 11], ALU.max))
            for s in range(SCALES):
                link(V.tensor_scalar(rw[s], absw, c("widths", lo=s, n=1), EPS, ALU.mult, ALU.add))
                link(V.reciprocal(rw[s], rw[s]))
            link(V.tensor_tensor(sw2, c("swts"), c("swts"), ALU.mult))
            dve.wait_ge(tact, 2)
            link(V.tensor_tensor(amp, cxs, tv[:, 13], ALU.mult))
            link(V.tensor_tensor(amps, embt[:, :, 0:D], bc(amp, D), ALU.mult))
            V.tensor_copy(tv[:, 14], amp).then_inc(tvec, 1)

            def product(i):
                j = i % 2
                dve.wait_ge(sind, i + 1)
                for s in range(SCALES):
                    q = slice(512 * s, 512 * (s + 1))
                    ins = V.scalar_tensor_tensor(out=ex[j][:, q], in0=ex[j][:, q], scalar=sw2[:, s:s + 1],
                                                 in1=rr[j][:, q], op0=ALU.mult, op1=ALU.mult)
                link(ins)
                link(V.tensor_tensor(ex[j][:, 0:1024], ex[j][:, 0:1024], ex[j][:, 1024:2048], ALU.add))
                if i >= 2:
                    dve.wait_ge(field_mm, i - 1)
                V.tensor_tensor(bas[j], ex[j][:, 0:512], ex[j][:, 512:1024], ALU.add).then_inc(basis, 1)

            def field(b):
                dve.wait_ge(field_mm, ST * (b + 1))
                for pt in range(ST):
                    ins = V.tensor_copy(tok[:, ST * b + pt, :], banks[4 + pt][:, 0:D])
                ins.then_inc(field_out, 1)

            for i in range(TT):
                b, st, j = i // ST, i % ST, i % 2
                if st == 0:
                    dve.wait_ge(pos_in, 16 * (b + 1))
                link(V.tensor_scalar(xd[j], posb[:, 512 * (b % 2):512 * (b % 2 + 1)], cen[:, i:i + 1], None, ALU.subtract))
                if i >= 2:
                    dve.wait_ge(expd, i - 1)
                for s in range(SCALES):
                    ins = V.tensor_scalar(zz[j][:, 512 * s:512 * (s + 1)], xd[j], rw[s][:, i:i + 1], None, ALU.mult)
                link(ins)
                link(V.tensor_scalar(rr[j], zz[j], ph[:, i:i + 1], None, ALU.add))
                link(V.tensor_copy(kk[j], rr[j]))
                V.tensor_tensor(rr[j], rr[j], kk[j], ALU.subtract).then_inc(zk, 1)
                dve.wait_ge(zk, i + 1)
                if i >= 1:
                    product(i - 1)
                    if st == 0:
                        field(b - 1)
            product(TT - 1)
            field(B - 1)

            with dve.Fori(0, LAYERS) as l:
                for xp in range(NPAIR):
                    dve.wait_ge(t_mm, 32 * l + xp + 1)
                    if xp >= 2:
                        dve.wait_ge(f1_mm, 32 * l + xp - 1)
                    V.tensor_copy(xt[xp % 2], banks[xp % 2][:, :]).then_inc(xt_ready, 1)
                for ky in range(0, KY, 2):
                    dve.wait_ge(f2_mm, 16 * l + ky + 1)
                    for dst, src in spectrum_parts(ky):
                        ins = V.tensor_copy(dst, src)
                    ins.then_inc(s_dve, 1)
                for ky in range(KY):
                    dve.wait_ge(mix_mm, 16 * l + NW + ky + 1)
                    if ky >= 2:
                        dve.wait_ge(z_out[(ky - 2) % 4], 64 * (4 * l + (ky - 2) // 4 + 1))
                    V.tensor_copy(zs[ky % 2], banks[ky % 2][:, :]).then_inc(zs_ready, 1)
                for q in range(32):
                    dve.wait_ge(o_act, 32 * l + q + 1)
                    V.bn_stats(stats[:, q, :], hbuf[:, q % BP, 512 * (q // BP):512 * (q // BP + 1)]).then_inc(o_stats, 1)
                dve.wait_ge(o_stats, 32 * l + 32)
                V.memset(bn[:, 4:5], 0.0)
                V.bn_aggr(bn[:, 0:2], stats[:, :, :]).then_inc(bn_dve, 1)
                dve.wait_ge(bn_mm, l + 1)
                m, v, om, ov = bn[:, 0:1], bn[:, 1:2], banks[0][:, 0:1], banks[0][:, 1:2]
                V.tensor_tensor(bn[:, 2:4], bn[:, 0:2], banks[0][:, 0:2], ALU.add)
                V.tensor_tensor(bn[:, 4:5], m, om, ALU.subtract).then_inc(bn_dve, 1)
                dve.wait_ge(bn_dve, 6 * l + 2)
                V.tensor_scalar(bn[:, 5:6], bn[:, 4:5], bn[:, 4:5], 0.25, ALU.mult, ALU.mult)
                V.tensor_scalar(bn[:, 6:7], bn[:, 3:4], 0.5, EPS, ALU.mult, ALU.add)
                V.tensor_scalar(bn[:, 7:8], bn[:, 2:3], 0.5, None, ALU.mult).then_inc(bn_dve, 1)
                dve.wait_ge(bn_dve, 6 * l + 3)
                V.tensor_tensor(bn[:, 8:9], bn[:, 5:6], bn[:, 6:7], ALU.add).then_inc(bn_dve, 1)
                dve.wait_ge(bn_act, l + 1)
                V.reciprocal(bn[:, 10:11], bn[:, 9:10]).then_inc(bn_dve, 1)
                dve.wait_ge(bn_dve, 6 * l + 5)
                V.tensor_tensor(bn[:, 11:12], bn[:, 10:11], lcst[:, 129:130], ALU.mult).then_inc(bn_rs, 1)
                dve.wait_ge(bn_rs, 2 * l + 1)
                V.tensor_tensor(bn[:, 12:13], bn[:, 11:12], bn[:, 7:8], ALU.mult).then_inc(bn_rs, 1)
                dve.wait_ge(bn_rs, 2 * l + 2)
                V.tensor_tensor(bn[:, 13:14], lcst[:, 130:131], bn[:, 12:13], ALU.subtract).then_inc(bn_dve, 1)

            for b in range(B):
                dve.wait_ge(fc2_mm, 8 * (b + 1))
                if b >= 2:
                    dve.wait_ge(img_in, 16 * (b - 1))
                V.tensor_scalar(stage[0:8, 512 * (4 + b % 2):512 * (5 + b % 2)], banks[4 + b % 2][0:8, :],
                                c("fc2_b", slice(0, 8)), None, ALU.add).then_inc(ft_ready, 1)

            def layer_norm(src, dst, tmp, k):
                link(V.reduce_sum(lnv[:, 0], src, AX_X))
                link(V.tensor_scalar(lnv[:, 1], lnv[:, 0], 1.0 / D, None, ALU.mult))
                link(V.tensor_tensor(dst, src, bc(lnv[:, 1], D), ALU.subtract))
                link(V.tensor_tensor(tmp, dst, dst, ALU.mult))
                link(V.reduce_sum(lnv[:, 2], tmp, AX_X))
                V.tensor_scalar(lnv[:, 3], lnv[:, 2], 1.0 / D, EPS, ALU.mult, ALU.add).then_inc(ln_dve, 1)
                dve.wait_ge(ln_act, k)
                link(V.reciprocal(lnv[:, 5], lnv[:, 4]))
                V.tensor_tensor(dst, dst, bc(lnv[:, 5], D), ALU.mult).then_inc(ln_dve, 1)
                dve.wait_ge(ln_dve, 2 * (k - 1))

            agd = c("agd")
            o = lambda i: co[:, i:i + 1]
            dve.wait_ge(ln_act, 1)
            dts = o(0)
            link(V.tensor_tensor(o(1), dts, agd[:, 0:1], ALU.mult))
            link(V.tensor_tensor(o(2), agd[:, 1:2], o(1), ALU.subtract))
            link(V.tensor_scalar(o(2), o(2), 0.0, None, ALU.max))
            link(V.tensor_tensor(o(3), o(1), o(2), ALU.add))
            link(V.tensor_tensor(o(4), o(3), o(3), ALU.mult))
            link(V.tensor_scalar(o(4), o(4), 0.25, None, ALU.mult))
            link(V.tensor_tensor(o(5), agd[:, 0:1], o(4), ALU.subtract))
            link(V.tensor_scalar(o(5), o(5), 0.0, None, ALU.max))
            link(V.tensor_tensor(o(6), o(4), o(5), ALU.add))
            link(V.tensor_tensor(o(7), dts, o(3), ALU.mult))
            link(V.tensor_scalar(o(8), o(7), -1.0, 1.0, ALU.mult, ALU.add))
            link(V.tensor_tensor(o(9), dts, o(6), ALU.mult))
            link(V.tensor_scalar(o(9), o(9), -1.0, None, ALU.mult))
            link(V.memset(co[:, 10:14], 1.0))
            lo, hi = slice(0, 64), slice(64, 128)
            for col, top, bot in ((10, 8, 9), (11, 0, None), (12, 8, 0), (13, 9, None)):
                link(V.tensor_copy(co[lo, col:col + 1], co[lo, top:top + 1]))
                if bot is not None:
                    link(V.tensor_copy(co[hi, col:col + 1], co[hi, bot:bot + 1]))
            V.tensor_scalar(mp[:, 1, 0:64], c("eye2"), o(10), None, ALU.mult)
            V.tensor_scalar(mp[:, 1, 64:128], c("eye2"), o(11), None, ALU.mult)
            V.tensor_scalar(mrow[:, 0:64], c("eye2"), o(12), None, ALU.mult)
            V.tensor_scalar(mrow[:, 64:128], c("eye2"), o(13), None, ALU.mult).then_inc(pw_out, 1)
            for k in range(2, T + 1):
                dve.wait_ge(pw_mm, k - 1)
                V.tensor_copy(mp[:, k, :], banks[7][:, 0:P]).then_inc(pw_out, 1)

            dve.wait_ge(img_in, 16 * B)
            dve.wait_ge(field_out, B)
            layer_norm(tok[:, :, :], un, w1, 2)
            link(V.tensor_tensor(w1, un, c("dvec").unsqueeze(1).to_broadcast([P, TILES, D]), ALU.mult))
            link(V.tensor_tensor(w1, w1, tok[:, :, :], ALU.add))
            for g in range(9):
                dve.wait_ge(tp_mm, g + 1)
                src = banks[g % 4][0:64, :]
                if g < 8:
                    V.tensor_copy(utb[:, g, X:L], src).then_inc(tp_out, 1)
                else:
                    V.tensor_copy(utb[:, :, 0:X], src.rearrange("p (b x) -> p b x", b=B)).then_inc(tp_out, 1)
            with dve.Fori(1, T) as j:
                dve.wait_ge(st_mm, j)
                V.tensor_tensor(sx4[:, :, :, bass.ds(j, 1)], banks[0][:, 0:288].rearrange("p (g c j) -> p g c j", g=16, j=1),
                                sx4[:, :, :, bass.ds(j, 1)], ALU.add).then_inc(st_out, 1)
            dve.wait_ge(st_out, T - 1)
            V.tensor_copy(cy[:, :, 1], sx4[:, :, 0, T - 1]).then_inc(cy_out, 1)
            for ch in range(2, CH):
                dve.wait_ge(cy_mm, ch - 1)
                V.tensor_tensor(cy[:, :, ch], banks[4][:, 0:16], sx4[:, :, ch - 1, T - 1], ALU.add).then_inc(cy_out, 1)
            for j in range(T):
                dve.wait_ge(fx_mm, j + 1)
                V.tensor_tensor(sx4[:, :, 1:CH, j], banks[j % 4][:, 0:16 * (CH - 1)].rearrange("p (g c) -> p g c", g=16),
                                sx4[:, :, 1:CH, j], ALU.add).then_inc(fx_out, 1)
            for g in range(5):
                n = min(8, TILES - 8 * g)
                dve.wait_ge(ao_mm, g + 1)
                V.tensor_tensor(h2[:, 8 * g:8 * g + n, :], banks[g][:, 0:64 * n].rearrange("p (t d) -> p t d", d=D),
                                w1[:, 8 * g:8 * g + n, :], ALU.add).then_inc(ao_out, 1)
            dve.wait_ge(ao_out, 5)
            layer_norm(h2, un, w1, 3)
            for g in range(9):
                dve.wait_ge(tp2_mm, g + 1)
                V.tensor_copy(u2t[:, 512 * g:512 * (g + 1)], banks[g % 4][0:64, :]).then_inc(tp2_out, 1)
            dve.wait_ge(lg_mm, 9)
            link(V.tensor_copy(lg, banks[6][:, 0:216].rearrange("p (t e) -> p t e", e=E)))
            mx, sm, rs, p1, p2, seen = (gs[:, k] for k in range(6))
            link(V.tensor_reduce(mx, lg, axis=AX_X, op=ALU.max))
            V.tensor_tensor(lg, lg, bc(mx, E), ALU.subtract).then_inc(gate, 1)
            dve.wait_ge(gate_act, 1)
            link(V.reduce_sum(sm, pr, AX_X))
            link(V.reciprocal(rs, sm))
            link(V.tensor_tensor(pr, pr, bc(rs, E), ALU.mult))
            cur = pr
            for rank in range(2):
                top = (p1, p2)[rank]
                eq, sel, nxt = gv[:, 3 * rank], gv[:, 3 * rank + 1], gv[:, 3 * rank + 2]
                link(V.tensor_reduce(top, cur, axis=AX_X, op=ALU.max))
                link(V.tensor_tensor(eq, cur, bc(top, E), ALU.is_equal))
                link(V.memset(seen, 0.0))
                for e in range(E):
                    link(V.tensor_tensor(sel[:, :, e], eq[:, :, e], seen, ALU.is_gt))
                    if e < E - 1:
                        link(V.tensor_tensor(seen, seen, eq[:, :, e], ALU.max))
                if rank == 0:
                    link(V.scalar_tensor_tensor(out=nxt, in0=sel, scalar=-4.0, in1=cur, op0=ALU.mult, op1=ALU.add))
                    cur = nxt
            V.tensor_tensor(gs[:, 6], p2, p1, ALU.subtract).then_inc(gate, 1)
            dve.wait_ge(gate_act, 2)
            link(V.tensor_scalar(gs[:, 8], gs[:, 7], 1.0, None, ALU.add))
            link(V.reciprocal(gs[:, 9], gs[:, 8]))
            link(V.tensor_tensor(gs[:, 10], gs[:, 7], gs[:, 9], ALU.mult))
            link(V.tensor_tensor(gv[:, 0], gv[:, 1], bc(gs[:, 9], E), ALU.mult))
            link(V.tensor_tensor(gv[:, 3], gv[:, 4], bc(gs[:, 10], E), ALU.mult))
            V.tensor_tensor(gates, gv[:, 0], gv[:, 3], ALU.add).then_inc(gate, 1)
            for g in range(9):
                dve.wait_ge(gt_mm, g + 1)
                V.tensor_copy(gtt[:, 512 * g:512 * (g + 1)], banks[7 - g % 2][0:6, :]).then_inc(gt_out, 1)
            for n in range(9):
                for k in range(EP):
                    m = EP * n + k
                    dve.wait_ge(gb_mm, m + 1)
                    if k == 0:
                        dve.wait_ge(e2_act, EP * (n + 1))
                        if n >= 2:
                            dve.wait_ge(e3_mm, n - 1)
                    V.tensor_tensor(hb3[n % 2][:, 512 * k:512 * (k + 1)], banks[4 + m % 2][:, :],
                                    hb2[n % 2][:, 512 * k:512 * (k + 1)], ALU.mult).then_inc(gb_out, 1)
                dve.wait_ge(e3_mm, n + 1)
                V.tensor_tensor(w1t[:, 4 * n:4 * n + 4, :], banks[6 + n % 2][:, 0:256].rearrange("p (t d) -> p t d", d=D),
                                h2[:, 4 * n:4 * n + 4, :], ALU.add).then_inc(res, 1)

        @block.scalar
        def _(act):
            A = nc.scalar.activation
            act.wait_ge(const_in, 16)
            act.wait_ge(pad0, 2)
            for b in range(B):
                i = b % 2
                act.wait_ge(conv1_mm, b + 1)
                if b >= 2:
                    act.wait_ge(conv2_mm, b - 1)
                A(g1[i][:, 2:2 + S], banks[i][:, :], ACT.Gelu, bias=c("cb1")).then_inc(conv1_act, 1)
                act.wait_ge(conv2_mm, b + 1)
                if b >= 2:
                    act.wait_ge(ctx_mm, b - 1)
                A(g2[i][:, 1:1 + S], banks[2 + i][0:64, :], ACT.Gelu, bias=c("cb2", slice(0, 64))).then_inc(conv2_act, 1)
            act.wait_ge(ctx_mm, B)
            act.wait_ge(emb_out, B)
            A(tv[:, 4], banks[7][:, 0:TT], ACT.Sigmoid, bias=c("cb3")).then_inc(tact, 1)
            A(tv[:, 13], embt[:, :, 66], ACT.Sigmoid).then_inc(tact, 1)
            act.wait_ge(tvec, 1)
            for i in range(TT):
                j = i % 2
                act.wait_ge(zsq, i + 1)
                if i >= 2:
                    act.wait_ge(basis, i - 1)
                A(ex[j], zz[j], ACT.Exp, scale=-0.5).then_inc(expd, 1)
                act.wait_ge(zk, i + 1)
                A(rr[j], rr[j], ACT.Sin, scale=TWO_PI_IN).then_inc(sind, 1)
            act.wait_ge(field_out, B)
            for n in range(32):
                xg, bp = n % 8, n // 8
                act.wait_ge(fc0_mm, n + 1)
                A(hbuf[:, bp, 512 * xg:512 * (xg + 1)], banks[4 + n % 4][:, :], ACT.Identity,
                  bias=c("fc0_b")).then_inc(fc0_act, 1)
            act.wait_ge(fc0_act, 32)
            nc.scalar.copy(bn[:, 14:15], c("fc0_b")).then_inc(h_ready, 16)
            nc.scalar.copy(bn[:, 15:16], c("fc0_b")).then_inc(mix_mm, NW)
            with act.Fori(0, LAYERS) as l:
                for g in range(16):
                    act.wait_ge(f1_mm, 32 * l + 2 * g + 2)
                    if g >= 4:
                        act.wait_ge(a_in[g % 4], 16 * (4 * l + g // 4))
                    A(af[g % 4], banks[2 + g % 2][:, :], ACT.Copy).then_inc(af_ready, 1)
                for ky in range(1, KY, 2):
                    act.wait_ge(f2_mm, 16 * l + ky + 1)
                    for dst, src in spectrum_parts(ky):
                        ins = A(dst, src, ACT.Copy)
                    ins.then_inc(s_act, 1)

                def y_move(ky):
                    act.wait_ge(ys_ready, 16 * l + ky + 1)
                    act.dma_start(abuf[ky::16, :, :].rearrange("p a n -> p (a n)"), ys[ky % 4]).then_inc(y_in[ky % 4], 16)

                for ky in range(KY):
                    act.wait_ge(i1_mm, 16 * l + ky + 1)
                    if ky >= 4:
                        act.wait_ge(y_in[ky % 4], 16 * (4 * l + ky // 4))
                    A(ys[ky % 4], banks[2 + ky % 2][:, :], ACT.Copy).then_inc(ys_ready, 1)
                    if ky:
                        y_move(ky - 1)
                y_move(KY - 1)
                act.wait_ge(lc_in, 16 * (l + 1))
                for q in range(32):
                    xg, bp = q // BP, q % BP
                    act.wait_ge(o_mm, 32 * l + q + 1)
                    A(hbuf[:, bp, 512 * xg:512 * (xg + 1)], banks[4 + q % 4][:, :], ACT.Identity,
                      bias=lcst[:, 128:129]).then_inc(o_act, 1)
                act.wait_ge(bn_dve, 6 * l + 4)
                A(bn[:, 9:10], bn[:, 8:9], ACT.Sqrt).then_inc(bn_act, 1)
                act.wait_ge(bn_dve, 6 * l + 6)
                act.wait_ge(o_act, 32 * l + 32)
                for g in range(16):
                    px = hbuf[:, :, 256 * g:256 * (g + 1)]
                    A(px, px, ACT.Gelu, scale=bn[:, 11:12], bias=bn[:, 13:14]).then_inc(h_ready, 1)
            for n in range(64):
                act.wait_ge(fc1_mm, n + 1)
                if n >= 4:
                    act.wait_ge(fc2_mm, n - 3)
                A(stage[:, 512 * (n % 4):512 * (n % 4 + 1)], banks[n % 4][:, :], ACT.Gelu, bias=c("fc1_b")).then_inc(fc1_act, 1)
            act.wait_ge(fc1_mm, 64)
            A(co[:, 0:1], c("agd", lo=2, n=1), ACT.Sigmoid).then_inc(ln_act, 1)
            act.wait_ge(ln_dve, 1)
            A(lnv[:, 4], lnv[:, 3], ACT.Sqrt).then_inc(ln_act, 1)
            for m in range(18):
                act.wait_ge(bu_mm, m + 1)
                A(sx[:, 512 * m:512 * (m + 1)], banks[4 + m % 2][:, :], ACT.Copy, scale=co[:, 0:1]).then_inc(bu_out, 1)
            act.wait_ge(ln_dve, 3)
            A(lnv[:, 4], lnv[:, 3], ACT.Sqrt).then_inc(ln_act, 1)
            for n in range(9):
                act.wait_ge(rh_mm, n + 1)
                if n >= 2:
                    act.wait_ge(lg_mm, n - 1)
                else:
                    nc.scalar.activation(rh[n][32:33, :], sx[32:33, 0:512], ACT.Copy, scale=0.0, bias=1.0)
                A(rh[n % 2][0:32, :], banks[4 + n % 2][0:32, :], ACT.Relu, bias=c("rb1", slice(0, 32))).then_inc(rh_act, 1)
            act.wait_ge(gate, 1)
            A(pr, lg, ACT.Exp).then_inc(gate_act, 1)
            act.wait_ge(gate, 2)
            A(gs[:, 7], gs[:, 6], ACT.Exp).then_inc(gate_act, 1)
            for n in range(9):
                for k in range(EP):
                    m = EP * n + k
                    act.wait_ge(e1_mm, m + 1)
                    if k == 0 and n >= 2:
                        act.wait_ge(e2_mm, EP * (n - 1))
                    A(hb0[n % 2][:, 512 * k:512 * (k + 1)], banks[m % 2][:, :], ACT.Relu,
                      bias=c("eb1", lo=k, n=1)).then_inc(e1_act, 1)
                for k in range(EP):
                    m = EP * n + k
                    act.wait_ge(e2_mm, m + 1)
                    if k == 0 and n >= 2:
                        act.wait_ge(gb_out, EP * (n - 1))
                    A(hb2[n % 2][:, 512 * k:512 * (k + 1)], banks[2 + m % 2][:, :], ACT.Relu,
                      bias=c("eb2", lo=k, n=1)).then_inc(e2_act, 1)

        @block.tensor
        def _(pe):
            mm, tr = nc.tensor.matmul, nc.tensor.transpose
            pe.wait_ge(const_in, 16)
            for b in range(B):
                i = b % 2
                pe.wait_ge(onehot, b + 1)
                if b >= 2:
                    pe.wait_ge(conv1_act, b - 1)
                for t in range(4):
                    ins = mm(banks[i][:, :], c("cw1", lo=128 * t, n=128), oh[i][:, 2 * t:2 * t + S],
                             start=(t == 0), stop=(t == 3))
                ins.then_inc(conv1_mm, 1)
                if b >= 1:
                    pe.wait_ge(emb_out, b)
                for st in range(ST):
                    ins = mm(banks[6][:, 68 * st:68 * (st + 1)], oh[i][0:64, 3 + P * st:3 + P * (st + 1)],
                             c("emb", slice(0, 64)), start=True, stop=True)
                ins.then_inc(emb_mm, 1)
                pe.wait_ge(conv1_act, b + 1)
                if b >= 2:
                    pe.wait_ge(conv2_act, b - 1)
                for t in range(5):
                    ins = mm(banks[2 + i][0:64, :], c("cw2", lo=64 * t, n=64), g1[i][:, t:t + S],
                             start=(t == 0), stop=(t == 4))
                ins.then_inc(conv2_mm, 1)
                pe.wait_ge(conv2_act, b + 1)
                for st in range(ST):
                    for t in range(3):
                        ins = mm(banks[7][:, ST * b + st:ST * b + st + 1], g2[i][:, P * st + t:P * st + t + P],
                                 c("cw3", slice(0, 64), lo=t, n=1), start=(t == 0), stop=(t == 2))
                ins.then_inc(ctx_mm, 1)
            pe.wait_ge(tvec, 1)
            pe.wait_ge(tact, 2)
            for i in range(TT):
                b, st = i // ST, i % ST
                pe.wait_ge(basis, i + 1)
                if st == 0 and b:
                    pe.wait_ge(field_out, b)
                for pt in range(ST):
                    ins = mm(banks[4 + pt][:, 0:D], bas[i % 2][:, P * pt:P * (pt + 1)], amps[:, i, :],
                             start=(st == 0), stop=(st == ST - 1))
                ins.then_inc(field_mm, 1)
            pe.wait_ge(field_out, B)
            for n in range(32):
                xg, bp = n % 8, n // 8
                if xg == 0:
                    pe.wait_ge(x_in, 16 * (bp + 1))
                if n >= 4:
                    pe.wait_ge(fc0_act, n - 3)
                mm(banks[4 + n % 4][:, :], c("fc0", slice(0, 6)), xin[:, 512 * xg:512 * (xg + 1)],
                   start=True, stop=True).then_inc(fc0_mm, 1)

            with pe.Fori(0, LAYERS) as l:
                def to_rows(xp):
                    if xp % 2 == 0:
                        pe.wait_ge(h_ready, 16 * l + xp // 2 + 1)
                    if xp >= 2:
                        pe.wait_ge(xt_ready, 32 * l + xp - 1)
                    for bp in range(BP):
                        ins = tr(banks[xp % 2][:, P * bp:P * (bp + 1)], hbuf[:, bp, P * xp:P * (xp + 1)], c("ident"))
                    ins.then_inc(t_mm, 1)

                to_rows(0)
                for xp in range(NPAIR):
                    if xp < NPAIR - 1:
                        to_rows(xp + 1)
                    g, half = xp // 2, xp % 2
                    pe.wait_ge(xt_ready, 32 * l + xp + 1)
                    if half == 0 and g >= 2:
                        pe.wait_ge(af_ready, 16 * l + g - 1)
                    mm(banks[2 + g % 2][64 * half:64 * half + 64, :], c("dft_y"), xt[xp % 2],
                       start=True, stop=True).then_inc(f1_mm, 1)
                for i in range(4):
                    pe.wait_ge(a_in[i], 64 * (l + 1))
                for ky in range(KY):
                    if ky >= 2:
                        spectrum_done(pe, l, ky - 1)
                    for bp in range(BP):
                        ins = mm(banks[4 + ky % 2][:, P * bp:P * (bp + 1)], abuf[:, ky, P * bp:P * (bp + 1)],
                                 c("dft_x"), start=True, stop=True)
                    ins.then_inc(f2_mm, 1)

                def inverse_x(ky):
                    pe.wait_ge(z_in[ky % 4], 16 * (4 * l + ky // 4 + 1))
                    if ky >= 2:
                        pe.wait_ge(ys_ready, 16 * l + ky - 1)
                    mm(banks[2 + ky % 2][:, :], c("idft_x", slice(0, 64)), z2[ky % 4],
                       start=True, stop=True).then_inc(i1_mm, 1)

                LAG = 3
                for ky in range(KY + LAG):
                    if ky < KY:
                        pe.wait_ge(w_in[ky % NW], 16 * (4 * l + ky // NW + 1))
                        spectrum_done(pe, l, ky + 1)
                        if ky >= 2:
                            pe.wait_ge(zs_ready, 16 * l + ky - 1)
                        for k in range(8):
                            for q in range(4):
                                kx = 8 * q + k
                                ins = mm(banks[ky % 2][32 * q:32 * q + 16, 64 * k:64 * (k + 1)],
                                         spec[:, ky, 2 * kx:2 * kx + 2, :].rearrange("p r b -> p (r b)"),
                                         wring[:, ky % NW, C * kx:C * (kx + 1)], start=True, stop=True)
                        ins.then_inc(mix_mm, 1)
                    if ky >= LAG:
                        inverse_x(ky - LAG)
                pe.wait_ge(lc_in, 16 * (l + 1))
                for i in range(4):
                    pe.wait_ge(y_in[i], 64 * (l + 1))
                for q in range(32):
                    xg, bp = q // BP, q % BP
                    if q >= 4:
                        pe.wait_ge(o_act, 32 * l + q - 3)
                    mm(banks[4 + q % 4][:, :], lcst[:, 0:P], hbuf[:, bp, 512 * xg:512 * (xg + 1)], start=True, stop=False)
                    for h in range(2):
                        ins = mm(banks[4 + q % 4][:, 256 * h:256 * (h + 1)], abuf[:, 2 * xg + h, P * bp:P * (bp + 1)],
                                 c("idft_y"), start=False, stop=(h == 1))
                    ins.then_inc(o_mm, 1)
                pe.wait_ge(bn_dve, 6 * l + 1)
                mm(banks[0][:, 0:2], c("swap"), bn[:, 0:2], start=True, stop=True).then_inc(bn_mm, 1)

            pe.wait_ge(h_ready, 16 * (LAYERS + 1))
            def head2(n):
                b, xg = n // 8, n % 8
                pe.wait_ge(fc1_act, n + 1)
                if xg == 0 and b >= 2:
                    pe.wait_ge(ft_ready, b - 1)
                ins = mm(banks[4 + b % 2][0:8, :], c("fc2", lo=7 - xg, n=8), stage[:, 512 * (n % 4):512 * (n % 4 + 1)],
                         start=(xg == 0), stop=(xg == 7))
                ins.then_inc(fc2_mm, 1)

            for n in range(64):
                b, xg = n // 8, n % 8
                if n >= 4:
                    pe.wait_ge(fc1_act, n - 3)
                r = slice(64 * (b % 2), 64 * (b % 2) + 64)
                mm(banks[n % 4][:, :], c("fc1", r), hbuf[r, b // 2, 512 * xg:512 * (xg + 1)],
                   start=True, stop=True).then_inc(fc1_mm, 1)
                if n >= 2:
                    head2(n - 2)
            head2(62)
            head2(63)
            for k in range(2, T + 1):
                pe.wait_ge(pw_out, k - 1)
                mm(banks[7][:, 0:P], mrow[:, :], mp[:, k - 1, :], start=True, stop=True).then_inc(pw_mm, 1)
            pe.wait_ge(ln_dve, 2)
            for g in range(9):
                if g >= 4:
                    pe.wait_ge(tp_out, g - 3)
                for k in range(4):
                    ins = tr(banks[g % 4][0:64, P * k:P * (k + 1)], un[:, 4 * g + k, :], c("ident"))
                ins.then_inc(tp_mm, 1)
            pe.wait_ge(tp_out, 9)
            pe.wait_ge(pw_out, T)
            for m in range(18):
                if m >= 2:
                    pe.wait_ge(bu_out, m - 1)
                mm(banks[4 + m % 2][:, :], c("bmat", slice(0, 64), lo=P * (m // 9), n=P),
                   ut[:, 512 * (m % 9):512 * (m % 9 + 1)], start=True, stop=True).then_inc(bu_mm, 1)
            pe.wait_ge(bu_out, 18)
            mm(banks[0][:, 0:288], mp[:, 1, :], sx4[:, :, :, 0], start=True, stop=True).then_inc(st_mm, 1)
            with pe.Fori(1, T - 1) as j:
                pe.wait_ge(st_out, j)
                mm(banks[0][:, 0:288], mp[:, 1, :], sx4[:, :, :, bass.ds(j, 1)], start=True, stop=True).then_inc(st_mm, 1)
            for ch in range(2, CH):
                pe.wait_ge(cy_out, ch - 1)
                mm(banks[4][:, 0:16], mp[:, T, :], cy[:, :, ch - 1], start=True, stop=True).then_inc(cy_mm, 1)
            pe.wait_ge(cy_out, CH - 1)
            pe.wait_ge(st_out, T - 1)
            for j in range(T):
                if j >= 4:
                    pe.wait_ge(fx_out, j - 3)
                mm(banks[j % 4][:, 0:16 * (CH - 1)], mp[:, j + 1, :], cy[:, :, 1:CH], start=True, stop=True).then_inc(fx_mm, 1)
            pe.wait_ge(fx_out, T)
            xr = sx[64:128, :].rearrange("p (r b t) -> p r b t", r=2, b=B)
            for i in range(TILES):
                if i < TT:
                    t0 = X + P * (i % ST)
                    parts = [(slice(0, P), i // ST, t0, t0 + P)]
                else:
                    parts = [(slice(64 * b2, 64 * b2 + 64), 2 * (i - TT) + b2, 0, X) for b2 in range(2)]
                for rows, b, lo, hi in parts:
                    for r in range(2):
                        ins = mm(banks[i // 8][rows, 64 * (i % 8):64 * (i % 8 + 1)], xr[:, r, b, lo:hi],
                                 c("cmat", slice(64, 128), lo=64 * r, n=64), start=(r == 0), stop=(r == 1))
                if i % 8 == 7 or i == TILES - 1:
                    ins.then_inc(ao_mm, 1)
            pe.wait_ge(ln_dve, 4)
            for g in range(9):
                if g >= 4:
                    pe.wait_ge(tp2_out, g - 3)
                for k in range(4):
                    ins = tr(banks[g % 4][0:64, P * k:P * (k + 1)], un[:, 4 * g + k, :], c("ident"))
                ins.then_inc(tp2_mm, 1)
            pe.wait_ge(tp2_out, 9)

            def cols(n):
                return u2t[:, 512 * n:512 * (n + 1)]

            def logits(n):
                pe.wait_ge(rh_act, n + 1)
                for k in range(4):
                    i = 4 * n + k
                    ins = mm(banks[6][:, E * i:E * (i + 1)], rh[n % 2][:, P * k:P * (k + 1)], c("rw2", slice(0, 33)),
                             start=True, stop=True)
                ins.then_inc(lg_mm, 1)

            for n in range(9):
                if n >= 2:
                    pe.wait_ge(rh_act, n - 1)
                mm(banks[4 + n % 2][0:32, :], c("rw1", slice(0, 64)), cols(n), start=True, stop=True).then_inc(rh_mm, 1)
                if n:
                    logits(n - 1)
            logits(8)
            pe.wait_ge(gate, 3)
            for g in range(9):
                if g >= 2:
                    pe.wait_ge(gt_out, g - 1)
                for k in range(4):
                    ins = tr(banks[7 - g % 2][0:6, P * k:P * (k + 1)], gates[:, 4 * g + k, :], c("ident"))
                ins.then_inc(gt_mm, 1)
            pe.wait_ge(gt_out, 9)

            for n in range(9):
                for k in range(EP):
                    m = EP * n + k
                    if m >= 2:
                        pe.wait_ge(e1_act, m - 1)
                    mm(banks[m % 2][:, :], c("ew1", slice(0, 64), lo=P * k, n=P), cols(n), start=True, stop=True).then_inc(e1_mm, 1)
                for k in range(EP):
                    m = EP * n + k
                    pe.wait_ge(e1_act, m + 1)
                    if m >= 2:
                        pe.wait_ge(e2_act, m - 1)
                    mm(banks[2 + m % 2][:, :], c("ew2", lo=P * k, n=P), hb0[n % 2][:, 512 * k:512 * (k + 1)],
                       start=True, stop=True).then_inc(e2_mm, 1)
                for k in range(EP):
                    m = EP * n + k
                    if m >= 2:
                        pe.wait_ge(gb_out, m - 1)
                    mm(banks[4 + m % 2][:, :], c("sel", slice(64, 70), lo=P * k, n=P), gtt[:, 512 * n:512 * (n + 1)],
                       start=True, stop=True).then_inc(gb_mm, 1)
                pe.wait_ge(gb_out, EP * (n + 1))
                if n >= 2:
                    pe.wait_ge(res, n - 1)
                for t in range(4):
                    dst = banks[6 + n % 2][:, D * t:D * (t + 1)]
                    for k in range(EP):
                        mm(dst, hb3[n % 2][:, 512 * k + P * t:512 * k + P * (t + 1)], c("ew3", lo=D * k, n=D),
                           start=(k == 0), stop=False)
                    ins = mm(dst, gtt[:, 512 * n + P * t:512 * n + P * (t + 1)], c("eb3", slice(64, 70)), start=False, stop=True)
                ins.then_inc(e3_mm, 1)


def spectra():
    th = 2 * np.pi / X
    x = np.arange(X)
    ky = np.arange(KY)
    kx = np.concatenate([np.arange(16), np.arange(48, 64)])
    dft_y = np.zeros((2, Y, 2, 2, KY))
    ang = th * np.outer(x, ky)
    for i in range(2):
        dft_y[i, :, i, 0] = np.cos(ang)
        dft_y[i, :, i, 1] = -np.sin(ang)
    ax = th * np.outer(x, kx)
    cs, sn = np.cos(ax), np.sin(ax)
    fwd = np.zeros((X, 2, 2, KX, 2))
    fwd[:, 0, 0, :, 0], fwd[:, 1, 0, :, 0] = cs, sn
    fwd[:, 0, 0, :, 1], fwd[:, 1, 0, :, 1] = -sn, cs
    fwd[:, :, 1, :, 0], fwd[:, :, 1, :, 1] = -fwd[:, :, 0, :, 1], fwd[:, :, 0, :, 0]
    dft_x = fwd.reshape(16, 4, 2, -1).transpose(1, 2, 0, 3).reshape(P, 128)
    inv = np.zeros((KX, 2, X, 2))
    inv[:, 0, :, 0], inv[:, 1, :, 0] = cs.T / X, -sn.T / X
    inv[:, 0, :, 1], inv[:, 1, :, 1] = sn.T / X, cs.T / X
    inv = inv.reshape(4, 8, 2, 16, 4, 2).transpose(1, 0, 2, 4, 5, 3).reshape(64, P)
    idft_y = np.zeros((4, 2, KY, 4, Y))
    wt = np.where(ky == 0, 1.0, 2.0)[:, None] / Y
    for i in range(4):
        idft_y[i, 0, :, i] = wt * np.cos(ang.T)
        idft_y[i, 1, :, i] = -wt * np.sin(ang.T)
    return dft_y.reshape(P, 64), dft_x, inv, idft_y.reshape(P, 256)


def kernel(**inputs):
    import concourse.bacc as bacc
    from concourse.bass_utils import run_bass_kernel_spmd

    a = {k: np.asarray(v) for k, v in inputs.items()}
    tk = {k[7:]: v for k, v in a.items() if k.startswith("L0_tok_")}
    tx = {k[7:]: v for k, v in a.items() if k.startswith("L0_txt_")}
    at = {k[8:]: v for k, v in a.items() if k.startswith("L0_attn_")}
    ff = {k[7:]: v for k, v in a.items() if k.startswith("L0_ffn_")}
    f4 = np.float32
    cst = np.zeros((P, CW), f4)

    def put(name, v, row=0, col=0):
        v = v.reshape(v.shape[0], -1)
        lo = AT[name][0] + col
        cst[row:row + v.shape[0], lo:lo + v.shape[1]] = v

    dft_y, dft_x, idft_x, idft_y = spectra()
    put("ident", np.eye(P, dtype=f4))
    put("dft_y", dft_y.astype(f4)); put("dft_x", dft_x.astype(f4))
    put("idft_x", idft_x.astype(f4)); put("idft_y", idft_y.astype(f4))
    put("swap", np.roll(np.eye(P, dtype=f4), 64, axis=0))
    for b2 in range(2):
        r = 64 * b2
        put("fc0", tk["fc0_w"], 3 * b2, r)
        put("fc0_b", tk["fc0_b"][:, None], r)
        put("fc1", tk["fc1_w"], r)
        for e in range(4):
            t = 2 * e + b2
            if t < 7:
                put("cw1", tx["w1"][:, :, t].T, r, P * e)
        put("vocab", np.arange(64, dtype=f4)[:, None], r)
        put("agd", np.stack([at["A_diag"], at["G_diag"], at["dt"]], 1), r)
        put("eye2", np.eye(64, dtype=f4), r)
        for k in range(EP):
            e = 2 * k + b2
            put("ew1", ff["expert_w1"][e], 0, P * k + r)
            put("eb1", ff["expert_b1"][e][:, None], r, k)
            put("ew2", ff["expert_w2"][e], r, P * k + r)
            put("eb2", ff["expert_b2"][e][:, None], r, k)
            put("ew3", ff["expert_w3"][e], r, D * k)
            put("sel", np.ones((1, 64), f4), 64 + e, P * k + r)
    put("fc1_b", tk["fc1_b"][:, None]); put("fc2", tk["fc2_w"], 0, 7)
    put("fc2_b", np.broadcast_to(tk["fc2_b"][None], (P, 1)))
    put("cb1", tx["b1"][:, None]); put("cb2", tx["b2"][:, None])
    put("cw2", tx["w2"].transpose(1, 2, 0)); put("cw3", tx["w3"][0])
    put("cb3", np.broadcast_to(tx["b3"][None], (P, 1)))
    put("emb", np.concatenate([tx["emb"], tx["locality_shapes"]], 1))
    put("bytepos", np.linspace(0.0, 1.0, S, dtype=f4).reshape(ST, P).T)
    put("widths", np.broadcast_to(tx["multiscale_widths"][None], (P, SCALES)))
    put("swts", np.broadcast_to(tx["scale_weights"][None], (P, SCALES)))
    put("bmat", at["Bmat"][:, :, 0].T, 0, 0); put("bmat", at["Bmat"][:, :, 1].T, 0, P)
    put("cmat", at["Cmat"][:, :, 0].T, 64, 0); put("cmat", at["Cmat"][:, :, 1].T, 64, 64)
    put("dvec", np.broadcast_to(at["D"][None], (P, D)))
    put("rw1", ff["router_w1"]); put("rb1", ff["router_b1"][:, None])
    put("rw2", ff["router_w2"]); put("rw2", ff["router_b2"][None], 32)
    put("eb3", ff["expert_b3"], 64)
    lc = np.zeros((LAYERS, P, 131), f4)
    for b2 in range(2):
        r = slice(64 * b2, 64 * b2 + 64)
        lc[:, r, r] = tk["pw_w"].transpose(0, 2, 1)
        lc[:, r, 128], lc[:, r, 129], lc[:, r, 130] = tk["pw_b"], tk["gamma"], tk["beta"]
    wre = np.concatenate([tk["w1r"], tk["w2r"]], 3)
    wim = np.concatenate([tk["w1i"], tk["w2i"]], 3)
    ws = np.stack([wre, wim], 1).transpose(0, 5, 1, 2, 4, 3).reshape(LAYERS * KY, P, KX * C)
    xs = a["x"].reshape(BP, 2, PX, 3).transpose(0, 1, 3, 2).reshape(BP, 6, PX)
    arrays = {"xs": xs, "toks": a["x_txt"], "pos": a["fside_BS_continuous_positions"],
              "consts": cst, "lconst": lc, "wspec": ws}
    arrays = {k: np.ascontiguousarray(v) for k, v in arrays.items()}
    nc = bacc.Bacc("TRN2", target_bir_lowering=False, num_devices=1)
    args = [nc.dram_tensor(k, v.shape, mybir.dt.from_np(v.dtype), kind="ExternalInput").ap() for k, v in arrays.items()]
    out = nc.dram_tensor("out", (B, L, D), F32, kind="ExternalOutput").ap()
    build_program(nc, *args, out)
    r = run_bass_kernel_spmd(nc, [arrays], core_ids=[0])
    return r.results[0]["out"]
```

```python
from contextlib import ExitStack

import concourse.bass as bass
from concourse import mybir
import numpy as np

F32 = mybir.dt.float32
I32 = mybir.dt.int32
ALU = mybir.AluOpType
ACT = mybir.ActivationFunctionType
AX_X = mybir.AxisListType.X

P = 128
B, BP = 8, 4
X = Y = 64
C = D = 64
LAYERS = 4
KX, KY = 32, 16
PX = X * Y
NPAIR = X // 2
S = 512
ST = S // P
SCALES = 4
L = X + S
TILES = B * L // P
TT = B * ST
T = 16
CH = S // T
E, EP = 6, 3
EPS = 1e-5
TWO_PI_IN = 2 * np.pi * (1 - 2.0 ** -21)
NS = 8
NW = 8
WC = KX * C // 2


TILES_OF_CONSTANTS = {
    "main": [("ident", 128), ("dft_y", 64), ("dft_x", 128), ("idft_x", 256), ("idft_y", 256)],
    "text": [("cw1", 512), ("cb1", 1), ("cw2", 320), ("cb2", 1), ("cw3", 6), ("cb3", 1), ("emb", 68),
             ("vocab", 1), ("bytepos", ST), ("widths", SCALES), ("swts", SCALES), ("fc0", 128), ("fc0_b", 1),
             ("agd", 3)],
    "tail": [("fc1", 256), ("fc1_b", 1), ("fc2", 15), ("fc2_b", 1), ("eye2", 64), ("bmat", 256), ("cmat", 128), ("dvec", 64), ("rw1", 32), ("rb1", 1),
             ("rw2", 6), ("ew1", 384), ("eb1", 3), ("ew2", 384), ("eb2", 3), ("ew3", 384), ("eb3", 64)],
}
AT, WIDTH = {}, {}
for _tile, _cols in TILES_OF_CONSTANTS.items():
    _n = 0
    for _name, _w in _cols:
        AT[_name] = (_tile, _n, _n + _w)
        _n += _w
    WIDTH[_tile] = _n

UNITS = 16
AT_STEP = {}
for _k, _part in enumerate("usrp"):
    for _u in range(2):
        AT_STEP["forward", 8 + 4 * _u + _k] = (_u, _part)
    for _u in range(8):
        AT_STEP["mix", 4 * _u + _k] = (2 + _u, _part)
    for _u in range(6):
        AT_STEP["out", 5 * _u + _k] = (10 + _u, _part)
AT_STEP["out", 31] = (UNITS, "p")
STEPS = KY + 2
FORWARD_X = [(2, 3), (4, 5), (6, 7), (8, 9), (10, 11), (12,), (13,), (14,), (15,)] + [()] * (STEPS - 9)
INVERSE_X = [()] * 9 + [(0, 1), (2, 3), (4, 5), (6, 7), (8, 9), (10, 11), (12, 13), (), (14, 15)]
READ_Z = [(), (0,), (1,), (2,), (3,)] + [()] * 5 + [(4, 5), (6, 7), (8, 9), (10, 11), (12, 13), (14,), (15,), ()]
ODD_POWERS = [(3, 1), (5, 3), (9, 4), (13, 3)]
GA = 8


def build_program(nc, xs, toks, pos, cmain, ctext, ctail, lconst, wspec, out):
    nc.disable_value_cache = True
    with ExitStack() as ctx:
        def sb(name, shape, dt=F32):
            return ctx.enter_context(nc.sbuf_tensor(name, shape, dt))

        def sem(name):
            return ctx.enter_context(nc.semaphore(name))

        hbuf = sb("hbuf", [P, BP, PX])
        abuf = sb("abuf", [P, 16, B * C])
        big = sb("big", [P, NW * WC + NS * 512])
        stage = sb("stage", [P, 6 * 512])
        tok = sb("tok", [P, TILES, D])
        amps = sb("amps", [P, TT, D])
        tv = sb("tv", [P, 12, TT])
        posb = sb("posb", [P, S])
        xd = sb("xd", [P, S])
        eb = sb("eb", [P, 2, 1024])
        rb = sb("rb", [P, 2, 1024])
        kb = sb("kb", [P, 2 * S])
        basis = sb("basis", [P, S])
        ampr = sb("ampr", [P, 2, D])
        fieldt = sb("fieldt", [D, S])
        cst = sb("cst", [P, WIDTH["main"]])
        lcst = sb("lcst", [P, 131])
        stats = sb("stats", [P, 32, 6])
        bn = sb("bn", [P, 16])
        banks = [ctx.enter_context(nc.psum_tensor(f"bank{i}", [P, 512], F32)) for i in range(8)]
        zdram = nc.dram_tensor("zdram", (KY, 8, 4, 16, 64), F32).ap()

        wring = big[:, 0:NW * WC].rearrange("p (n w) -> p n w", w=WC)
        spec = big[:, NW * WC:NW * WC + NS * 512].rearrange("p (s k b) -> p s k b", s=NS, b=B)
        af = [stage[:, 512 * i:512 * (i + 1)] for i in range(4)]
        zs = [stage[:, 512 * i:512 * (i + 1)] for i in range(2)]
        z2 = [stage[64 * (i % 2):64 * (i % 2) + 64, 512 * (2 + i // 2):512 * (3 + i // 2)] for i in range(4)]
        NY = 2
        ys = [stage[:, 512 * (4 + i):512 * (5 + i)] for i in range(NY)]
        OB = (4, 5, 6, 0, 1, 2)
        NO = len(OB)
        ab1 = abuf[:, :, :].rearrange("p a n -> p (a n)")
        hb1 = hbuf[:, :, :].rearrange("p a n -> p (a n)")
        sp1 = big[:, :]
        csts = {"main": cst, "text": ab1[:, 4608:4608 + WIDTH["text"]], "tail": ab1[:, 5632:5632 + WIDTH["tail"]]}

        def c(name, rows=slice(0, P), lo=0, n=None):
            tile, a, b = AT[name]
            return csts[tile][rows, a + lo:(b if n is None else a + lo + n)]

        xt = [big[:, NW * WC + 512 * i:NW * WC + 512 * (i + 1)] for i in range(4)]
        XB = (0, 1, 4, 5)

        const_in = sem("const_in")
        toks_in = sem("toks_in"); onehot = sem("onehot"); pad0 = sem("pad0")
        conv1_mm = sem("conv1_mm"); conv1_act = sem("conv1_act"); conv2_mm = sem("conv2_mm")
        conv2_act = sem("conv2_act"); ctx_mm = sem("ctx_mm"); emb_mm = sem("emb_mm"); emb_out = sem("emb_out")
        tvec = sem("tvec"); tact = sem("tact")
        tail_in = sem("tail_in"); text_in = sem("text_in")
        pos_in = sem("pos_in"); xd_ready = sem("xd_ready"); r_done = sem("r_done"); squared = sem("squared")
        exp_done = sem("exp_done"); sin_done = sem("sin_done"); product = sem("product"); e_free = sem("e_free")
        summed = sem("summed"); field_mm = sem("field_mm"); field_sb = sem("field_sb"); field_tr = sem("field_tr")
        field_out = sem("field_out"); vch = sem("vch"); dstep = sem("dstep"); pstep = sem("pstep")
        x_in = sem("x_in"); fc0_mm = sem("fc0_mm"); h_ready = sem("h_ready"); lc_in = sem("lc_in")
        w_in = [sem(f"w_in{i}") for i in range(NW)]
        t_mm = sem("t_mm"); xt_dve = sem("xt_dve"); xt_act = sem("xt_act"); f1_mm = sem("f1_mm"); af_dve = sem("af_dve"); af_act = sem("af_act")
        a_in = [sem(f"a_in{i}") for i in range(4)]
        f2_mm = sem("f2_mm"); s_act = sem("s_act"); s_dve = sem("s_dve"); mix_mm = sem("mix_mm")
        zs_ready = sem("zs_ready"); z_out = [sem(f"z_out{i}") for i in range(4)]
        z_in = [sem(f"z_in{i}") for i in range(4)]
        i1_mm = sem("i1_mm"); inverse_in = sem("inverse_in"); ys_ready = sem("ys_ready"); y_in = [sem(f"y_in{i}") for i in range(NY)]
        o_mm = sem("o_mm"); o_stats = sem("o_stats"); o_act = sem("o_act"); bn_dve = sem("bn_dve")
        bn_mm = sem("bn_mm"); bn_act = sem("bn_act")
        fc1_mm = sem("fc1_mm"); fc1_act = sem("fc1_act"); fc2_mm = sem("fc2_mm"); fc0_act = sem("fc0_act"); bn_rs = sem("bn_rs"); ft_ready = sem("ft_ready")
        img_in = sem("img_in")
        ln_dve = sem("ln_dve"); ln_act = sem("ln_act"); tp_mm = sem("tp_mm"); tp_out = sem("tp_out")
        pw_mm = sem("pw_mm"); pw_out = sem("pw_out"); bu_mm = sem("bu_mm"); bu_out = sem("bu_out")
        st_mm = sem("st_mm"); st_out = sem("st_out"); ke_mm = sem("ke_mm"); ke_out = sem("ke_out")
        ki_mm = sem("ki_mm"); ki_out = sem("ki_out"); tpi_mm = sem("tpi_mm"); tpi_out = sem("tpi_out")
        bi_mm = sem("bi_mm"); bi_out = sem("bi_out"); skip = sem("skip"); pch = sem("pch"); cy_mm = sem("cy_mm"); cy_out = sem("cy_out")
        fx_mm = sem("fx_mm"); fx_out = sem("fx_out"); ao_mm = sem("ao_mm"); ao_out = sem("ao_out")
        tp2_mm = sem("tp2_mm"); tp2_out = sem("tp2_out")
        rh_mm = sem("rh_mm"); rh_act = sem("rh_act"); lg_mm = sem("lg_mm"); gate = sem("gate")
        gate_act = sem("gate_act"); gt_mm = sem("gt_mm"); gt_out = sem("gt_out"); gated = sem("gated"); reduced = sem("reduced"); halved = sem("halved")
        e1_mm = sem("e1_mm"); e1_act = sem("e1_act"); e2_mm = sem("e2_mm"); e2_act = sem("e2_act")
        e3_mm = sem("e3_mm"); res = sem("res")
        stored = sem("stored")

        toki = ab1[:, 0:1024].bitcast(I32)
        oh = [ab1[:, 1024 + 520 * i:1024 + 520 * (i + 1)] for i in range(2)]
        g1 = [ab1[:, 2064 + 516 * i:2064 + 516 * (i + 1)] for i in range(2)]
        g2 = [ab1[:, 3096 + 516 * i:3096 + 516 * (i + 1)] for i in range(2)]
        embt = sp1[:, 8192:8192 + TT * 68].rearrange("p (t e) -> p t e", e=68)
        xin = [sp1[0:6, PX * i:PX * (i + 1)] for i in range(2)]

        eb3, rb3 = (x[:, :, :].rearrange("p a n -> p (a n)").rearrange("p (t d) -> p t d", d=D) for x in (eb, rb))
        NH = 8
        hid = [sp1[:, 512 * i:512 * (i + 1)] for i in range(NH)]
        ft = [stage[:, 512 * i:512 * (i + 1)] for i in range(2)]
        ut = ab1[0:64, 0:B * L]
        un_t, un_i = eb3, kb[:, 0:4 * D].rearrange("p (t d) -> p t d", d=D)
        w1_t, w1_i = rb3, kb[:, 4 * D:8 * D].rearrange("p (t d) -> p t d", d=D)
        lnv = kb[:, 8 * D:8 * D + 8 * TILES].rearrange("p (k t) -> p k t", t=TILES)
        sx = sp1[:, 4096:4096 + 16 * S]
        sx4 = sx.rearrange("p (g c j) -> p g c j", c=CH, j=T)
        si = sp1[:, 0:16 * X].rearrange("p (g t) -> p g t", t=X)
        pm = amps[:, :, :].rearrange("p t d -> p (t d)").rearrange("p (k n) -> p k n", n=P)
        ph = ab1[:, 4608:4608 + 4 * P].rearrange("p (k n) -> p k n", n=P)
        qm = [x[:, P * i:P * (i + 1)] for x in (xd, posb) for i in range(4)]
        ends = stage[:, 1024:1536].rearrange("p (g c) -> p g c", c=CH)
        carry = stage[:, 1536:2048].rearrange("p (g c) -> p g c", c=CH)
        co = tv[:, 10, 8:22]

        def power(e):
            return pm[:, 2 ** e - 1, :] if e <= 4 else ph[:, e - 5, :]

        un = sp1[:, 4096:4096 + TILES * D].rearrange("p (t d) -> p t d", d=D)
        w1 = sp1[:, 6400:6400 + TILES * D].rearrange("p (t d) -> p t d", d=D)
        h2 = sp1[:, 1024:1024 + TILES * D].rearrange("p (t d) -> p t d", d=D)
        u2t = ab1[0:64, 0:B * L]
        gtt = ab1[64:70, 0:B * L]
        wr1 = sp1[:, 8704:11204]
        lg = wr1[:, 0:216].rearrange("p (t e) -> p t e", e=E)
        pr = wr1[:, 216:432].rearrange("p (t e) -> p t e", e=E)
        gv = wr1[:, 432:432 + 216 * 6].rearrange("p (k t e) -> p k t e", k=6, e=E)
        gs = wr1[:, 1728:1728 + 12 * TILES].rearrange("p (k t) -> p k t", t=TILES)
        gates = wr1[:, 2200:2200 + TILES * (E + 1)].rearrange("p (t e) -> p t e", e=E + 1)
        rh = [stage[0:33, 512 * i:512 * (i + 1)] for i in range(2)]
        NM = EP * TILES // 4
        ha = hb1[:, 0:512 * NM]
        hr = [hb1[:, 512 * (NM + i):512 * (NM + i + 1)] for i in range(4)]
        prod = [x[:, :, :].rearrange("p a n -> p (a n)")[:, 0:4 * (E + 1) * D].rearrange("p (t e d) -> p t e d", t=4, d=D)
                for x in (eb, rb)]
        w1t = tok

        def bc(v, n):
            return v.unsqueeze(2).to_broadcast([P, v.shape[1], n])

        def spectrum_parts(ky):
            src = banks[4 + ky % 2][:, :].rearrange("p (b k) -> p b k", b=BP)
            for part in range(2):
                for b2 in range(2):
                    yield (spec[64 * part:64 * part + 64, ky % NS, :, b2::2].rearrange("p k b -> p b k"),
                           src[64 * b2:64 * b2 + 64, :, 64 * part:64 * part + 64])

        def spectrum_room(eng, l, ky):
            eng.wait_ge(f2_mm, 16 * l + ky + 1)
            if ky >= NS:
                eng.wait_ge(mix_mm, 32 * l + NW + 2 * (ky - NS + 1))

        def rows_done(eng, l, g):
            eng.wait_ge(xt_dve, (GA + 16) * l + (2 * g + 2 if g < GA else GA + g + 1))
            if g >= GA:
                eng.wait_ge(xt_act, (16 - GA) * l + g - GA + 1)

        def y_done(eng, l, g):
            if g < GA:
                eng.wait_ge(af_dve, GA * l + g + 1)
            else:
                eng.wait_ge(af_act, (16 - GA) * l + g - GA + 1)

        def spectrum_done(eng, l, n):
            eng.wait_ge(s_dve, 8 * l + (n + 1) // 2)
            if n > 1:
                eng.wait_ge(s_act, 8 * l + n // 2)

        block = ctx.enter_context(nc.Block())

        @block.sync
        def _(sp):
            sp.dma_start(csts["text"], ctext).then_inc(text_in, 16)
            for b in range(B):
                if b >= 2:
                    sp.wait_ge(onehot, b - 1)
                sp.dma_start(toki[:, 512 * (b % 2):512 * (b % 2 + 1)], toks[b:b + 1, :].to_broadcast([P, S])
                             ).then_inc(toks_in, 16)
                sp.wait_ge(toks_in, 16 * (b + 1))
                if b in (0, 1, 3, 5):
                    bp = (b + 1) // 2
                    if bp >= 2:
                        sp.wait_ge(fc0_mm, 8 * (bp - 1))
                    sp.dma_start(xin[bp % 2], xs[bp]).then_inc(x_in, 16)
                    sp.wait_ge(x_in, 16 * (bp + 1))
            sp.dma_start(cst[:, :], cmain).then_inc(const_in, 16)

            with sp.Fori(0, LAYERS) as l:
                def weights(n):
                    used = sp.snap(32 * l + n + 1)
                    if n == 0:
                        moved = sp.snap(l + 1)
                        sp.wait_ge(inverse_in, moved)
                    sp.wait_ge(mix_mm, used)
                    sp.wait_ge(const_in, 16)
                    sp.dma_start(wring[:, n % NW, :], wspec[bass.ds(2 * KY * l + n, 1)].rearrange("l p n -> (l p) n")
                                 ).then_inc(w_in[n % NW], 16)

                def positions(i):
                    sp.dma_start(posb[:, :], pos[bass.ds(2 * l + i, 1), :].to_broadcast([P, S])).then_inc(pos_in, 16)

                for n in range(NW):
                    weights(n)
                started = sp.snap(16 * l + 1)
                halfway = sp.snap(8 * l + ST)
                sp.wait_ge(h_ready, started)
                sp.wait_ge(const_in, 16)
                positions(0)
                for g in range(16):
                    y_done(sp, l, g)
                    sp.dma_start(abuf[g::16, :, :].rearrange("p a n -> p (a n)"), af[g % 4]).then_inc(a_in[g % 4], 16)

                def z_read(ky):
                    stored, used = sp.snap(64 * (4 * l + ky // 4 + 1)), sp.snap(16 * l + ky - 3)
                    sp.wait_ge(z_out[ky % 4], stored)
                    if ky >= 4:
                        sp.wait_ge(i1_mm, used)
                    sp.dma_start(z2[ky % 4], zdram[ky].rearrange("k q (r b) o -> (k q r) (b o)", r=2)
                                 ).then_inc(z_in[ky % 4], 16)

                for step in range(STEPS):
                    if step < KY:
                        filled = sp.snap(16 * l + step + 1)
                        sp.wait_ge(zs_ready, filled)
                        for q in range(4):
                            sp.dma_start(zdram[step, :, q].rearrange("k m o -> m k o"),
                                         zs[step % 2][32 * q:32 * q + 16, :].rearrange("m (k o) -> m k o", k=8)
                                         ).then_inc(z_out[step % 4], 16)
                    for ky in READ_Z[step]:
                        z_read(ky)
                    for n in range(2 * step + NW, min(2 * step + NW + 2, 2 * KY)):
                        weights(n)
                    if step == 8:
                        sp.wait_ge(xd_ready, halfway)
                        sp.wait_ge(const_in, 16)
                        positions(1)
            sp.wait_ge(o_mm, 32 * LAYERS)
            sp.dma_start(csts["tail"], ctail).then_inc(tail_in, 16)
            for b in range(B):
                sp.wait_ge(ft_ready, b // 4 + 1)
                sp.dma_start(tok[64 * (b % 2):64 * (b % 2) + 64, TT + b // 2, :],
                             ft[b // 4][32 * (b % 4):32 * (b % 4) + 8, :]).then_inc(img_in, 16)
            for b in range(B):
                sp.wait_ge(res, b + 1)
                sp.dma_start(out[b, X:L, :].rearrange("(t p) d -> p t d", p=P),
                             w1t[:, ST * b:ST * (b + 1), :]).then_inc(stored, 16)
            sp.wait_ge(res, B + 1)
            for b in range(B):
                sp.dma_start(out[b, 0:X, :], w1t[64 * (b % 2):64 * (b % 2) + 64, TT + b // 2, :]).then_inc(stored, 16)
            sp.wait_ge(stored, 32 * B)

        @block.gpsimd
        def _(pool):
            for i in range(2):
                nc.gpsimd.memset(oh[i], 0.0)
                nc.gpsimd.memset(g1[i], 0.0)
                nc.gpsimd.memset(g2[i], 0.0).then_inc(pad0, 1)
            nc.gpsimd.memset(ampr[:, 0, :], 0.0).then_inc(e_free, 1)
            nc.gpsimd.memset(ampr[:, 1, :], 0.0).then_inc(summed, 1)
            nc.gpsimd.memset(basis[:, :], 0.0).then_inc(field_mm, 1)
            nc.gpsimd.memset(fieldt[:, :], 0.0).then_inc(inverse_in, 1)
            pool.wait_ge(tvec, 1)
            G = nc.gpsimd.tensor_tensor
            with pool.Fori(0, LAYERS) as l:
                def unit_sum(m):
                    e, t = eb[:, m % 2, :], m // 2
                    pool.wait_ge(product, 16 * l + m + 1)
                    if m % 2 == 0:
                        pool.wait_ge(field_mm, 8 * l + t + 1)
                        G(basis[:, :], e[:, 0:S], e[:, S:2 * S], ALU.add).then_inc(e_free, 1)
                        nc.gpsimd.tensor_copy(ampr[:, t % 2, :], amps[:, bass.ds(8 * l + t, 1), :].rearrange("p a d -> p (a d)")
                                              ).then_inc(pstep, 1)
                    else:
                        G(e[:, 0:S], e[:, 0:S], e[:, S:2 * S], ALU.add).then_inc(pstep, 1)
                        pool.wait_ge(pstep, 16 * l + 2 * t + 2)
                        G(basis[:, :], basis[:, :], e[:, 0:S], ALU.add).then_inc(summed, 1)

                for m in range(UNITS):
                    if m == 4:
                        pool.wait_ge(h_ready, 16 * l + 16)
                        pool.dma_start(lcst[:, :], lconst[bass.ds(l, 1)].rearrange("l p n -> (l p) n")).then_inc(lc_in, 16)
                    unit_sum(m)
            for k, (w, u, t, n) in enumerate(((w1_t, un_t, tok[:, 0:TT, :], TT), (w1_i, un_i, tok[:, TT:TILES, :], TILES - TT))):
                pool.wait_ge(ln_dve, 2 * (k + 1))
                G(w, u, c("dvec").unsqueeze(1).to_broadcast([P, n, D]), ALU.mult).then_inc(pch, 1)
                pool.wait_ge(pch, k + 1)
                G(w, w, t, ALU.add).then_inc(skip, 1)
            for n in range(9):
                pool.wait_ge(gated, 4 * (n + 1))
                G(prod[n % 2][:, :, 1:4, :], prod[n % 2][:, :, 1:4, :], prod[n % 2][:, :, 4:7, :], ALU.add).then_inc(halved, 1)

        @block.vector
        def _(dve):
            links = [0]

            def link(ins):
                links[0] += 1
                ins.then_inc(vch, 1)
                dve.wait_ge(vch, links[0])

            V = nc.vector
            dve.wait_ge(text_in, 16)
            dve.wait_ge(pad0, 2)
            for b in range(B):
                i = b % 2
                dve.wait_ge(toks_in, 16 * (b + 1))
                if b >= 2:
                    dve.wait_ge(conv1_mm, b - 1)
                    dve.wait_ge(emb_mm, b - 1)
                t = toki[:, 512 * i:512 * (i + 1)]
                V.tensor_scalar(oh[i][0:64, 3:3 + S], t[0:64, :], c("vocab", slice(0, 64)), None, ALU.is_equal)
                V.tensor_scalar(oh[i][64:128, 2:2 + S], t[64:128, :], c("vocab", slice(64, 128)), None,
                                ALU.is_equal).then_inc(onehot, 1)
                if b >= 1:
                    dve.wait_ge(emb_mm, b)
                    V.tensor_copy(embt[:, ST * (b - 1):ST * b, :],
                                  banks[6][:, 0:ST * 68].rearrange("p (t e) -> p t e", e=68)).then_inc(emb_out, 1)
            dve.wait_ge(emb_mm, B)
            V.tensor_copy(embt[:, ST * (B - 1):ST * B, :],
                          banks[6][:, 0:ST * 68].rearrange("p (t e) -> p t e", e=68)).then_inc(emb_out, 1)
            dve.wait_ge(emb_out, B)
            lp = [embt[:, :, 64 + k] for k in range(4)]
            cen, ph, absw, amp, cxs = tv[:, 0], tv[:, 1], tv[:, 2], tv[:, 3], tv[:, 4]
            rw = [tv[:, 5 + s] for s in range(SCALES)]
            sw2 = tv[:, 10, 0:SCALES]
            link(V.tensor_scalar(tv[:, 9], lp[0], 0.05, None, ALU.mult))
            link(V.tensor_tensor(cen.rearrange("p (b t) -> p b t", t=ST), tv[:, 9].rearrange("p (b t) -> p b t", t=ST),
                                 c("bytepos").unsqueeze(1).to_broadcast([P, B, ST]), ALU.add))
            link(V.tensor_scalar(ph, lp[3], 0.5, 0.25, ALU.mult, ALU.add))
            link(V.tensor_scalar(tv[:, 9], lp[1], -1.0, None, ALU.mult))
            link(V.tensor_tensor(absw, lp[1], tv[:, 9], ALU.max))
            for s in range(SCALES):
                link(V.tensor_scalar(rw[s], absw, c("widths", lo=s, n=1), EPS, ALU.mult, ALU.add))
                link(V.reciprocal(rw[s], rw[s]))
            link(V.tensor_tensor(sw2, c("swts"), c("swts"), ALU.mult))
            dve.wait_ge(tact, 2)
            link(V.tensor_tensor(amp, cxs, tv[:, 11], ALU.mult))
            link(V.tensor_tensor(amps[:, :, :], embt[:, :, 0:D], bc(amp, D), ALU.mult))
            V.tensor_copy(tv[:, 9], amp).then_inc(tvec, 1)

            agd = c("agd")
            o = lambda i: co[:, i:i + 1]
            dve.wait_ge(tact, 3)
            dts = o(0)
            link(V.tensor_tensor(o(1), dts, agd[:, 0:1], ALU.mult))
            link(V.tensor_tensor(o(2), agd[:, 1:2], o(1), ALU.subtract))
            link(V.tensor_scalar(o(2), o(2), 0.0, None, ALU.max))
            link(V.tensor_tensor(o(3), o(1), o(2), ALU.add))
            link(V.tensor_tensor(o(4), o(3), o(3), ALU.mult))
            link(V.tensor_scalar(o(4), o(4), 0.25, None, ALU.mult))
            link(V.tensor_tensor(o(5), agd[:, 0:1], o(4), ALU.subtract))
            link(V.tensor_scalar(o(5), o(5), 0.0, None, ALU.max))
            link(V.tensor_tensor(o(6), o(4), o(5), ALU.add))
            link(V.tensor_tensor(o(7), dts, o(3), ALU.mult))
            link(V.tensor_scalar(o(8), o(7), -1.0, 1.0, ALU.mult, ALU.add))
            link(V.tensor_tensor(o(9), dts, o(6), ALU.mult))
            link(V.tensor_scalar(o(9), o(9), -1.0, None, ALU.mult))
            link(V.memset(co[:, 10:14], 1.0))
            lo, hi = slice(0, 64), slice(64, 128)
            for col, top, bot in ((10, 8, 9), (11, 0, None), (12, 8, 0), (13, 9, None)):
                link(V.tensor_copy(co[lo, col:col + 1], co[lo, top:top + 1]))
                if bot is not None:
                    link(V.tensor_copy(co[hi, col:col + 1], co[hi, bot:bot + 1]))
            CHAINED = 32

            def basis_part(l, stage_name, step, chained):
                m, part = AT_STEP.get((stage_name, step), (0, ""))
                t, e, r = m // 2, eb[:, m % 2, :], rb[:, m % 2, :]

                def chain(ins):
                    chained[0] += 1
                    ins.then_inc(dstep, 1)
                    dve.wait_ge(dstep, CHAINED * l + chained[0])

                def of_byte(v):
                    return v[:, bass.ds(8 * l + t, 1)]

                if part == "u" and m % 2 == 0:
                    if m % 8 == 0:
                        dve.wait_ge(pos_in, 32 * l + 16 * (t // ST) + 16)
                    if m:
                        dve.wait_ge(squared, 16 * l + m)
                    V.tensor_scalar(xd[:, :], posb[:, :], of_byte(cen), None, ALU.subtract).then_inc(xd_ready, 1)
                    dve.wait_ge(xd_ready, 8 * l + t + 1)
                if "u" in part:
                    if m >= 2:
                        dve.wait_ge(product, 16 * l + m - 1)
                    for k in range(2):
                        ins = V.tensor_scalar(r[:, S * k:S * (k + 1)], xd[:, :], of_byte(rw[2 * (m % 2) + k]), of_byte(ph),
                                              ALU.mult, ALU.add)
                    chain(ins)
                if "r" in part:
                    chain(V.tensor_copy(kb[:, :].bitcast(I32), r))
                    V.tensor_tensor(r, r, kb[:, :].bitcast(I32), ALU.subtract).then_inc(r_done, 1)
                if "p" in part and m:
                    e, r = eb[:, (m - 1) % 2, :], rb[:, (m - 1) % 2, :]
                    dve.wait_ge(exp_done, 16 * l + m)
                    dve.wait_ge(sin_done, 16 * l + m)
                    for k in range(2):
                        s = 2 * ((m - 1) % 2) + k
                        ins = V.scalar_tensor_tensor(out=e[:, S * k:S * (k + 1)], in0=e[:, S * k:S * (k + 1)],
                                                     scalar=sw2[:, s:s + 1], in1=r[:, S * k:S * (k + 1)],
                                                     op0=ALU.mult, op1=ALU.mult)
                    ins.then_inc(product, 1)

            with dve.Fori(0, LAYERS) as l:
                chained = [0]
                for g in range(16):
                    for xp in (2 * g, 2 * g + 1)[:2 if g < GA else 1]:
                        dve.wait_ge(t_mm, 32 * l + xp + 1)
                        if g >= 2:
                            dve.wait_ge(f1_mm, 16 * l + g - 1)
                        V.tensor_copy(xt[xp % 4], banks[XB[xp % 4]][:, :]).then_inc(xt_dve, 1)
                    if 0 < g <= GA:
                        dve.wait_ge(f1_mm, 16 * l + g)
                        if g > 4:
                            dve.wait_ge(a_in[(g - 1) % 4], 16 * (4 * l + (g - 1) // 4))
                        V.tensor_copy(af[(g - 1) % 4], banks[2 + (g - 1) % 2][:, :]).then_inc(af_dve, 1)
                    basis_part(l, "forward", g, chained)

                def spectrum(ky):
                    spectrum_room(dve, l, ky)
                    for dst, src in spectrum_parts(ky):
                        ins = V.tensor_copy(dst, src)
                    ins.then_inc(s_dve, 1)

                spectrum(0)
                for ky in range(KY):
                    for nxt in FORWARD_X[ky]:
                        if nxt % 2 == 0:
                            spectrum(nxt)
                    basis_part(l, "mix", 2 * ky, chained)
                    dve.wait_ge(mix_mm, 32 * l + NW + 2 * ky + 2)
                    if ky >= 2:
                        dve.wait_ge(z_out[(ky - 2) % 4], 64 * (4 * l + (ky - 2) // 4 + 1))
                    V.tensor_copy(zs[ky % 2], banks[ky % 2][:, :]).then_inc(zs_ready, 1)
                    basis_part(l, "mix", 2 * ky + 1, chained)
                for q in range(32):
                    dve.wait_ge(o_act, 32 * l + q + 1)
                    V.bn_stats(stats[:, q, :], hbuf[:, q % BP, 512 * (q // BP):512 * (q // BP + 1)]).then_inc(o_stats, 1)
                    basis_part(l, "out", q, chained)
                dve.wait_ge(o_stats, 32 * l + 32)
                V.memset(bn[:, 4:5], 0.0)
                V.bn_aggr(bn[:, 0:2], stats[:, :, :]).then_inc(bn_dve, 1)
                dve.wait_ge(bn_mm, l + 1)
                m, v, om, ov = bn[:, 0:1], bn[:, 1:2], banks[0][:, 0:1], banks[0][:, 1:2]
                V.tensor_tensor(bn[:, 2:4], bn[:, 0:2], banks[0][:, 0:2], ALU.add)
                V.tensor_tensor(bn[:, 4:5], m, om, ALU.subtract).then_inc(bn_dve, 1)
                dve.wait_ge(bn_dve, 6 * l + 2)
                V.tensor_scalar(bn[:, 5:6], bn[:, 4:5], bn[:, 4:5], 0.25, ALU.mult, ALU.mult)
                V.tensor_scalar(bn[:, 6:7], bn[:, 3:4], 0.5, EPS, ALU.mult, ALU.add)
                V.tensor_scalar(bn[:, 7:8], bn[:, 2:3], 0.5, None, ALU.mult).then_inc(bn_dve, 1)
                dve.wait_ge(bn_dve, 6 * l + 3)
                V.tensor_tensor(bn[:, 8:9], bn[:, 5:6], bn[:, 6:7], ALU.add).then_inc(bn_dve, 1)
                dve.wait_ge(bn_act, l + 1)
                V.reciprocal(bn[:, 10:11], bn[:, 9:10]).then_inc(bn_dve, 1)
                dve.wait_ge(bn_dve, 6 * l + 5)
                V.tensor_tensor(bn[:, 11:12], bn[:, 10:11], lcst[:, 129:130], ALU.mult).then_inc(bn_rs, 1)
                dve.wait_ge(bn_rs, 2 * l + 1)
                V.tensor_tensor(bn[:, 12:13], bn[:, 11:12], bn[:, 7:8], ALU.mult).then_inc(bn_rs, 1)
                dve.wait_ge(bn_rs, 2 * l + 2)
                V.tensor_tensor(bn[:, 13:14], lcst[:, 130:131], bn[:, 12:13], ALU.subtract).then_inc(bn_dve, 1)

                assert chained[0] == CHAINED

            dve.wait_ge(tail_in, 16)
            dve.wait_ge(field_mm, 8 * LAYERS + 1)
            dve.wait_ge(o_act, 32 * LAYERS)
            V.tensor_scalar(pm[:, 0, 0:64], c("eye2"), o(10), None, ALU.mult)
            V.tensor_scalar(pm[:, 0, 64:128], c("eye2"), o(11), None, ALU.mult)
            V.tensor_scalar(qm[0][:, 0:64], c("eye2"), o(12), None, ALU.mult)
            V.tensor_scalar(qm[0][:, 64:128], c("eye2"), o(13), None, ALU.mult).then_inc(pw_out, 1)
            for e in range(1, 9):
                dve.wait_ge(pw_mm, e)
                if e < 8:
                    V.tensor_copy(qm[e], banks[4][:, P:2 * P])
                V.tensor_copy(power(e), banks[4][:, 0:P]).then_inc(pw_out, 1)
            for i, (k, n) in enumerate(ODD_POWERS):
                dve.wait_ge(pw_mm, 9 + i)
                V.tensor_copy(pm[:, k - 1:k - 1 + n, :], banks[4 + i % 2][:, 0:P * n].rearrange("p (k n) -> p k n", n=P)
                              ).then_inc(pw_out, 1)
            im = c("cmat", lo=64, n=64)
            link(V.tensor_scalar(im, im, -1.0, None, ALU.mult))

            def layer_norm(src, dst, tmp, tiles, k):
                v = lambda i: lnv[:, i, tiles]
                link(V.reduce_sum(v(0), src, AX_X))
                link(V.tensor_scalar(v(1), v(0), 1.0 / D, None, ALU.mult))
                link(V.tensor_tensor(dst, src, bc(v(1), D), ALU.subtract))
                link(V.tensor_tensor(tmp, dst, dst, ALU.mult))
                link(V.reduce_sum(v(2), tmp, AX_X))
                V.tensor_scalar(v(3), v(2), 1.0 / D, EPS, ALU.mult, ALU.add).then_inc(ln_dve, 1)
                dve.wait_ge(ln_act, k)
                link(V.reciprocal(v(5), v(4)))
                V.tensor_tensor(dst, dst, bc(v(5), D), ALU.mult).then_inc(ln_dve, 1)

            dve.wait_ge(field_out, B)
            layer_norm(tok[:, 0:TT, :], un_t, w1_t, slice(0, TT), 1)
            for g in range(B):
                dve.wait_ge(tp_mm, g + 1)
                V.tensor_copy(ut[:, S * g:S * (g + 1)], banks[6 + g % 2][0:64, :]).then_inc(tp_out, 1)
            for m in range(16):
                dve.wait_ge(bu_mm, m + 1)
                V.tensor_scalar(sx[:, S * m:S * (m + 1)], banks[6 + m % 2][:, :], o(0), None, ALU.mult).then_inc(bu_out, 1)

            def image_tokens(half):
                dve.wait_ge(fc2_mm, 8 * (half + 1))
                for q in range(4):
                    r = slice(32 * q, 32 * q + 8)
                    ins = V.tensor_scalar(ft[half][r, :], banks[4 + half][r, :], c("fc2_b", r), None, ALU.add)
                ins.then_inc(ft_ready, 1)

            for j in range(1, T):
                dve.wait_ge(st_mm, j)
                V.tensor_tensor(sx4[:, :, :, j], banks[6][:, :].rearrange("p (g c) -> p g c", c=CH), sx4[:, :, :, j],
                                ALU.add).then_inc(st_out, 1)
                if j == 5:
                    image_tokens(0)
            dve.wait_ge(st_out, T - 1)
            V.tensor_copy(ends, sx4[:, :, :, T - 1]).then_inc(ke_out, 1)
            for i in range(5):
                d = 2 ** i
                dve.wait_ge(ke_mm, i + 1)
                V.tensor_tensor(ends[:, :, d:CH], banks[7][:, 0:16 * (CH - d)].rearrange("p (g c) -> p g c", g=16),
                                ends[:, :, d:CH], ALU.add).then_inc(ke_out, 1)
            image_tokens(1)

            dve.wait_ge(img_in, 16 * B)
            layer_norm(tok[:, TT:TILES, :], un_i, w1_i, slice(TT, TILES), 2)
            dve.wait_ge(tpi_mm, 1)
            V.tensor_copy(ut[:, B * S:B * L], banks[0][0:64, :]).then_inc(tpi_out, 1)
            dve.wait_ge(bi_out, 2)
            for i in range(6):
                d = 2 ** i
                for ri in range(2):
                    dve.wait_ge(ki_mm, 2 * i + ri + 1)
                    V.tensor_tensor(si[:, 8 * ri:8 * ri + 8, d:X],
                                    banks[2 * (i % 2) + ri][:, 0:8 * (X - d)].rearrange("p (g t) -> p g t", g=8),
                                    si[:, 8 * ri:8 * ri + 8, d:X], ALU.add).then_inc(ki_out, 1)
            dve.wait_ge(ki_out, 12)
            V.tensor_copy(carry[:, :, 0], si[:, :, X - 1]).then_inc(cy_out, 1)
            for i in range(5):
                d = 2 ** i
                dve.wait_ge(cy_mm, i + 1)
                V.tensor_copy(carry[:, :, d:2 * d], banks[4 + i % 2][:, 0:16 * d].rearrange("p (g c) -> p g c", g=16)
                              ).then_inc(cy_out, 1)
            dve.wait_ge(cy_out, 6)
            V.tensor_tensor(carry[:, :, 1:CH], carry[:, :, 1:CH], ends[:, :, 0:CH - 1], ALU.add).then_inc(cy_out, 1)
            for j in range(T):
                dve.wait_ge(fx_mm, j + 1)
                V.tensor_tensor(sx4[:, :, :, j], banks[j % 4][:, :].rearrange("p (g c) -> p g c", g=16),
                                sx4[:, :, :, j], ALU.add).then_inc(fx_out, 1)
            dve.wait_ge(skip, 2)
            for g in range(5):
                w = w1_t[:, 8 * g:8 * g + 8, :] if g < 4 else w1_i
                n = 8 if g < 4 else 4
                dve.wait_ge(ao_mm, g + 1)
                V.tensor_tensor(h2[:, 8 * g:8 * g + n, :], banks[g][:, 0:64 * n].rearrange("p (t d) -> p t d", d=D),
                                w, ALU.add).then_inc(ao_out, 1)
            dve.wait_ge(ao_out, 5)
            layer_norm(h2, un, w1, slice(0, TILES), 3)
            for g in range(9):
                dve.wait_ge(tp2_mm, g + 1)
                V.tensor_copy(u2t[:, 512 * g:512 * (g + 1)], banks[g % 4][0:64, :]).then_inc(tp2_out, 1)
            dve.wait_ge(lg_mm, 9)
            link(V.tensor_copy(lg, banks[6][:, 0:216].rearrange("p (t e) -> p t e", e=E)))
            mx, sm, rs, p1, p2, seen = (gs[:, k] for k in range(6))
            link(V.tensor_reduce(mx, lg, axis=AX_X, op=ALU.max))
            V.tensor_tensor(lg, lg, bc(mx, E), ALU.subtract).then_inc(gate, 1)
            dve.wait_ge(gate_act, 1)
            link(V.reduce_sum(sm, pr, AX_X))
            link(V.reciprocal(rs, sm))
            link(V.tensor_tensor(pr, pr, bc(rs, E), ALU.mult))
            cur = pr
            for rank in range(2):
                top = (p1, p2)[rank]
                eq, sel, nxt = gv[:, 3 * rank], gv[:, 3 * rank + 1], gv[:, 3 * rank + 2]
                link(V.tensor_reduce(top, cur, axis=AX_X, op=ALU.max))
                link(V.tensor_tensor(eq, cur, bc(top, E), ALU.is_equal))
                link(V.memset(seen, 0.0))
                for e in range(E):
                    link(V.tensor_tensor(sel[:, :, e], eq[:, :, e], seen, ALU.is_gt))
                    if e < E - 1:
                        link(V.tensor_tensor(seen, seen, eq[:, :, e], ALU.max))
                if rank == 0:
                    link(V.scalar_tensor_tensor(out=nxt, in0=sel, scalar=-4.0, in1=cur, op0=ALU.mult, op1=ALU.add))
                    cur = nxt
            V.tensor_tensor(gs[:, 6], p2, p1, ALU.subtract).then_inc(gate, 1)
            dve.wait_ge(gate_act, 2)
            link(V.tensor_scalar(gs[:, 8], gs[:, 7], 1.0, None, ALU.add))
            link(V.reciprocal(gs[:, 9], gs[:, 8]))
            link(V.tensor_tensor(gs[:, 10], gs[:, 7], gs[:, 9], ALU.mult))
            link(V.tensor_tensor(gv[:, 0], gv[:, 1], bc(gs[:, 9], E), ALU.mult))
            link(V.tensor_tensor(gv[:, 3], gv[:, 4], bc(gs[:, 10], E), ALU.mult))
            V.memset(gates[:, :, 0], 1.0)
            V.tensor_tensor(gates[:, :, 1:E + 1], gv[:, 0], gv[:, 3], ALU.add).then_inc(gate, 1)
            dve.wait_ge(gate, 3)
            for g in range(9):
                dve.wait_ge(gt_mm, g + 1)
                V.tensor_copy(gtt[:, 512 * g:512 * (g + 1)], banks[7 - g % 2][0:E, :]).then_inc(gt_out, 1)
            for n in range(10):
                if n < 9:
                    for t in range(4):
                        i = 4 * n + t
                        dve.wait_ge(e3_mm, i + 1)
                        if n >= 2 and t == 0:
                            dve.wait_ge(res, n - 1)
                        V.tensor_tensor(prod[n % 2][:, t], banks[4 + t][:, 0:(E + 1) * D].rearrange("p (e d) -> p e d", d=D),
                                        gates[:, i, :].unsqueeze(2).to_broadcast([P, E + 1, D]), ALU.mult).then_inc(gated, 1)
                if n:
                    w = w1[:, 4 * n - 4:4 * n, :]
                    dve.wait_ge(halved, n)
                    V.tensor_reduce(w, prod[(n - 1) % 2][:, :, 0:4, :].rearrange("p t e d -> p t d e"), axis=AX_X, op=ALU.add
                                    ).then_inc(reduced, 1)
                    dve.wait_ge(reduced, n)
                    V.tensor_tensor(w1t[:, 4 * n - 4:4 * n, :], w, h2[:, 4 * n - 4:4 * n, :], ALU.add).then_inc(res, 1)

        @block.scalar
        def _(act):
            A = nc.scalar.activation
            act.wait_ge(text_in, 16)
            act.wait_ge(pad0, 2)
            def lift(n):
                xg, bp = n % 8, n // 8
                act.wait_ge(fc0_mm, n + 1)
                A(hbuf[:, bp, 512 * xg:512 * (xg + 1)], banks[4 + n % 2][:, :], ACT.Identity,
                  bias=c("fc0_b")).then_inc(fc0_act, 1)

            for q in range(BP):
                for i in range(2):
                    act.wait_ge(conv1_mm, 2 * q + i + 1)
                    if q:
                        act.wait_ge(conv2_mm, q)
                    A(g1[i][:, 2:2 + S], banks[i][:, :], ACT.Gelu, bias=c("cb1")).then_inc(conv1_act, 1)
                for n in range(8 * q, 8 * q + 4):
                    lift(n)
                act.wait_ge(conv2_mm, q + 1)
                if q >= 2:
                    act.wait_ge(ctx_mm, q - 1)
                A(g2[q % 2][:, 1:1 + S], banks[2 + q % 2][:, :], ACT.Gelu, bias=c("cb2")).then_inc(conv2_act, 1)
                for n in range(8 * q + 4, 8 * q + 8):
                    lift(n)
            act.wait_ge(ctx_mm, BP)
            act.wait_ge(emb_out, B)
            A(tv[:, 4].rearrange("p (q i s) -> p q i s", q=BP, i=2),
              banks[7][:, 0:TT].rearrange("p (q s i) -> p q i s", q=BP, i=2), ACT.Sigmoid, bias=c("cb3")).then_inc(tact, 1)
            A(tv[:, 11], embt[:, :, 66], ACT.Sigmoid).then_inc(tact, 1)
            A(tv[:, 10, 8:9], c("agd", lo=2, n=1), ACT.Sigmoid).then_inc(tact, 1)
            act.wait_ge(fc0_act, 32)
            nc.scalar.copy(bn[:, 14:15], c("fc0_b")).then_inc(h_ready, 16)
            nc.scalar.copy(bn[:, 15:16], c("fc0_b")).then_inc(mix_mm, NW)

            def basis_part(l, stage_name, step):
                m, part = AT_STEP.get((stage_name, step), (0, ""))
                if part == "s":
                    if m % 2 == 0:
                        act.wait_ge(xd_ready, 8 * l + m // 2 + 1)
                        act.wait_ge(e_free, 8 * l + m // 2 + 1)
                    else:
                        act.wait_ge(summed, 8 * l + m // 2 + 1)
                    for k in range(2):
                        ins = A(eb[:, m % 2, S * k:S * (k + 1)], xd[:, :], ACT.Square,
                                scale=tv[:, 5 + 2 * (m % 2) + k, bass.ds(8 * l + m // 2, 1)])
                    ins.then_inc(squared, 1)
                if part == "p" and m < UNITS:
                    for f in (("exp", "sin"), ("sin", "exp"))[m % 2]:
                        if f == "exp":
                            act.wait_ge(squared, 16 * l + m + 1)
                            A(eb[:, m % 2, :], eb[:, m % 2, :], ACT.Exp, scale=-0.5).then_inc(exp_done, 1)
                        else:
                            act.wait_ge(r_done, 16 * l + m + 1)
                            A(rb[:, m % 2, :], rb[:, m % 2, :], ACT.Sin, scale=TWO_PI_IN).then_inc(sin_done, 1)

            def field_down(l, i):
                act.wait_ge(field_mm, 8 * l + 4 * i + 5)
                A(fieldt[:, :], banks[7][0:64, :], ACT.Copy).then_inc(field_sb, 1)

            def field_tokens(l, i):
                act.wait_ge(field_tr, 2 * l + i + 1)
                A(tok[:, bass.ds(8 * l + 4 * i, ST), :], banks[7][:, 0:ST * D].rearrange("p (t d) -> p t d", d=D),
                  ACT.Copy).then_inc(field_out, 1)

            with act.Fori(0, LAYERS) as l:
                for g in range(GA, 17):
                    if g < 16:
                        act.wait_ge(t_mm, 32 * l + 2 * g + 2)
                        act.wait_ge(f1_mm, 16 * l + g - 1)
                        A(xt[(2 * g + 1) % 4], banks[XB[(2 * g + 1) % 4]][:, :], ACT.Copy).then_inc(xt_act, 1)
                    if g > GA:
                        act.wait_ge(f1_mm, 16 * l + g)
                        act.wait_ge(a_in[(g - 1) % 4], 16 * (4 * l + (g - 1) // 4))
                        A(af[(g - 1) % 4], banks[2 + (g - 1) % 2][:, :], ACT.Copy).then_inc(af_act, 1)
                        basis_part(l, "forward", g - 1)

                def spectrum(ky):
                    spectrum_room(act, l, ky)
                    for dst, src in spectrum_parts(ky):
                        ins = A(dst, src, ACT.Copy)
                    ins.then_inc(s_act, 1)

                def y_move(ky):
                    act.wait_ge(ys_ready, 16 * l + ky + 1)
                    act.dma_start(abuf[ky::16, :, :].rearrange("p a n -> p (a n)"), ys[ky % NY]).then_inc(y_in[ky % NY], 16)

                spectrum(1)
                for step in range(STEPS):
                    for nxt in FORWARD_X[step]:
                        if nxt % 2 == 1:
                            spectrum(nxt)
                    basis_part(l, "mix", 2 * step - 1)
                    for ky in INVERSE_X[step]:
                        act.wait_ge(i1_mm, 16 * l + ky + 1)
                        if ky >= NY:
                            act.wait_ge(y_in[ky % NY], 16 * (KY // NY * l + ky // NY))
                        A(ys[ky % NY], banks[2 + ky % 2][:, :], ACT.Copy).then_inc(ys_ready, 1)
                        if ky:
                            y_move(ky - 1)
                y_move(KY - 1)
                act.wait_ge(lc_in, 16 * (l + 1))
                for q in range(32):
                    xg, bp = q // BP, q % BP
                    act.wait_ge(o_mm, 32 * l + q + 1)
                    A(hbuf[:, bp, 512 * xg:512 * (xg + 1)], banks[OB[q % NO]][:, :], ACT.Identity,
                      bias=lcst[:, 128:129]).then_inc(o_act, 1)
                    basis_part(l, "out", q)
                    if q == 2:
                        field_down(l, 0)
                    if q == 6:
                        field_tokens(l, 0)
                act.wait_ge(bn_dve, 6 * l + 4)
                A(bn[:, 9:10], bn[:, 8:9], ACT.Sqrt).then_inc(bn_act, 1)
                field_down(l, 1)
                act.wait_ge(bn_dve, 6 * l + 6)
                act.wait_ge(o_act, 32 * l + 32)
                for g in range(16):
                    px = hbuf[:, :, 256 * g:256 * (g + 1)]
                    A(px, px, ACT.Gelu, scale=bn[:, 11:12], bias=bn[:, 13:14]).then_inc(h_ready, 1)
                    if g == 2:
                        field_tokens(l, 1)
            act.wait_ge(ln_dve, 1)
            A(lnv[:, 4, 0:TT], lnv[:, 3, 0:TT], ACT.Sqrt).then_inc(ln_act, 1)
            act.wait_ge(tail_in, 16)
            for n in range(64):
                act.wait_ge(fc1_mm, n + 1)
                if n >= NH and n % 4 == 0:
                    act.wait_ge(fc2_mm, (n - NH) // 4 + 1)
                A(hid[n % NH], banks[n % 4][:, :], ACT.Gelu, bias=c("fc1_b")).then_inc(fc1_act, 1)
            act.wait_ge(ln_dve, 3)
            A(lnv[:, 4, TT:TILES], lnv[:, 3, TT:TILES], ACT.Sqrt).then_inc(ln_act, 1)
            for ri in range(2):
                act.wait_ge(bi_mm, ri + 1)
                A(si[:, 8 * ri:8 * ri + 8, :], banks[2 + ri][:, :].rearrange("p (g t) -> p g t", t=X), ACT.Copy,
                  scale=co[:, 0:1]).then_inc(bi_out, 1)
            act.wait_ge(ln_dve, 5)
            A(lnv[:, 4], lnv[:, 3], ACT.Sqrt).then_inc(ln_act, 1)
            for n in range(9):
                act.wait_ge(rh_mm, n + 1)
                if n >= 2:
                    act.wait_ge(lg_mm, n - 1)
                else:
                    nc.scalar.activation(rh[n][32:33, :], cst[32:33, 0:512], ACT.Copy, scale=0.0, bias=1.0)
                A(rh[n % 2][0:32, :], banks[4 + n % 2][0:32, :], ACT.Relu, bias=c("rb1", slice(0, 32))).then_inc(rh_act, 1)
            for m in range(NM + 1):
                if m < NM:
                    act.wait_ge(e1_mm, m + 1)
                    if m >= 4:
                        act.wait_ge(e2_mm, m - 3)
                    A(hr[m % 4], banks[m % 2][:, :], ACT.Relu, bias=c("eb1", lo=m % EP, n=1)).then_inc(e1_act, 1)
                if m:
                    act.wait_ge(e2_mm, m)
                    A(ha[:, 512 * (m - 1):512 * m], banks[2 + (m - 1) % 2][:, :], ACT.Relu,
                      bias=c("eb2", lo=(m - 1) % EP, n=1)).then_inc(e2_act, 1)
                if m == 1:
                    act.wait_ge(gate, 1)
                    A(pr, lg, ACT.Exp).then_inc(gate_act, 1)
                if m == 9:
                    act.wait_ge(gate, 2)
                    A(gs[:, 7], gs[:, 6], ACT.Exp).then_inc(gate_act, 1)

        @block.tensor
        def _(pe):
            mm, tr = nc.tensor.matmul, nc.tensor.transpose
            pe.wait_ge(text_in, 16)
            def lift(n):
                xg, bp = n % 8, n // 8
                if xg == 0:
                    pe.wait_ge(x_in, 16 * (bp + 1))
                if n >= 2:
                    pe.wait_ge(fc0_act, n - 1)
                mm(banks[4 + n % 2][:, :], c("fc0", slice(0, 6)), xin[bp % 2][:, 512 * xg:512 * (xg + 1)],
                   start=True, stop=True).then_inc(fc0_mm, 1)

            for q in range(BP):
                for i in range(2):
                    b = 2 * q + i
                    pe.wait_ge(onehot, b + 1)
                    if q:
                        pe.wait_ge(conv1_act, b - 1)
                    for t in range(4):
                        ins = mm(banks[i][:, :], c("cw1", lo=128 * t, n=128), oh[i][:, 2 * t:2 * t + S],
                                 start=(t == 0), stop=(t == 3))
                    ins.then_inc(conv1_mm, 1)
                    if b >= 1:
                        pe.wait_ge(emb_out, b)
                    for st in range(ST):
                        ins = mm(banks[6][:, 68 * st:68 * (st + 1)], oh[i][0:64, 3 + P * st:3 + P * (st + 1)],
                                 c("emb", slice(0, 64)), start=True, stop=True)
                    ins.then_inc(emb_mm, 1)
                for n in range(8 * q, 8 * q + 4):
                    lift(n)
                pe.wait_ge(conv1_act, 2 * q + 2)
                if q >= 2:
                    pe.wait_ge(conv2_act, q - 1)
                for t in range(5):
                    for i in range(2):
                        ins = mm(banks[2 + q % 2][64 * i:64 * i + 64, :], c("cw2", lo=64 * t, n=64), g1[i][:, t:t + S],
                                 start=(t == 0), stop=(t == 4))
                ins.then_inc(conv2_mm, 1)
                for n in range(8 * q + 4, 8 * q + 8):
                    lift(n)
                pe.wait_ge(conv2_act, q + 1)
                for st in range(ST):
                    at = 2 * (ST * q + st)
                    for t in range(3):
                        ins = mm(banks[7][:, at:at + 2], g2[q % 2][:, P * st + t:P * st + t + P], c("cw3", lo=2 * t, n=2),
                                 start=(t == 0), stop=(t == 2))
                ins.then_inc(ctx_mm, 1)
            pe.wait_ge(const_in, 16)

            def field(l, t):
                pe.wait_ge(summed, 8 * l + t + 2)
                if t == ST:
                    pe.wait_ge(field_out, 2 * l + 1)
                mm(banks[7][0:D, :], ampr[:, t % 2, :], basis[:, :], start=(t % ST == 0), stop=(t % ST == ST - 1)
                   ).then_inc(field_mm, 1)

            def field_transpose(l, i):
                pe.wait_ge(field_sb, 2 * l + i + 1)
                for pt in range(ST):
                    ins = mm(banks[7][:, D * pt:D * (pt + 1)], fieldt[:, P * pt:P * (pt + 1)], c("ident", slice(0, D), n=D),
                             start=True, stop=True)
                ins.then_inc(field_tr, 1)

            def basis_part(l, stage_name, step):
                m, part = AT_STEP.get((stage_name, step), (0, ""))
                if "p" in part and m < UNITS and m % 2 and m >= 3:
                    field(l, (m - 3) // 2)

            with pe.Fori(0, LAYERS) as l:
                def to_rows(xp):
                    if xp % 2 == 0:
                        pe.wait_ge(h_ready, 16 * l + xp // 2 + 1)
                    if xp >= 4 and xp % 2 == 0:
                        rows_done(pe, l, xp // 2 - 2)
                    for bp in range(BP):
                        ins = tr(banks[XB[xp % 4]][:, P * bp:P * (bp + 1)], hbuf[:, bp, P * xp:P * (xp + 1)], c("ident"))
                    ins.then_inc(t_mm, 1)

                to_rows(0)
                to_rows(1)
                for g in range(NPAIR // 2):
                    if g < NPAIR // 2 - 1:
                        to_rows(2 * g + 2)
                        to_rows(2 * g + 3)
                    rows_done(pe, l, g)
                    if g >= 2:
                        y_done(pe, l, g - 2)
                    for half in range(2):
                        ins = mm(banks[2 + g % 2][64 * half:64 * half + 64, :], c("dft_y"), xt[(2 * g + half) % 4],
                                 start=True, stop=True)
                    ins.then_inc(f1_mm, 1)
                    basis_part(l, "forward", g)
                for i in range(4):
                    pe.wait_ge(a_in[i], 64 * (l + 1))
                def forward_x(ky):
                    if ky >= 2:
                        spectrum_done(pe, l, ky - 1)
                    for bp in range(BP):
                        ins = mm(banks[4 + ky % 2][:, P * bp:P * (bp + 1)], abuf[:, ky, P * bp:P * (bp + 1)],
                                 c("dft_x"), start=True, stop=True)
                    ins.then_inc(f2_mm, 1)

                def inverse_x(pair):
                    for ky in pair:
                        pe.wait_ge(z_in[ky % 4], 16 * (4 * l + ky // 4 + 1))
                    lo = 512 * (2 + pair[0] // 2 % 2)
                    for ky in pair:
                        if ky >= 2:
                            pe.wait_ge(ys_ready, 16 * l + ky - 1)
                        mm(banks[2 + ky % 2][:, :], c("idft_x", lo=P * (ky % 2), n=P), stage[:, lo:lo + 512],
                           start=True, stop=True).then_inc(i1_mm, 1)

                def pointwise(q):
                    xg, bp = q // BP, q % BP
                    mm(banks[OB[q % NO]][:, :], lcst[:, 0:P], hbuf[:, bp, 512 * xg:512 * (xg + 1)], start=True, stop=False)

                forward_x(0)
                forward_x(1)
                for ky in range(STEPS):
                    for nxt in FORWARD_X[ky]:
                        forward_x(nxt)
                    if ky < KY:
                        spectrum_done(pe, l, ky + 1)
                        if ky >= 2:
                            pe.wait_ge(zs_ready, 16 * l + ky - 1)
                        for half in range(2):
                            n = 2 * ky + half
                            pe.wait_ge(w_in[n % NW], 16 * (2 * KY // NW * l + n // NW + 1))
                            for k in range(4 * half, 4 * half + 4):
                                for q in range(4):
                                    kx = 8 * q + k
                                    ins = mm(banks[ky % 2][32 * q:32 * q + 16, 64 * k:64 * (k + 1)],
                                             spec[:, ky % NS, 2 * kx:2 * kx + 2, :].rearrange("p r b -> p (r b)"),
                                             wring[:, n % NW, C * (4 * (k % 4) + q):C * (4 * (k % 4) + q + 1)],
                                             start=True, stop=True)
                            ins.then_inc(mix_mm, 1)
                        basis_part(l, "mix", 2 * ky + 1)
                    if ky >= KY:
                        if ky == KY:
                            pe.wait_ge(lc_in, 16 * (l + 1))
                            pe.wait_ge(zs_ready, 16 * (l + 1))
                        for q in range(2 * (ky - KY), 2 * (ky - KY) + 2):
                            pointwise(q)
                    if INVERSE_X[ky]:
                        inverse_x(INVERSE_X[ky])
                for i in range(NY):
                    pe.wait_ge(y_in[i], 16 * KY // NY * (l + 1))
                for q in range(32):
                    xg, bp = q // BP, q % BP
                    if q >= 4:
                        if q >= NO:
                            pe.wait_ge(o_act, 32 * l + q - NO + 1)
                        pointwise(q)
                    for h in range(2):
                        ins = mm(banks[OB[q % NO]][:, 256 * h:256 * (h + 1)], abuf[:, 2 * xg + h, P * bp:P * (bp + 1)],
                                 c("idft_y"), start=False, stop=(h == 1))
                        if q == 0 and h == 0:
                            ins.then_inc(inverse_in, 1)
                    ins.then_inc(o_mm, 1)
                    basis_part(l, "out", q)
                    if q == 4:
                        field_transpose(l, 0)
                pe.wait_ge(bn_dve, 6 * l + 1)
                for half in (0, 64):
                    ins = mm(banks[0][half:half + 64, 0:2], c("ident", lo=64 - half, n=64), bn[:, 0:2], start=True, stop=True)
                ins.then_inc(bn_mm, 1)
                field(l, 2 * ST - 1)
                field_transpose(l, 1)

            for e in range(1, 9):
                pe.wait_ge(pw_out, e)
                ins = mm(banks[4][:, 0:P], qm[e - 1], power(e - 1), start=True, stop=True)
                if e < 8:
                    ins = mm(banks[4][:, P:2 * P], power(e - 1), qm[e - 1], start=True, stop=True)
                ins.then_inc(pw_mm, 1)
            for i, (k, n) in enumerate(ODD_POWERS):
                pe.wait_ge(pw_out, 9 + i)
                e = k.bit_length() - 1
                lo = k - 2 ** e
                mm(banks[4 + i % 2][:, 0:P * n], qm[e], pm[:, lo - 1:lo - 1 + n, :].rearrange("p k n -> p (k n)"),
                   start=True, stop=True).then_inc(pw_mm, 1)

            def text_part(n):
                if n in range(12, 20):
                    g = n - 12
                    if g == 0:
                        pe.wait_ge(pw_out, 9 + len(ODD_POWERS))
                        pe.wait_ge(ln_dve, 2)
                    elif g >= 2:
                        pe.wait_ge(tp_out, g - 1)
                    for k in range(4):
                        ins = tr(banks[6 + g % 2][0:64, P * k:P * (k + 1)], un_t[:, 4 * g + k, :], c("ident"))
                    ins.then_inc(tp_mm, 1)
                if n in range(20, 28):
                    for m in (2 * n - 40, 2 * n - 39):
                        if m == 0:
                            pe.wait_ge(tp_out, B)
                        elif m >= 2:
                            pe.wait_ge(bu_out, m - 1)
                        mm(banks[6 + m % 2][:, :], c("bmat", slice(0, 64), lo=P * (m // B), n=P),
                           ut[:, S * (m % B):S * (m % B + 1)], start=True, stop=True).then_inc(bu_mm, 1)
                if n >= 32 and n % 2 == 0 and n // 2 - 15 < T:
                    j = n // 2 - 15
                    if j == 1:
                        pe.wait_ge(bu_out, 16)
                    else:
                        pe.wait_ge(st_out, j - 1)
                    mm(banks[6][:, :], power(0), sx4[:, :, :, j - 1], start=True, stop=True).then_inc(st_mm, 1)

            pe.wait_ge(tail_in, 16)
            pe.wait_ge(h_ready, 16 * (LAYERS + 1))
            def head2(k):
                half, xg = k // 8, k % 8
                pe.wait_ge(fc1_act, 4 * k + 4)
                for q in range(4):
                    ins = mm(banks[4 + half][32 * q:32 * q + 8, :], c("fc2", lo=7 - xg, n=8), hid[(4 * k + q) % NH],
                             start=(xg == 0), stop=(xg == 7))
                ins.then_inc(fc2_mm, 1)

            for n in range(64):
                k, q = n // 4, n % 4
                b, xg = 4 * (k // 8) + q, k % 8
                if n >= 4:
                    pe.wait_ge(fc1_act, n - 3)
                mm(banks[n % 4][:, :], c("fc1", lo=P * (b % 2), n=P), hbuf[:, b // 2, 512 * xg:512 * (xg + 1)],
                   start=True, stop=True).then_inc(fc1_mm, 1)
                if n >= 4 and q == 1:
                    head2(k - 1)
                text_part(n)
            head2(15)
            for i in range(5):
                pe.wait_ge(ke_out, i + 1)
                mm(banks[7][:, 0:16 * (CH - 2 ** i)], power(4 + i), ends[:, :, 0:CH - 2 ** i], start=True, stop=True
                   ).then_inc(ke_mm, 1)
            pe.wait_ge(ln_dve, 4)
            for k in range(4):
                ins = tr(banks[0][0:64, P * k:P * (k + 1)], un_i[:, k, :], c("ident"))
            ins.then_inc(tpi_mm, 1)
            pe.wait_ge(tpi_out, 1)
            for ri in range(2):
                mm(banks[2 + ri][:, :], c("bmat", slice(0, 64), lo=P * ri, n=P), ut[:, B * S:B * L],
                   start=True, stop=True).then_inc(bi_mm, 1)
            pe.wait_ge(bi_out, 2)
            for i in range(6):
                d = 2 ** i
                for ri in range(2):
                    if i:
                        pe.wait_ge(ki_out, 2 * i - 1 + ri)
                    mm(banks[2 * (i % 2) + ri][:, 0:8 * (X - d)], power(i), si[:, 8 * ri:8 * ri + 8, 0:X - d],
                       start=True, stop=True).then_inc(ki_mm, 1)
            for i in range(5):
                pe.wait_ge(cy_out, i + 1)
                mm(banks[4 + i % 2][:, 0:16 * 2 ** i], power(4 + i), carry[:, :, 0:2 ** i], start=True, stop=True
                   ).then_inc(cy_mm, 1)
            pe.wait_ge(cy_out, 7)
            for j in range(T):
                if j >= 4:
                    pe.wait_ge(fx_out, j - 3)
                mm(banks[j % 4][:, :], pm[:, j, :], carry, start=True, stop=True).then_inc(fx_mm, 1)
            pe.wait_ge(fx_out, T)
            for i in range(TILES):
                if i < TT:
                    t0 = P * (i % ST)
                    parts = [(slice(0, P), [sx[:, S * (B * ri + i // ST) + t0:S * (B * ri + i // ST) + t0 + P] for ri in range(2)])]
                else:
                    parts = [(slice(64 * b2, 64 * b2 + 64), [si[:, B * ri + 2 * (i - TT) + b2, :] for ri in range(2)])
                             for b2 in range(2)]
                for rows, x in parts:
                    for ri in range(2):
                        ins = mm(banks[i // 8][rows, 64 * (i % 8):64 * (i % 8 + 1)], x[ri], c("cmat", lo=64 * ri, n=64),
                                 start=(ri == 0), stop=(ri == 1))
                if i % 8 == 7 or i == TILES - 1:
                    ins.then_inc(ao_mm, 1)
            pe.wait_ge(ln_dve, 6)
            for g in range(9):
                if g >= 4:
                    pe.wait_ge(tp2_out, g - 3)
                for k in range(4):
                    ins = tr(banks[g % 4][0:64, P * k:P * (k + 1)], un[:, 4 * g + k, :], c("ident"))
                ins.then_inc(tp2_mm, 1)
            pe.wait_ge(tp2_out, 9)

            def cols(n):
                return u2t[:, 512 * n:512 * (n + 1)]

            def logits(n):
                pe.wait_ge(rh_act, n + 1)
                for k in range(4):
                    i = 4 * n + k
                    ins = mm(banks[6][:, E * i:E * (i + 1)], rh[n % 2][:, P * k:P * (k + 1)], c("rw2", slice(0, 33)),
                             start=True, stop=True)
                ins.then_inc(lg_mm, 1)

            for n in range(9):
                if n >= 2:
                    pe.wait_ge(rh_act, n - 1)
                mm(banks[4 + n % 2][0:32, :], c("rw1", slice(0, 64)), cols(n), start=True, stop=True).then_inc(rh_mm, 1)
                if n:
                    logits(n - 1)
            logits(8)

            def gates_to_rows():
                pe.wait_ge(gate, 3)
                for g in range(9):
                    if g >= 2:
                        pe.wait_ge(gt_out, g - 1)
                    for k in range(4):
                        ins = tr(banks[7 - g % 2][0:E, P * k:P * (k + 1)], gates[:, 4 * g + k, 1:E + 1], c("ident"))
                    ins.then_inc(gt_mm, 1)
                pe.wait_ge(gt_out, 9)

            def outputs(n):
                for t in range(4):
                    if n:
                        pe.wait_ge(gated, 4 * (n - 1) + t + 1)
                    for k in range(EP):
                        m = EP * n + k
                        mm(banks[4 + t][:, D + P * k:D + P * (k + 1)], ha[:, 512 * m + P * t:512 * m + P * (t + 1)],
                           c("ew3", lo=P * k, n=P), start=True, stop=True)
                    mm(banks[4 + t][:, 0:D], gtt[:, 512 * n + P * t:512 * n + P * (t + 1)],
                       c("eb3", slice(64, 70)), start=True, stop=True).then_inc(e3_mm, 1)

            for m in range(NM + 1):
                if m < NM:
                    if m >= 2:
                        pe.wait_ge(e1_act, m - 1)
                    mm(banks[m % 2][:, :], c("ew1", slice(0, 64), lo=P * (m % EP), n=P), cols(m // EP),
                       start=True, stop=True).then_inc(e1_mm, 1)
                if m:
                    pe.wait_ge(e1_act, m)
                    if m >= 3:
                        pe.wait_ge(e2_act, m - 2)
                    mm(banks[2 + (m - 1) % 2][:, :], c("ew2", lo=P * ((m - 1) % EP), n=P), hr[(m - 1) % 4],
                       start=True, stop=True).then_inc(e2_mm, 1)
                if m == 15:
                    gates_to_rows()
                if m > 15 and m % 3 != 0:
                    n = 2 * (m // 3 - 5) + m % 3 - 1
                    outputs(n)
            pe.wait_ge(e2_act, NM)
            outputs(8)


def spectra():
    th = 2 * np.pi / X
    x = np.arange(X)
    ky = np.arange(KY)
    kx = np.concatenate([np.arange(16), np.arange(48, 64)])
    dft_y = np.zeros((2, Y, 2, 2, KY))
    ang = th * np.outer(x, ky)
    for i in range(2):
        dft_y[i, :, i, 0] = np.cos(ang)
        dft_y[i, :, i, 1] = -np.sin(ang)
    ax = th * np.outer(x, kx)
    cs, sn = np.cos(ax), np.sin(ax)
    fwd = np.zeros((X, 2, 2, KX, 2))
    fwd[:, 0, 0, :, 0], fwd[:, 1, 0, :, 0] = cs, sn
    fwd[:, 0, 0, :, 1], fwd[:, 1, 0, :, 1] = -sn, cs
    fwd[:, :, 1, :, 0], fwd[:, :, 1, :, 1] = -fwd[:, :, 0, :, 1], fwd[:, :, 0, :, 0]
    dft_x = fwd.reshape(16, 4, 2, -1).transpose(1, 2, 0, 3).reshape(P, 128)
    inv = np.zeros((KX, 2, X, 2))
    inv[:, 0, :, 0], inv[:, 1, :, 0] = cs.T / X, -sn.T / X
    inv[:, 0, :, 1], inv[:, 1, :, 1] = sn.T / X, cs.T / X
    inv = inv.reshape(4, 8, 2, 16, 4, 2).transpose(1, 0, 2, 4, 5, 3).reshape(64, P)
    idft_y = np.zeros((4, 2, KY, 4, Y))
    wt = np.where(ky == 0, 1.0, 2.0)[:, None] / Y
    for i in range(4):
        idft_y[i, 0, :, i] = wt * np.cos(ang.T)
        idft_y[i, 1, :, i] = -wt * np.sin(ang.T)
    return dft_y.reshape(P, 64), dft_x, inv, idft_y.reshape(P, 256)


def kernel(**inputs):
    import concourse.bacc as bacc
    from concourse.bass_utils import run_bass_kernel_spmd

    a = {k: np.asarray(v) for k, v in inputs.items()}
    tk = {k[7:]: v for k, v in a.items() if k.startswith("L0_tok_")}
    tx = {k[7:]: v for k, v in a.items() if k.startswith("L0_txt_")}
    at = {k[8:]: v for k, v in a.items() if k.startswith("L0_attn_")}
    ff = {k[7:]: v for k, v in a.items() if k.startswith("L0_ffn_")}
    f4 = np.float32
    csts = {tile: np.zeros((P, w), f4) for tile, w in WIDTH.items()}

    def put(name, v, row=0, col=0):
        v = v.reshape(v.shape[0], -1)
        tile, lo, _ = AT[name]
        lo += col
        csts[tile][row:row + v.shape[0], lo:lo + v.shape[1]] = v

    dft_y, dft_x, idft_x, idft_y = spectra()
    put("ident", np.eye(P, dtype=f4))
    put("dft_y", dft_y.astype(f4)); put("dft_x", dft_x.astype(f4))
    put("idft_x", idft_x.astype(f4)); put("idft_x", idft_x.astype(f4), 64, P)
    put("idft_y", idft_y.astype(f4))
    for b2 in range(2):
        r = 64 * b2
        put("fc0", tk["fc0_w"], 3 * b2, r)
        put("fc0_b", tk["fc0_b"][:, None], r)
        put("fc1", tk["fc1_w"], r, P * b2)
        for e in range(4):
            t = 2 * e + b2
            if t < 7:
                put("cw1", tx["w1"][:, :, t].T, r, P * e)
        put("vocab", np.arange(64, dtype=f4)[:, None], r)
        put("agd", np.stack([at["A_diag"], at["G_diag"], at["dt"]], 1), r)
        put("eye2", np.eye(64, dtype=f4), r)
        for t in range(3):
            put("cw3", tx["w3"][0, :, t:t + 1], r, 2 * t + b2)
        for k in range(EP):
            e = 2 * k + b2
            put("ew1", ff["expert_w1"][e], 0, P * k + r)
            put("eb1", ff["expert_b1"][e][:, None], r, k)
            put("ew2", ff["expert_w2"][e], r, P * k + r)
            put("eb2", ff["expert_b2"][e][:, None], r, k)
            put("ew3", ff["expert_w3"][e], r, P * k + r)
    put("fc1_b", tk["fc1_b"][:, None]); put("fc2", tk["fc2_w"], 0, 7)
    put("fc2_b", np.broadcast_to(tk["fc2_b"][None], (P, 1)))
    put("cb1", tx["b1"][:, None]); put("cb2", np.tile(tx["b2"][:, None], (2, 1)))
    put("cw2", tx["w2"].transpose(1, 2, 0)); 
    put("cb3", np.broadcast_to(tx["b3"][None], (P, 1)))
    put("emb", np.concatenate([tx["emb"], tx["locality_shapes"]], 1))
    put("bytepos", np.linspace(0.0, 1.0, S, dtype=f4).reshape(ST, P).T)
    put("widths", np.broadcast_to(tx["multiscale_widths"][None], (P, SCALES)))
    put("swts", np.broadcast_to(tx["scale_weights"][None], (P, SCALES)))
    put("bmat", at["Bmat"][:, :, 0].T, 0, 0); put("bmat", at["Bmat"][:, :, 1].T, 0, P)
    put("cmat", at["Cmat"][:, :, 0].T, 64, 0); put("cmat", at["Cmat"][:, :, 1].T, 64, 64)
    put("dvec", np.broadcast_to(at["D"][None], (P, D)))
    put("rw1", ff["router_w1"]); put("rb1", ff["router_b1"][:, None])
    put("rw2", ff["router_w2"]); put("rw2", ff["router_b2"][None], 32)
    put("eb3", ff["expert_b3"], 64)
    lc = np.zeros((LAYERS, P, 131), f4)
    for b2 in range(2):
        r = slice(64 * b2, 64 * b2 + 64)
        lc[:, r, r] = tk["pw_w"].transpose(0, 2, 1)
        lc[:, r, 128], lc[:, r, 129], lc[:, r, 130] = tk["pw_b"], tk["gamma"], tk["beta"]
    wre = np.concatenate([tk["w1r"], tk["w2r"]], 3)
    wim = np.concatenate([tk["w1i"], tk["w2i"]], 3)
    ws = np.stack([wre, wim], 1).transpose(0, 5, 1, 2, 4, 3).reshape(LAYERS * KY, P, 4, 2, 4, C)
    ws = ws.transpose(0, 3, 1, 4, 2, 5).reshape(LAYERS * KY * 2, P, WC)
    xs = a["x"].reshape(BP, 2, PX, 3).transpose(0, 1, 3, 2).reshape(BP, 6, PX)
    arrays = {"xs": xs, "toks": a["x_txt"], "pos": a["fside_BS_continuous_positions"],
              "cmain": csts["main"], "ctext": csts["text"], "ctail": csts["tail"], "lconst": lc, "wspec": ws}
    arrays = {k: np.ascontiguousarray(v) for k, v in arrays.items()}
    nc = bacc.Bacc("TRN2", target_bir_lowering=False, num_devices=1)
    args = [nc.dram_tensor(k, v.shape, mybir.dt.from_np(v.dtype), kind="ExternalInput").ap() for k, v in arrays.items()]
    out = nc.dram_tensor("out", (B, L, D), F32, kind="ExternalOutput").ap()
    build_program(nc, *args, out)
    r = run_bass_kernel_spmd(nc, [arrays], core_ids=[0])
    return r.results[0]["out"]
```

```python
from contextlib import ExitStack

import concourse.bass as bass
from concourse import mybir
import numpy as np

F32 = mybir.dt.float32
I32 = mybir.dt.int32
ALU = mybir.AluOpType
ACT = mybir.ActivationFunctionType
AX_X = mybir.AxisListType.X

P = 128
B, BP = 8, 4
X = Y = 64
C = D = 64
LAYERS = 4
KX, KY = 32, 16
PX = X * Y
NPAIR = X // 2
S = 512
ST = S // P
SCALES = 4
L = X + S
TILES = B * L // P
TT = B * ST
T = 16
CH = S // T
E, EP = 6, 3
EPS = 1e-5
TWO_PI_IN = 2 * np.pi * (1 - 2.0 ** -21)
NS = 8
NW = 8
WC = KX * C // 2


TILES_OF_CONSTANTS = {
    "main": [("ident", 128), ("dft_y", 64), ("dft_x", 128), ("idft_x", 256), ("idft_y", 256)],
    "text": [("cw1", 512), ("cb1", 1), ("cw2", 320), ("cb2", 1), ("cw3", 6), ("cb3", 1), ("emb", 68),
             ("vocab", 1), ("bytepos", ST), ("widths", SCALES), ("swts", SCALES), ("fc0", 128), ("fc0_b", 1),
             ("agd", 3)],
    "tail": [("fc1", 256), ("fc1_b", 1), ("fc2", 15), ("fc2_b", 1), ("eye2", 64), ("bmat", 256), ("cmat", 128),
             ("dvec", 64), ("rw1", 32), ("rb1", 1),
             ("rw2", 24), ("rb2", 6), ("ew1", 384), ("eb1", 3), ("ew2", 384), ("eb2", 3), ("ew3", 384), ("eb3", 64)],
}
AT, WIDTH = {}, {}
for _tile, _cols in TILES_OF_CONSTANTS.items():
    _n = 0
    for _name, _w in _cols:
        AT[_name] = (_tile, _n, _n + _w)
        _n += _w
    WIDTH[_tile] = _n

UNITS = 16
AT_STEP = {}
for _k, _part in enumerate("usrp"):
    for _u in range(2):
        AT_STEP["forward", 8 + 4 * _u + _k] = (_u, _part)
    for _u in range(8):
        AT_STEP["mix", 4 * _u + _k] = (2 + _u, _part)
    for _u in range(6):
        AT_STEP["out", 5 * _u + _k] = (10 + _u, _part)
AT_STEP["out", 31] = (UNITS, "p")

STEPS = KY + 2
FORWARD_X = [(2, 3), (4, 5), (6, 7), (8, 9), (10, 11), (12,), (13,), (14,), (15,)] + [()] * (STEPS - 9)
INVERSE_X = [()] * 9 + [(0, 1), (2, 3), (4, 5), (6, 7), (8, 9), (10, 11), (12, 13), (), (14, 15)]
READ_Z = [(), (0,), (1,), (2,), (3,), (), (), (), (), (4, 5), (6, 7), (8, 9), (10, 11), (12,), (13,), (14,), (15,), ()]
ODD_POWERS = [(3, 1), (5, 3), (9, 4), (13, 3)]
POWER_ROUNDS = 8 + len(ODD_POWERS)
SCAN_AT = 35
GA = 8


def build_program(nc, xs, toks, pos, cmain, ctext, ctail, lconst, wspec, out):
    nc.disable_value_cache = True
    with ExitStack() as ctx:
        def sb(name, shape, dt=F32):
            return ctx.enter_context(nc.sbuf_tensor(name, shape, dt))

        def sem(name):
            return ctx.enter_context(nc.semaphore(name))

        hbuf = sb("hbuf", [P, BP, PX])
        abuf = sb("abuf", [P, 16, B * C])
        big = sb("big", [P, NW * WC + NS * 512])
        stage = sb("stage", [P, 6 * 512])
        tok = sb("tok", [P, TILES, D])
        amps = sb("amps", [P, TT, D])
        tv = sb("tv", [P, 12, TT])
        posb = sb("posb", [P, S])
        xd = sb("xd", [P, S])
        eb = sb("eb", [P, 2, 1024])
        rb = sb("rb", [P, 2, 1024])
        kb = sb("kb", [P, 2 * S])
        basis = sb("basis", [P, S])
        ampr = sb("ampr", [P, 2, D])
        fieldt = sb("fieldt", [D, S])
        cst = sb("cst", [P, WIDTH["main"]])
        lcst = sb("lcst", [P, 131])
        stats = sb("stats", [P, 32, 6])
        bn = sb("bn", [P, 16])
        banks = [ctx.enter_context(nc.psum_tensor(f"bank{i}", [P, 512], F32)) for i in range(8)]
        zdram = nc.dram_tensor("zdram", (KY, 8, 4, 16, 64), F32).ap()

        wring = big[:, 0:NW * WC].rearrange("p (n w) -> p n w", w=WC)
        spec = big[:, NW * WC:NW * WC + NS * 512].rearrange("p (s k b) -> p s k b", s=NS, b=B)
        af = [stage[:, 512 * i:512 * (i + 1)] for i in range(4)]
        zs = [stage[:, 512 * i:512 * (i + 1)] for i in range(2)]
        z2 = [stage[:, 512 * (2 + i):512 * (3 + i)] for i in range(2)]
        z2 += [big[:, NW * WC + 512 * i:NW * WC + 512 * (i + 1)] for i in range(6)]
        NY = 4
        ys = [stage[:, 512 * i:512 * (i + 1)] for i in (4, 5, 2, 3)]
        OB = (4, 5, 6, 0, 1, 2)
        NO = len(OB)
        ab1 = abuf[:, :, :].rearrange("p a n -> p (a n)")
        hb1 = hbuf[:, :, :].rearrange("p a n -> p (a n)")
        sp1 = big[:, :]
        csts = {"main": cst, "text": ab1[:, 4608:4608 + WIDTH["text"]], "tail": ab1[:, 5632:5632 + WIDTH["tail"]]}

        def c(name, rows=slice(0, P), lo=0, n=None):
            tile, a, b = AT[name]
            return csts[tile][rows, a + lo:(b if n is None else a + lo + n)]

        xt = [big[:, NW * WC + 512 * i:NW * WC + 512 * (i + 1)] for i in range(4)]
        XB = (0, 1, 4, 5)

        const_in = sem("const_in")
        toks_in = [sem(f"toks_in{i}") for i in range(2)]; onehot = sem("onehot"); pad0 = sem("pad0")
        conv1_mm = sem("conv1_mm"); conv1_act = sem("conv1_act"); conv2_mm = sem("conv2_mm")
        conv2_act = sem("conv2_act"); ctx_mm = sem("ctx_mm"); emb_mm = sem("emb_mm"); emb_out = sem("emb_out")
        tvec = sem("tvec"); tact = sem("tact")
        tail_in = sem("tail_in"); text_in = sem("text_in")
        pos_in = sem("pos_in"); xd_ready = sem("xd_ready"); r_done = sem("r_done"); squared = sem("squared")
        exp_done = sem("exp_done"); sin_done = sem("sin_done"); product = sem("product"); e_free = sem("e_free")
        summed = sem("summed"); field_mm = sem("field_mm"); field_sb = sem("field_sb"); field_tr = sem("field_tr")
        field_out = sem("field_out"); vch = sem("vch"); dstep = sem("dstep"); pstep = sem("pstep")
        x_in = [sem(f"x_in{i}") for i in range(2)]; fc0_mm = sem("fc0_mm"); h_ready = sem("h_ready"); lc_in = sem("lc_in")
        w_in = [sem(f"w_in{i}") for i in range(NW)]
        t_mm = sem("t_mm"); xt_dve = sem("xt_dve"); xt_act = sem("xt_act"); f1_mm = sem("f1_mm")
        af_dve = sem("af_dve"); af_act = sem("af_act")
        a_in = [sem(f"a_in{i}") for i in range(4)]
        f2_mm = sem("f2_mm"); s_act = sem("s_act"); s_dve = sem("s_dve"); mix_mm = sem("mix_mm")
        zs_ready = sem("zs_ready"); z_out = [sem(f"z_out{i}") for i in range(4)]
        z_in = [sem(f"z_in{i}") for i in range(8)]
        i1_mm = sem("i1_mm"); inverse_in = sem("inverse_in")
        ys_ready = sem("ys_ready"); y_in = [sem(f"y_in{i}") for i in range(NY)]
        o_mm = sem("o_mm"); o_stats = sem("o_stats"); o_act = sem("o_act"); bn_dve = sem("bn_dve")
        bn_mm = sem("bn_mm"); bn_act = sem("bn_act")
        fc1_mm = sem("fc1_mm"); fc1_act = sem("fc1_act"); fc2_mm = sem("fc2_mm"); fc0_act = sem("fc0_act")
        bn_rs = sem("bn_rs"); ft_ready = sem("ft_ready")
        img_in = sem("img_in")
        ln_dve = sem("ln_dve"); ln_act = sem("ln_act"); tp_mm = sem("tp_mm"); tp_out = sem("tp_out")
        pw_mm = sem("pw_mm"); pw_out = sem("pw_out"); bu_mm = sem("bu_mm"); bu_out = sem("bu_out")
        st_mm = sem("st_mm"); st_out = sem("st_out"); ke_mm = sem("ke_mm"); ke_out = sem("ke_out")
        ki_mm = sem("ki_mm"); ki_out = sem("ki_out"); tpi_mm = sem("tpi_mm"); tpi_out = sem("tpi_out")
        bi_mm = sem("bi_mm"); bi_out = sem("bi_out"); skip = sem("skip"); x_zero = sem("x_zero"); pch = sem("pch")
        cy_mm = sem("cy_mm"); cy_out = sem("cy_out")
        fx_mm = sem("fx_mm"); fx_out = sem("fx_out"); ao_mm = sem("ao_mm"); ao_out = sem("ao_out")
        tp2_mm = sem("tp2_mm"); tp2_out = sem("tp2_out")
        rh_mm = sem("rh_mm"); rh_act = sem("rh_act"); lg_mm = sem("lg_mm"); gate = sem("gate")
        gate_act = sem("gate_act"); gt_mm = sem("gt_mm"); gt_out = sem("gt_out")
        gated = sem("gated"); reduced = sem("reduced"); halved = sem("halved")
        e1_mm = sem("e1_mm"); e1_act = sem("e1_act"); e2_mm = sem("e2_mm"); e2_act = sem("e2_act")
        e3_mm = sem("e3_mm"); res = sem("res")
        stored = sem("stored")

        toki = ab1[:, 0:1024].bitcast(I32)
        oh = [ab1[:, 1024 + 520 * i:1024 + 520 * (i + 1)] for i in range(2)]
        g1 = [ab1[:, 2064 + 516 * i:2064 + 516 * (i + 1)] for i in range(2)]
        g2 = [ab1[:, 3096 + 516 * i:3096 + 516 * (i + 1)] for i in range(2)]
        embt = sp1[:, 8192:8192 + TT * 68].rearrange("p (t e) -> p t e", e=68)
        xin = [sp1[0:6, PX * i:PX * (i + 1)] for i in range(2)]

        eb3, rb3 = (x[:, :, :].rearrange("p a n -> p (a n)").rearrange("p (t d) -> p t d", d=D) for x in (eb, rb))
        NH = 8
        hid = [sp1[:, 512 * i:512 * (i + 1)] for i in range(NH)]
        ft = [stage[:, 512 * i:512 * (i + 1)] for i in range(2)]
        ut = ab1[0:64, 0:B * L]
        un_t, un_i = eb3, kb[:, 0:4 * D].rearrange("p (t d) -> p t d", d=D)
        w1_t, w1_i = rb3, kb[:, 4 * D:8 * D].rearrange("p (t d) -> p t d", d=D)
        lnv = kb[:, 8 * D:8 * D + 8 * TILES].rearrange("p (k t) -> p k t", t=TILES)
        sx = sp1[:, 4096:4096 + 16 * S]
        sx4 = sx.rearrange("p (g c j) -> p g c j", c=CH, j=T)
        si = sp1[:, 0:16 * X].rearrange("p (g t) -> p g t", t=X)
        pm = amps[:, :, :].rearrange("p t d -> p (t d)").rearrange("p (k n) -> p k n", n=P)
        ph = ab1[:, 4608:4608 + 4 * P].rearrange("p (k n) -> p k n", n=P)
        qm = [x[:, P * i:P * (i + 1)] for x in (xd, posb) for i in range(4)]
        ends = stage[:, 1024:1536].rearrange("p (g c) -> p g c", c=CH)
        carry = stage[:, 1536:2048].rearrange("p (g c) -> p g c", c=CH)
        co = tv[:, 10, 8:22]

        def power(e):
            return pm[:, 2 ** e - 1, :] if e <= 4 else ph[:, e - 5, :]

        un = hb1[:, 0:TILES * D].rearrange("p (t d) -> p t d", d=D)
        sq = hb1[:, TILES * D:2 * TILES * D].rearrange("p (t d) -> p t d", d=D)
        w1 = sp1[:, 6400:6400 + TILES * D].rearrange("p (t d) -> p t d", d=D)
        h2 = sp1[:, 1024:1024 + TILES * D].rearrange("p (t d) -> p t d", d=D)
        u2t = ab1[0:64, 0:B * L]
        gtt = ab1[64:70, 0:B * L]
        wr1 = sp1[:, 8704:11204]
        lg = wr1[:, 0:216].rearrange("p (t e) -> p t e", e=E)
        pr = wr1[:, 216:432].rearrange("p (t e) -> p t e", e=E)
        gv = wr1[:, 432:432 + 216 * 6].rearrange("p (k t e) -> p k t e", k=6, e=E)
        gs = wr1[:, 1728:1728 + 12 * TILES].rearrange("p (k t) -> p k t", t=TILES)
        gates = wr1[:, 2200:2200 + TILES * (E + 1)].rearrange("p (t e) -> p t e", e=E + 1)
        rh = [stage[:, 512 * i:512 * (i + 1)] for i in range(3)]
        NM = EP * TILES // 4
        ha = hb1[:, 0:512 * NM]
        hr = [hb1[:, 512 * (NM + i):512 * (NM + i + 1)] for i in range(4)]
        prod = [x[:, :, :].rearrange("p a n -> p (a n)")[:, 0:4 * (E + 1) * D].rearrange("p (t e d) -> p t e d", t=4, d=D)
                for x in (eb, rb)]
        w1t = tok

        def bc(v, n):
            return v.unsqueeze(2).to_broadcast([P, v.shape[1], n])

        def spectrum_parts(ky):
            src = banks[4 + ky % 2][:, :].rearrange("p (b k) -> p b k", b=BP)
            for part in range(2):
                for b2 in range(2):
                    yield (spec[64 * part:64 * part + 64, ky % NS, :, b2::2].rearrange("p k b -> p b k"),
                           src[64 * b2:64 * b2 + 64, :, 64 * part:64 * part + 64])

        def spectrum_room(eng, l, ky):
            eng.wait_ge(f2_mm, 16 * l + ky + 1)
            if ky >= NS:
                eng.wait_ge(mix_mm, 32 * l + NW + 2 * (ky - NS + 1))

        def rows_done(eng, l, g):
            eng.wait_ge(xt_dve, (GA + 16) * l + (2 * g + 2 if g < GA else GA + g + 1))
            if g >= GA:
                eng.wait_ge(xt_act, (16 - GA) * l + g - GA + 1)

        def y_done(eng, l, g):
            if g < GA:
                eng.wait_ge(af_dve, GA * l + g + 1)
            else:
                eng.wait_ge(af_act, (16 - GA) * l + g - GA + 1)

        def spectrum_done(eng, l, n):
            eng.wait_ge(s_dve, 8 * l + (n + 1) // 2)
            if n > 1:
                eng.wait_ge(s_act, 8 * l + n // 2)

        block = ctx.enter_context(nc.Block())

        @block.sync
        def _(sp):
            sp.dma_start(csts["text"], ctext).then_inc(text_in, 16)
            def ids(b):
                if b >= 2:
                    sp.wait_ge(onehot, b - 1)
                sp.dma_start(toki[:, 512 * (b % 2):512 * (b % 2 + 1)], toks[b:b + 1, :].to_broadcast([P, S])
                             ).then_inc(toks_in[b % 2], 16)

            def image(bp):
                if bp >= 2:
                    sp.wait_ge(fc0_mm, 8 * (bp - 1))
                sp.dma_start(xin[bp % 2], xs[bp]).then_inc(x_in[bp % 2], 16)

            ids(0)
            ids(1)
            image(0)
            image(1)
            for b in range(2, 6):
                ids(b)
            image(2)
            ids(6)
            ids(7)
            image(3)
            sp.dma_start(cst[:, :], cmain).then_inc(const_in, 16)

            with sp.Fori(0, LAYERS) as l:
                def weights(n):
                    used = sp.snap(32 * l + n + 1)
                    if n == 0:
                        moved = sp.snap(l + 1)
                        sp.wait_ge(inverse_in, moved)
                    sp.wait_ge(mix_mm, used)
                    sp.wait_ge(const_in, 16)
                    sp.dma_start(wring[:, n % NW, :], wspec[bass.ds(2 * KY * l + n, 1)].rearrange("l p n -> (l p) n")
                                 ).then_inc(w_in[n % NW], 16)

                def positions(i):
                    sp.dma_start(posb[:, :], pos[bass.ds(2 * l + i, 1), :].to_broadcast([P, S])).then_inc(pos_in, 16)

                for n in range(NW):
                    weights(n)
                started = sp.snap(16 * l + 1)
                halfway = sp.snap(8 * l + ST)
                sp.wait_ge(h_ready, started)
                sp.wait_ge(const_in, 16)
                positions(0)
                for g in range(16):
                    y_done(sp, l, g)
                    sp.dma_start(abuf[g::16, :, :].rearrange("p a n -> p (a n)"), af[g % 4]).then_inc(a_in[g % 4], 16)

                def z_read(ky):
                    stored = sp.snap(64 * (4 * l + ky // 4 + 1))
                    sp.wait_ge(z_out[ky % 4], stored)
                    sp.wait_ge(const_in, 16)
                    sp.dma_start(z2[ky // 2][64 * (ky % 2):64 * (ky % 2) + 64, :],
                                 zdram[ky].rearrange("k q (r b) o -> (k q r) (b o)", r=2)).then_inc(z_in[ky % 8], 16)

                for step in range(STEPS):
                    if step < KY:
                        filled = sp.snap(16 * l + step + 1)
                        sp.wait_ge(zs_ready, filled)
                        for q in range(4):
                            sp.dma_start(zdram[step, :, q].rearrange("k m o -> m k o"),
                                         zs[step % 2][32 * q:32 * q + 16, :].rearrange("m (k o) -> m k o", k=8)
                                         ).then_inc(z_out[step % 4], 16)
                    for ky in READ_Z[step]:
                        z_read(ky)
                    for n in range(2 * step + NW, min(2 * step + NW + 2, 2 * KY)):
                        weights(n)
                    if step == 8:
                        sp.wait_ge(xd_ready, halfway)
                        sp.wait_ge(const_in, 16)
                        positions(1)
            sp.wait_ge(o_mm, 32 * LAYERS)
            sp.dma_start(csts["tail"], ctail).then_inc(tail_in, 16)
            for b in range(B):
                sp.wait_ge(ft_ready, b // 4 + 1)
                sp.dma_start(tok[64 * (b % 2):64 * (b % 2) + 64, TT + b // 2, :],
                             ft[b // 4][32 * (b % 4):32 * (b % 4) + 8, :]).then_inc(img_in, 16)
            for b in range(B):
                sp.wait_ge(res, b + 1)
                sp.dma_start(out[b, X:L, :].rearrange("(t p) d -> p t d", p=P),
                             w1t[:, ST * b:ST * (b + 1), :]).then_inc(stored, 16)
            sp.wait_ge(res, B + 1)
            for b in range(B):
                sp.dma_start(out[b, 0:X, :], w1t[64 * (b % 2):64 * (b % 2) + 64, TT + b // 2, :]).then_inc(stored, 16)
            sp.wait_ge(stored, 32 * B)

        @block.gpsimd
        def _(pool):
            for i in range(2):
                nc.gpsimd.memset(oh[i], 0.0)
                nc.gpsimd.memset(g1[i], 0.0)
                nc.gpsimd.memset(g2[i], 0.0).then_inc(pad0, 1)
            nc.gpsimd.memset(ampr[:, 0, :], 0.0).then_inc(e_free, 1)
            nc.gpsimd.memset(ampr[:, 1, :], 0.0).then_inc(summed, 1)
            nc.gpsimd.memset(basis[:, :], 0.0).then_inc(field_mm, 1)
            nc.gpsimd.memset(fieldt[:, :], 0.0).then_inc(inverse_in, 1)
            pool.wait_ge(tvec, 1)
            G = nc.gpsimd.tensor_tensor
            with pool.Fori(0, LAYERS) as l:
                def unit_sum(m):
                    e, t = eb[:, m % 2, :], m // 2
                    pool.wait_ge(product, 16 * l + m + 1)
                    if m % 2 == 0:
                        pool.wait_ge(field_mm, 8 * l + t + 1)
                        G(basis[:, :], e[:, 0:S], e[:, S:2 * S], ALU.add).then_inc(e_free, 1)
                        nc.gpsimd.tensor_copy(ampr[:, t % 2, :], amps[:, bass.ds(8 * l + t, 1), :].rearrange("p a d -> p (a d)")
                                              ).then_inc(pstep, 1)
                    else:
                        G(e[:, 0:S], e[:, 0:S], e[:, S:2 * S], ALU.add).then_inc(pstep, 1)
                        pool.wait_ge(pstep, 16 * l + 2 * t + 2)
                        G(basis[:, :], basis[:, :], e[:, 0:S], ALU.add).then_inc(summed, 1)

                for m in range(UNITS):
                    if m == 4:
                        pool.wait_ge(h_ready, 16 * l + 16)
                        pool.dma_start(lcst[:, :], lconst[bass.ds(l, 1)].rearrange("l p n -> (l p) n")).then_inc(lc_in, 16)
                    unit_sum(m)
            pool.wait_ge(mix_mm, 32 * LAYERS + NW)
            pool.wait_ge(i1_mm, 16 * LAYERS)
            pool.wait_ge(summed, 8 * LAYERS + 1)
            nc.gpsimd.memset(sx[64:128, :], 0.0).then_inc(x_zero, 1)
            pool.wait_ge(x_zero, 1)
            for k, (w, u, t, n) in enumerate(((w1_t, un_t, tok[:, 0:TT, :], TT), (w1_i, un_i, tok[:, TT:TILES, :], TILES - TT))):
                pool.wait_ge(ln_dve, 2 * (k + 1))
                G(w, u, c("dvec").unsqueeze(1).to_broadcast([P, n, D]), ALU.mult).then_inc(pch, 1)
                pool.wait_ge(pch, k + 1)
                G(w, w, t, ALU.add).then_inc(skip, 1)
            for n in range(9):
                pool.wait_ge(gated, 4 * (n + 1))
                G(prod[n % 2][:, :, 1:4, :], prod[n % 2][:, :, 1:4, :], prod[n % 2][:, :, 4:7, :], ALU.add).then_inc(halved, 1)

        @block.vector
        def _(dve):
            links = [0]

            def link(ins):
                links[0] += 1
                ins.then_inc(vch, 1)
                dve.wait_ge(vch, links[0])

            V = nc.vector
            dve.wait_ge(text_in, 16)
            dve.wait_ge(pad0, 2)
            def one_hots(b):
                i = b % 2
                dve.wait_ge(toks_in[i], 16 * (b // 2 + 1))
                if b >= 2:
                    dve.wait_ge(conv1_mm, b - 1)
                    dve.wait_ge(emb_mm, b - 1)
                t = toki[:, 512 * i:512 * (i + 1)]
                V.tensor_scalar(oh[i][0:64, 3:3 + S], t[0:64, :], c("vocab", slice(0, 64)), None, ALU.is_equal)
                V.tensor_scalar(oh[i][64:128, 2:2 + S], t[64:128, :], c("vocab", slice(64, 128)), None,
                                ALU.is_equal).then_inc(onehot, 1)
                if b >= 1:
                    dve.wait_ge(emb_mm, b)
                    V.tensor_copy(embt[:, ST * (b - 1):ST * b, :],
                                  banks[6][:, 0:ST * 68].rearrange("p (t e) -> p t e", e=68)).then_inc(emb_out, 1)

            one_hots(0)
            one_hots(1)
            agd = c("agd")
            o = lambda i: co[:, i:i + 1]
            dve.wait_ge(tact, 1)
            dts = o(0)
            link(V.tensor_tensor(o(1), dts, agd[:, 0:1], ALU.mult))
            link(V.tensor_tensor(o(2), agd[:, 1:2], o(1), ALU.subtract))
            link(V.tensor_scalar(o(2), o(2), 0.0, None, ALU.max))
            link(V.tensor_tensor(o(3), o(1), o(2), ALU.add))
            link(V.tensor_tensor(o(4), o(3), o(3), ALU.mult))
            link(V.tensor_scalar(o(4), o(4), 0.25, None, ALU.mult))
            link(V.tensor_tensor(o(5), agd[:, 0:1], o(4), ALU.subtract))
            link(V.tensor_scalar(o(5), o(5), 0.0, None, ALU.max))
            link(V.tensor_tensor(o(6), o(4), o(5), ALU.add))
            link(V.tensor_tensor(o(7), dts, o(3), ALU.mult))
            link(V.tensor_scalar(o(8), o(7), -1.0, 1.0, ALU.mult, ALU.add))
            link(V.tensor_tensor(o(9), dts, o(6), ALU.mult))
            link(V.tensor_scalar(o(9), o(9), -1.0, None, ALU.mult))
            link(V.memset(co[:, 10:14], 1.0))
            lo, hi = slice(0, 64), slice(64, 128)
            for col, top, bot in ((10, 8, 9), (11, 0, None), (12, 8, 0), (13, 9, None)):
                link(V.tensor_copy(co[lo, col:col + 1], co[lo, top:top + 1]))
                if bot is not None:
                    link(V.tensor_copy(co[hi, col:col + 1], co[hi, bot:bot + 1]))
            for b in range(2, B):
                one_hots(b)
            dve.wait_ge(emb_mm, B)
            V.tensor_copy(embt[:, ST * (B - 1):ST * B, :],
                          banks[6][:, 0:ST * 68].rearrange("p (t e) -> p t e", e=68)).then_inc(emb_out, 1)
            dve.wait_ge(emb_out, B)
            lp = [embt[:, :, 64 + k] for k in range(4)]
            cen, ph, absw, amp, cxs = tv[:, 0], tv[:, 1], tv[:, 2], tv[:, 3], tv[:, 4]
            rw = [tv[:, 5 + s] for s in range(SCALES)]
            sw2 = tv[:, 10, 0:SCALES]
            link(V.tensor_scalar(tv[:, 9], lp[0], 0.05, None, ALU.mult))
            link(V.tensor_tensor(cen.rearrange("p (b t) -> p b t", t=ST), tv[:, 9].rearrange("p (b t) -> p b t", t=ST),
                                 c("bytepos").unsqueeze(1).to_broadcast([P, B, ST]), ALU.add))
            link(V.tensor_scalar(ph, lp[3], 0.5, 0.25, ALU.mult, ALU.add))
            link(V.tensor_scalar(tv[:, 9], lp[1], -1.0, None, ALU.mult))
            link(V.tensor_tensor(absw, lp[1], tv[:, 9], ALU.max))
            for s in range(SCALES):
                link(V.tensor_scalar(rw[s], absw, c("widths", lo=s, n=1), EPS, ALU.mult, ALU.add))
                link(V.reciprocal(rw[s], rw[s]))
            link(V.tensor_tensor(sw2, c("swts"), c("swts"), ALU.mult))
            dve.wait_ge(tact, 3)
            link(V.tensor_tensor(amp, cxs, tv[:, 11], ALU.mult))
            link(V.tensor_tensor(amps[:, :, :], embt[:, :, 0:D], bc(amp, D), ALU.mult))
            V.tensor_copy(tv[:, 9], amp).then_inc(tvec, 1)

            CHAINED = 32

            def basis_part(l, stage_name, step, chained):
                m, part = AT_STEP.get((stage_name, step), (0, ""))
                t, e, r = m // 2, eb[:, m % 2, :], rb[:, m % 2, :]

                def chain(ins):
                    chained[0] += 1
                    ins.then_inc(dstep, 1)
                    dve.wait_ge(dstep, CHAINED * l + chained[0])

                def of_byte(v):
                    return v[:, bass.ds(8 * l + t, 1)]

                if part == "u" and m % 2 == 0:
                    if m % 8 == 0:
                        dve.wait_ge(pos_in, 32 * l + 16 * (t // ST) + 16)
                    if m:
                        dve.wait_ge(squared, 16 * l + m)
                    V.tensor_scalar(xd[:, :], posb[:, :], of_byte(cen), None, ALU.subtract).then_inc(xd_ready, 1)
                    dve.wait_ge(xd_ready, 8 * l + t + 1)
                if "u" in part:
                    if m >= 2:
                        dve.wait_ge(product, 16 * l + m - 1)
                    for k in range(2):
                        ins = V.tensor_scalar(r[:, S * k:S * (k + 1)], xd[:, :], of_byte(rw[2 * (m % 2) + k]), of_byte(ph),
                                              ALU.mult, ALU.add)
                    chain(ins)
                if "r" in part:
                    chain(V.tensor_copy(kb[:, :].bitcast(I32), r))
                    V.tensor_tensor(r, r, kb[:, :].bitcast(I32), ALU.subtract).then_inc(r_done, 1)
                if "p" in part and m:
                    e, r = eb[:, (m - 1) % 2, :], rb[:, (m - 1) % 2, :]
                    dve.wait_ge(exp_done, 16 * l + m)
                    dve.wait_ge(sin_done, 16 * l + m)
                    for k in range(2):
                        s = 2 * ((m - 1) % 2) + k
                        ins = V.scalar_tensor_tensor(out=e[:, S * k:S * (k + 1)], in0=e[:, S * k:S * (k + 1)],
                                                     scalar=sw2[:, s:s + 1], in1=r[:, S * k:S * (k + 1)],
                                                     op0=ALU.mult, op1=ALU.mult)
                    ins.then_inc(product, 1)

            with dve.Fori(0, LAYERS) as l:
                chained = [0]
                for g in range(16):
                    for xp in (2 * g, 2 * g + 1)[:2 if g < GA else 1]:
                        dve.wait_ge(t_mm, 32 * l + xp + 1)
                        if g >= 2:
                            dve.wait_ge(f1_mm, 16 * l + g - 1)
                        V.tensor_copy(xt[xp % 4], banks[XB[xp % 4]][:, :]).then_inc(xt_dve, 1)
                    if 0 < g <= GA:
                        dve.wait_ge(f1_mm, 16 * l + g)
                        if g > 4:
                            dve.wait_ge(a_in[(g - 1) % 4], 16 * (4 * l + (g - 1) // 4))
                        V.tensor_copy(af[(g - 1) % 4], banks[2 + (g - 1) % 2][:, :]).then_inc(af_dve, 1)
                    basis_part(l, "forward", g, chained)

                def spectrum(ky):
                    spectrum_room(dve, l, ky)
                    for dst, src in spectrum_parts(ky):
                        ins = V.tensor_copy(dst, src)
                    ins.then_inc(s_dve, 1)

                spectrum(0)
                for ky in range(KY):
                    for nxt in FORWARD_X[ky]:
                        if nxt % 2 == 0:
                            spectrum(nxt)
                    basis_part(l, "mix", 2 * ky, chained)
                    dve.wait_ge(mix_mm, 32 * l + NW + 2 * ky + 2)
                    if ky >= 2:
                        dve.wait_ge(z_out[(ky - 2) % 4], 64 * (4 * l + (ky - 2) // 4 + 1))
                    V.tensor_copy(zs[ky % 2], banks[ky % 2][:, :]).then_inc(zs_ready, 1)
                    basis_part(l, "mix", 2 * ky + 1, chained)
                for q in range(32):
                    dve.wait_ge(o_act, 32 * l + q + 1)
                    V.bn_stats(stats[:, q, :], hbuf[:, q % BP, 512 * (q // BP):512 * (q // BP + 1)]).then_inc(o_stats, 1)
                    basis_part(l, "out", q, chained)
                dve.wait_ge(o_stats, 32 * l + 32)
                V.memset(bn[:, 4:5], 0.0)
                V.bn_aggr(bn[:, 0:2], stats[:, :, :]).then_inc(bn_dve, 1)
                dve.wait_ge(bn_mm, l + 1)
                m, v, om, ov = bn[:, 0:1], bn[:, 1:2], banks[0][:, 0:1], banks[0][:, 1:2]
                V.tensor_tensor(bn[:, 2:4], bn[:, 0:2], banks[0][:, 0:2], ALU.add)
                V.tensor_tensor(bn[:, 4:5], m, om, ALU.subtract).then_inc(bn_dve, 1)
                dve.wait_ge(bn_dve, 6 * l + 2)
                V.tensor_scalar(bn[:, 5:6], bn[:, 4:5], bn[:, 4:5], 0.25, ALU.mult, ALU.mult)
                V.tensor_scalar(bn[:, 6:7], bn[:, 3:4], 0.5, EPS, ALU.mult, ALU.add)
                V.tensor_scalar(bn[:, 7:8], bn[:, 2:3], 0.5, None, ALU.mult).then_inc(bn_dve, 1)
                dve.wait_ge(bn_dve, 6 * l + 3)
                V.tensor_tensor(bn[:, 8:9], bn[:, 5:6], bn[:, 6:7], ALU.add).then_inc(bn_dve, 1)
                dve.wait_ge(bn_act, l + 1)
                V.reciprocal(bn[:, 10:11], bn[:, 9:10]).then_inc(bn_dve, 1)
                dve.wait_ge(bn_dve, 6 * l + 5)
                V.tensor_tensor(bn[:, 11:12], bn[:, 10:11], lcst[:, 129:130], ALU.mult).then_inc(bn_rs, 1)
                dve.wait_ge(bn_rs, 2 * l + 1)
                V.tensor_tensor(bn[:, 12:13], bn[:, 11:12], bn[:, 7:8], ALU.mult).then_inc(bn_rs, 1)
                dve.wait_ge(bn_rs, 2 * l + 2)
                V.tensor_tensor(bn[:, 13:14], lcst[:, 130:131], bn[:, 12:13], ALU.subtract).then_inc(bn_dve, 1)

                assert chained[0] == CHAINED

            dve.wait_ge(tail_in, 16)
            dve.wait_ge(field_mm, 8 * LAYERS + 1)
            dve.wait_ge(o_act, 32 * LAYERS)
            V.tensor_scalar(pm[:, 0, 0:64], c("eye2"), o(10), None, ALU.mult)
            V.tensor_scalar(pm[:, 0, 64:128], c("eye2"), o(11), None, ALU.mult)
            V.tensor_scalar(qm[0][:, 0:64], c("eye2"), o(12), None, ALU.mult)
            V.tensor_scalar(qm[0][:, 64:128], c("eye2"), o(13), None, ALU.mult).then_inc(pw_out, 1)

            def power_round(i):
                dve.wait_ge(pw_mm, i)
                if i <= 8:
                    if i < 8:
                        V.tensor_copy(qm[i], banks[7][:, P:2 * P])
                    V.tensor_copy(power(i), banks[7][:, 0:P]).then_inc(pw_out, 1)
                else:
                    k, n = ODD_POWERS[i - 9]
                    V.tensor_copy(pm[:, k - 1:k - 1 + n, :], banks[7][:, 0:P * n].rearrange("p (k n) -> p k n", n=P)
                                  ).then_inc(pw_out, 1)

            im = c("cmat", lo=64, n=64)
            link(V.tensor_scalar(im, im, -1.0, None, ALU.mult))

            def layer_norm(src, dst, tmp, tiles, k):
                v = lambda i: lnv[:, i, tiles]
                link(V.reduce_sum(v(0), src, AX_X))
                link(V.tensor_scalar(v(1), v(0), 1.0 / D, None, ALU.mult))
                link(V.tensor_tensor(dst, src, bc(v(1), D), ALU.subtract))
                link(V.tensor_tensor(tmp, dst, dst, ALU.mult))
                link(V.reduce_sum(v(2), tmp, AX_X))
                V.tensor_scalar(v(3), v(2), 1.0 / D, EPS, ALU.mult, ALU.add).then_inc(ln_dve, 1)
                dve.wait_ge(ln_act, k)
                link(V.reciprocal(v(5), v(4)))
                V.tensor_tensor(dst, dst, bc(v(5), D), ALU.mult).then_inc(ln_dve, 1)

            dve.wait_ge(field_out, B)
            layer_norm(tok[:, 0:TT, :], un_t, w1_t, slice(0, TT), 1)
            for g in range(B):
                dve.wait_ge(tp_mm, g + 1)
                V.tensor_copy(ut[:, S * g:S * (g + 1)], banks[6 + g % 2][0:64, :]).then_inc(tp_out, 1)
            for m in range(8):
                dve.wait_ge(bu_mm, m + 1)
                for h in range(2):
                    rows = slice(64 * h, 64 * h + 64)
                    ins = V.tensor_scalar(sx[0:64, S * (2 * m + h):S * (2 * m + h + 1)], banks[6 + m % 2][rows, :],
                                          co[rows, 0:1], None, ALU.mult)
                ins.then_inc(bu_out, 1)

            def image_tokens(half):
                dve.wait_ge(fc2_mm, 8 * (half + 1))
                for q in range(4):
                    r = slice(32 * q, 32 * q + 8)
                    ins = V.tensor_scalar(ft[half][r, :], banks[4 + half][r, :], c("fc2_b", r), None, ALU.add)
                ins.then_inc(ft_ready, 1)

            def step(j):
                dve.wait_ge(st_mm, j)
                V.tensor_tensor(sx4[:, :, :, j], banks[6][:, :].rearrange("p (g c) -> p g c", c=CH), sx4[:, :, :, j],
                                ALU.add).then_inc(st_out, 1)

            def span(i):
                if i == 0:
                    dve.wait_ge(st_out, T - 1)
                    V.tensor_copy(ends, sx4[:, :, :, T - 1]).then_inc(ke_out, 1)
                d = 2 ** i
                dve.wait_ge(ke_mm, i + 1)
                V.tensor_tensor(ends[:, :, d:CH], banks[7][:, 0:16 * (CH - d)].rearrange("p (g c) -> p g c", g=16),
                                ends[:, :, d:CH], ALU.add).then_inc(ke_out, 1)

            for k in range(1, T + 5):
                if k <= POWER_ROUNDS:
                    power_round(k)
                if k < T:
                    step(k)
                else:
                    span(k - T)
                if k == 8:
                    image_tokens(0)
            image_tokens(1)

            dve.wait_ge(img_in, 16 * B)
            layer_norm(tok[:, TT:TILES, :], un_i, w1_i, slice(TT, TILES), 2)
            dve.wait_ge(tpi_mm, 1)
            V.tensor_copy(ut[:, B * S:B * L], banks[0][0:64, :]).then_inc(tpi_out, 1)
            dve.wait_ge(bi_out, 2)
            for i in range(6):
                d = 2 ** i
                for ri in range(2):
                    dve.wait_ge(ki_mm, 2 * i + ri + 1)
                    V.tensor_tensor(si[:, 8 * ri:8 * ri + 8, d:X],
                                    banks[2 * (i % 2) + ri][:, 0:8 * (X - d)].rearrange("p (g t) -> p g t", g=8),
                                    si[:, 8 * ri:8 * ri + 8, d:X], ALU.add).then_inc(ki_out, 1)
            dve.wait_ge(ki_out, 12)
            V.tensor_copy(carry[:, :, 0], si[:, :, X - 1]).then_inc(cy_out, 1)
            for i in range(5):
                d = 2 ** i
                dve.wait_ge(cy_mm, i + 1)
                V.tensor_copy(carry[:, :, d:2 * d], banks[4 + i % 2][:, 0:16 * d].rearrange("p (g c) -> p g c", g=16)
                              ).then_inc(cy_out, 1)
            dve.wait_ge(cy_out, 6)
            V.tensor_tensor(carry[:, :, 1:CH], carry[:, :, 1:CH], ends[:, :, 0:CH - 1], ALU.add).then_inc(cy_out, 1)
            for j in range(T):
                dve.wait_ge(fx_mm, j + 1)
                V.tensor_tensor(sx4[:, :, :, j], banks[j % 4][:, :].rearrange("p (g c) -> p g c", g=16),
                                sx4[:, :, :, j], ALU.add).then_inc(fx_out, 1)
            dve.wait_ge(skip, 2)
            for g in range(5):
                w = w1_t[:, 8 * g:8 * g + 8, :] if g < 4 else w1_i
                n = 8 if g < 4 else 4
                dve.wait_ge(ao_mm, g + 1)
                V.tensor_tensor(h2[:, 8 * g:8 * g + n, :], banks[g][:, 0:64 * n].rearrange("p (t d) -> p t d", d=D),
                                w, ALU.add).then_inc(ao_out, 1)
                if g == 1:
                    dve.wait_ge(ao_out, 2)
                    layer_norm(h2[:, 0:16, :], un[:, 0:16, :], sq[:, 0:16, :], slice(0, 16), 3)
            dve.wait_ge(ao_out, 5)
            layer_norm(h2[:, 16:TILES, :], un[:, 16:TILES, :], sq[:, 16:TILES, :], slice(16, TILES), 4)
            dve.wait_ge(lg_mm, 3)
            for g in range(3):
                q = 4 if g < 2 else 1
                ins = V.tensor_tensor(lg[:, 16 * g:16 * g + 4 * q, :].rearrange("p (q k) e -> p q k e", q=q),
                                      banks[4][:, 96 * g:96 * g + 24 * q].rearrange("p (k q e) -> p q k e", k=4, e=E),
                                      c("rb2").unsqueeze(1).unsqueeze(1).to_broadcast([P, q, 4, E]), ALU.add)
            link(ins)
            mx, sm, rs, p1, p2, seen = (gs[:, k] for k in range(6))
            link(V.tensor_reduce(mx, lg, axis=AX_X, op=ALU.max))
            V.tensor_tensor(lg, lg, bc(mx, E), ALU.subtract).then_inc(gate, 1)
            dve.wait_ge(gate_act, 1)
            link(V.reduce_sum(sm, pr, AX_X))
            link(V.reciprocal(rs, sm))
            link(V.tensor_tensor(pr, pr, bc(rs, E), ALU.mult))
            cur = pr
            for rank in range(2):
                top = (p1, p2)[rank]
                eq, sel, nxt = gv[:, 3 * rank], gv[:, 3 * rank + 1], gv[:, 3 * rank + 2]
                link(V.tensor_reduce(top, cur, axis=AX_X, op=ALU.max))
                link(V.tensor_tensor(eq, cur, bc(top, E), ALU.is_equal))
                link(V.memset(seen, 0.0))
                for e in range(E):
                    link(V.tensor_tensor(sel[:, :, e], eq[:, :, e], seen, ALU.is_gt))
                    if e < E - 1:
                        link(V.tensor_tensor(seen, seen, eq[:, :, e], ALU.max))
                if rank == 0:
                    link(V.scalar_tensor_tensor(out=nxt, in0=sel, scalar=-4.0, in1=cur, op0=ALU.mult, op1=ALU.add))
                    cur = nxt
            V.tensor_tensor(gs[:, 6], p2, p1, ALU.subtract).then_inc(gate, 1)
            dve.wait_ge(gate_act, 2)
            link(V.tensor_scalar(gs[:, 8], gs[:, 7], 1.0, None, ALU.add))
            link(V.reciprocal(gs[:, 9], gs[:, 8]))
            link(V.tensor_tensor(gs[:, 10], gs[:, 7], gs[:, 9], ALU.mult))
            link(V.tensor_tensor(gv[:, 0], gv[:, 1], bc(gs[:, 9], E), ALU.mult))
            link(V.tensor_tensor(gv[:, 3], gv[:, 4], bc(gs[:, 10], E), ALU.mult))
            V.memset(gates[:, :, 0], 1.0)
            V.tensor_tensor(gates[:, :, 1:E + 1], gv[:, 0], gv[:, 3], ALU.add).then_inc(gate, 1)
            dve.wait_ge(gate, 3)
            for g in range(9):
                dve.wait_ge(gt_mm, g + 1)
                V.tensor_copy(gtt[:, 512 * g:512 * (g + 1)], banks[7 - g % 2][0:E, :]).then_inc(gt_out, 1)
            for n in range(10):
                if n < 9:
                    for t in range(4):
                        i = 4 * n + t
                        dve.wait_ge(e3_mm, i + 1)
                        if n >= 2 and t == 0:
                            dve.wait_ge(res, n - 1)
                        V.tensor_tensor(prod[n % 2][:, t], banks[4 + t][:, 0:(E + 1) * D].rearrange("p (e d) -> p e d", d=D),
                                        gates[:, i, :].unsqueeze(2).to_broadcast([P, E + 1, D]), ALU.mult).then_inc(gated, 1)
                if n:
                    w = w1[:, 4 * n - 4:4 * n, :]
                    dve.wait_ge(halved, n)
                    V.tensor_reduce(w, prod[(n - 1) % 2][:, :, 0:4, :].rearrange("p t e d -> p t d e"), axis=AX_X, op=ALU.add
                                    ).then_inc(reduced, 1)
                    dve.wait_ge(reduced, n)
                    V.tensor_tensor(w1t[:, 4 * n - 4:4 * n, :], w, h2[:, 4 * n - 4:4 * n, :], ALU.add).then_inc(res, 1)

        @block.scalar
        def _(act):
            A = nc.scalar.activation
            act.wait_ge(text_in, 16)
            A(tv[:, 10, 8:9], c("agd", lo=2, n=1), ACT.Sigmoid).then_inc(tact, 1)
            act.wait_ge(pad0, 2)

            def lift(n):
                xg, bp = n % 8, n // 8
                act.wait_ge(fc0_mm, n + 1)
                A(hbuf[:, bp, 512 * xg:512 * (xg + 1)], banks[4 + n % 2][:, :], ACT.Identity,
                  bias=c("fc0_b")).then_inc(fc0_act, 1)

            for q in range(BP):
                for i in range(2):
                    act.wait_ge(conv1_mm, 2 * q + i + 1)
                    if q:
                        act.wait_ge(conv2_mm, q)
                    A(g1[i][:, 2:2 + S], banks[i][:, :], ACT.Gelu, bias=c("cb1")).then_inc(conv1_act, 1)
                for n in range(8 * q, 8 * q + 4):
                    lift(n)
                act.wait_ge(conv2_mm, q + 1)
                if q >= 2:
                    act.wait_ge(ctx_mm, q - 1)
                A(g2[q % 2][:, 1:1 + S], banks[2 + q % 2][:, :], ACT.Gelu, bias=c("cb2")).then_inc(conv2_act, 1)
                for n in range(8 * q + 4, 8 * q + 8):
                    lift(n)
            act.wait_ge(ctx_mm, BP)
            act.wait_ge(emb_out, B)
            A(tv[:, 4].rearrange("p (q i s) -> p q i s", q=BP, i=2),
              banks[7][:, 0:TT].rearrange("p (q s i) -> p q i s", q=BP, i=2), ACT.Sigmoid, bias=c("cb3")).then_inc(tact, 1)
            A(tv[:, 11], embt[:, :, 66], ACT.Sigmoid).then_inc(tact, 1)
            act.wait_ge(fc0_act, 32)
            nc.scalar.copy(bn[:, 14:15], c("fc0_b")).then_inc(h_ready, 16)
            nc.scalar.copy(bn[:, 15:16], c("fc0_b")).then_inc(mix_mm, NW)

            def basis_part(l, stage_name, step):
                m, part = AT_STEP.get((stage_name, step), (0, ""))
                if part == "s":
                    if m % 2 == 0:
                        act.wait_ge(xd_ready, 8 * l + m // 2 + 1)
                        act.wait_ge(e_free, 8 * l + m // 2 + 1)
                    else:
                        act.wait_ge(summed, 8 * l + m // 2 + 1)
                    for k in range(2):
                        ins = A(eb[:, m % 2, S * k:S * (k + 1)], xd[:, :], ACT.Square,
                                scale=tv[:, 5 + 2 * (m % 2) + k, bass.ds(8 * l + m // 2, 1)])
                    ins.then_inc(squared, 1)
                if part == "p" and m < UNITS:
                    for f in (("exp", "sin"), ("sin", "exp"))[m % 2]:
                        if f == "exp":
                            act.wait_ge(squared, 16 * l + m + 1)
                            A(eb[:, m % 2, :], eb[:, m % 2, :], ACT.Exp, scale=-0.5).then_inc(exp_done, 1)
                        else:
                            act.wait_ge(r_done, 16 * l + m + 1)
                            A(rb[:, m % 2, :], rb[:, m % 2, :], ACT.Sin, scale=TWO_PI_IN).then_inc(sin_done, 1)

            def field_down(l, i):
                act.wait_ge(field_mm, 8 * l + 4 * i + 5)
                A(fieldt[:, :], banks[7][0:64, :], ACT.Copy).then_inc(field_sb, 1)

            def field_tokens(l, i):
                act.wait_ge(field_tr, 2 * l + i + 1)
                A(tok[:, bass.ds(8 * l + 4 * i, ST), :], banks[7][:, 0:ST * D].rearrange("p (t d) -> p t d", d=D),
                  ACT.Copy).then_inc(field_out, 1)

            def image_layer(l):
                for g in range(GA, 17):
                    if g < 16:
                        act.wait_ge(t_mm, 32 * l + 2 * g + 2)
                        act.wait_ge(f1_mm, 16 * l + g - 1)
                        A(xt[(2 * g + 1) % 4], banks[XB[(2 * g + 1) % 4]][:, :], ACT.Copy).then_inc(xt_act, 1)
                    if g > GA:
                        act.wait_ge(f1_mm, 16 * l + g)
                        act.wait_ge(a_in[(g - 1) % 4], 16 * (4 * l + (g - 1) // 4))
                        A(af[(g - 1) % 4], banks[2 + (g - 1) % 2][:, :], ACT.Copy).then_inc(af_act, 1)
                        basis_part(l, "forward", g - 1)

                def spectrum(ky):
                    spectrum_room(act, l, ky)
                    for dst, src in spectrum_parts(ky):
                        ins = A(dst, src, ACT.Copy)
                    ins.then_inc(s_act, 1)

                def y_move(ky):
                    act.wait_ge(ys_ready, 16 * l + ky + 1)
                    act.dma_start(abuf[ky::16, :, :].rearrange("p a n -> p (a n)"), ys[ky % NY]).then_inc(y_in[ky % NY], 16)

                spectrum(1)
                for step in range(STEPS):
                    for nxt in FORWARD_X[step]:
                        if nxt % 2 == 1:
                            spectrum(nxt)
                    basis_part(l, "mix", 2 * step - 1)
                    for ky in INVERSE_X[step]:
                        act.wait_ge(i1_mm, 16 * l + ky + 1)
                        if ky >= NY:
                            act.wait_ge(y_in[ky % NY], 16 * (KY // NY * l + ky // NY))
                        A(ys[ky % NY], banks[2 + ky % 2][:, :], ACT.Copy).then_inc(ys_ready, 1)
                        if ky:
                            y_move(ky - 1)
                y_move(KY - 1)
                act.wait_ge(lc_in, 16 * (l + 1))
                for q in range(32):
                    xg, bp = q // BP, q % BP
                    act.wait_ge(o_mm, 32 * l + q + 1)
                    A(hbuf[:, bp, 512 * xg:512 * (xg + 1)], banks[OB[q % NO]][:, :], ACT.Identity,
                      bias=lcst[:, 128:129]).then_inc(o_act, 1)
                    basis_part(l, "out", q)
                    if q == 2:
                        field_down(l, 0)
                    if q == 6:
                        field_tokens(l, 0)
                act.wait_ge(o_act, 32 * l + 32)
                A(bn[:, 14:15], c("ident", n=1), ACT.Sqrt)
                act.wait_ge(bn_dve, 6 * l + 4)
                A(bn[:, 9:10], bn[:, 8:9], ACT.Sqrt).then_inc(bn_act, 1)
                A(bn[:, 15:16], c("ident", n=1), ACT.Gelu)
                field_down(l, 1)
                act.wait_ge(bn_dve, 6 * l + 6)

            def activate(g):
                px = hbuf[:, :, 256 * g:256 * (g + 1)]
                A(px, px, ACT.Gelu, scale=bn[:, 11:12], bias=bn[:, 13:14]).then_inc(h_ready, 1)

            with act.Fori(0, LAYERS - 1) as l:
                image_layer(l)
                for g in range(16):
                    activate(g)
                    if g == 2:
                        field_tokens(l, 1)
            image_layer(LAYERS - 1)
            AHEAD = 4
            for g in range(AHEAD):
                activate(g)
            act.wait_ge(tail_in, 16)
            for n in range(64):
                act.wait_ge(fc1_mm, n + 1)
                if n >= NH and n % 4 == 0:
                    act.wait_ge(fc2_mm, (n - NH) // 4 + 1)
                A(hid[n % NH], banks[n % 4][:, :], ACT.Gelu, bias=c("fc1_b")).then_inc(fc1_act, 1)
                if n == 1:
                    field_tokens(LAYERS - 1, 1)
                if n % 2 == 1 and n // 2 + AHEAD < 16:
                    activate(n // 2 + AHEAD)
                if n == 15:
                    act.wait_ge(ln_dve, 1)
                    A(lnv[:, 4, 0:TT], lnv[:, 3, 0:TT], ACT.Sqrt).then_inc(ln_act, 1)
            act.wait_ge(fc1_act, 64)
            A(bn[:, 14:15], c("ident", n=1), ACT.Sqrt)
            act.wait_ge(ln_dve, 3)
            A(lnv[:, 4, TT:TILES], lnv[:, 3, TT:TILES], ACT.Sqrt).then_inc(ln_act, 1)
            for ri in range(2):
                act.wait_ge(bi_mm, ri + 1)
                A(si[:, 8 * ri:8 * ri + 8, :], banks[2 + ri][:, :].rearrange("p (g t) -> p g t", t=X), ACT.Copy,
                  scale=co[:, 0:1]).then_inc(bi_out, 1)
            act.wait_ge(ln_dve, 5)
            A(lnv[:, 4, 0:16], lnv[:, 3, 0:16], ACT.Sqrt).then_inc(ln_act, 1)
            act.wait_ge(ln_dve, 7)
            A(lnv[:, 4, 16:TILES], lnv[:, 3, 16:TILES], ACT.Sqrt).then_inc(ln_act, 1)
            for g in range(9):
                act.wait_ge(tp2_mm, g + 1)
                A(u2t[:, 512 * g:512 * (g + 1)], banks[5 + g % 3][0:64, :], ACT.Copy).then_inc(tp2_out, 1)
            for g in range(3):
                rows = slice(0, P if g < 2 else 32)
                act.wait_ge(rh_mm, g + 1)
                A(rh[g][rows, :], banks[g][rows, :], ACT.Relu, bias=c("rb1", rows)).then_inc(rh_act, 1)
            for m in range(NM + 1):
                if m < NM:
                    act.wait_ge(e1_mm, m + 1)
                    if m >= 4:
                        act.wait_ge(e2_mm, m - 3)
                    A(hr[m % 4], banks[m % 2][:, :], ACT.Relu, bias=c("eb1", lo=m % EP, n=1)).then_inc(e1_act, 1)
                if m:
                    act.wait_ge(e2_mm, m)
                    A(ha[:, 512 * (m - 1):512 * m], banks[2 + (m - 1) % 2][:, :], ACT.Relu,
                      bias=c("eb2", lo=(m - 1) % EP, n=1)).then_inc(e2_act, 1)
                if m == 1:
                    act.wait_ge(gate, 1)
                    A(pr, lg, ACT.Exp).then_inc(gate_act, 1)
                if m == 9:
                    act.wait_ge(gate, 2)
                    A(gs[:, 7], gs[:, 6], ACT.Exp).then_inc(gate_act, 1)

        @block.tensor
        def _(pe):
            mm, tr = nc.tensor.matmul, nc.tensor.transpose
            pe.wait_ge(text_in, 16)
            def lift(n):
                xg, bp = n % 8, n // 8
                if xg == 0:
                    pe.wait_ge(x_in[bp % 2], 16 * (bp // 2 + 1))
                if n >= 2:
                    pe.wait_ge(fc0_act, n - 1)
                mm(banks[4 + n % 2][:, :], c("fc0", slice(0, 6)), xin[bp % 2][:, 512 * xg:512 * (xg + 1)],
                   start=True, stop=True).then_inc(fc0_mm, 1)

            for q in range(BP):
                for i in range(2):
                    b = 2 * q + i
                    pe.wait_ge(onehot, b + 1)
                    if q:
                        pe.wait_ge(conv1_act, b - 1)
                    for t in range(4):
                        ins = mm(banks[i][:, :], c("cw1", lo=128 * t, n=128), oh[i][:, 2 * t:2 * t + S],
                                 start=(t == 0), stop=(t == 3))
                    ins.then_inc(conv1_mm, 1)
                    if b >= 1:
                        pe.wait_ge(emb_out, b)
                    for st in range(ST):
                        ins = mm(banks[6][:, 68 * st:68 * (st + 1)], oh[i][0:64, 3 + P * st:3 + P * (st + 1)],
                                 c("emb", slice(0, 64)), start=True, stop=True)
                    ins.then_inc(emb_mm, 1)
                for n in range(8 * q, 8 * q + 4):
                    lift(n)
                pe.wait_ge(conv1_act, 2 * q + 2)
                if q >= 2:
                    pe.wait_ge(conv2_act, q - 1)
                for t in range(5):
                    for i in range(2):
                        ins = mm(banks[2 + q % 2][64 * i:64 * i + 64, :], c("cw2", lo=64 * t, n=64), g1[i][:, t:t + S],
                                 start=(t == 0), stop=(t == 4))
                ins.then_inc(conv2_mm, 1)
                for n in range(8 * q + 4, 8 * q + 8):
                    lift(n)
                pe.wait_ge(conv2_act, q + 1)
                for st in range(ST):
                    at = 2 * (ST * q + st)
                    for t in range(3):
                        ins = mm(banks[7][:, at:at + 2], g2[q % 2][:, P * st + t:P * st + t + P], c("cw3", lo=2 * t, n=2),
                                 start=(t == 0), stop=(t == 2))
                ins.then_inc(ctx_mm, 1)
            pe.wait_ge(const_in, 16)

            def field(l, t):
                pe.wait_ge(summed, 8 * l + t + 2)
                if t == ST:
                    pe.wait_ge(field_out, 2 * l + 1)
                mm(banks[7][0:D, :], ampr[:, t % 2, :], basis[:, :], start=(t % ST == 0), stop=(t % ST == ST - 1)
                   ).then_inc(field_mm, 1)

            def field_transpose(l, i):
                pe.wait_ge(field_sb, 2 * l + i + 1)
                for pt in range(ST):
                    ins = mm(banks[7][:, D * pt:D * (pt + 1)], fieldt[:, P * pt:P * (pt + 1)], c("ident", slice(0, D), n=D),
                             start=True, stop=True)
                ins.then_inc(field_tr, 1)

            def basis_part(l, stage_name, step):
                m, part = AT_STEP.get((stage_name, step), (0, ""))
                if "p" in part and m < UNITS and m % 2 and m >= 3:
                    field(l, (m - 3) // 2)

            with pe.Fori(0, LAYERS) as l:
                def to_rows(xp):
                    if xp % 2 == 0:
                        pe.wait_ge(h_ready, 16 * l + xp // 2 + 1)
                    if xp >= 4 and xp % 2 == 0:
                        rows_done(pe, l, xp // 2 - 2)
                    for bp in range(BP):
                        ins = tr(banks[XB[xp % 4]][:, P * bp:P * (bp + 1)], hbuf[:, bp, P * xp:P * (xp + 1)], c("ident"))
                    ins.then_inc(t_mm, 1)

                to_rows(0)
                to_rows(1)
                for g in range(NPAIR // 2):
                    if g < NPAIR // 2 - 1:
                        to_rows(2 * g + 2)
                        to_rows(2 * g + 3)
                    rows_done(pe, l, g)
                    if g >= 2:
                        y_done(pe, l, g - 2)
                    for half in range(2):
                        ins = mm(banks[2 + g % 2][64 * half:64 * half + 64, :], c("dft_y"), xt[(2 * g + half) % 4],
                                 start=True, stop=True)
                    ins.then_inc(f1_mm, 1)
                    basis_part(l, "forward", g)
                for i in range(4):
                    pe.wait_ge(a_in[i], 64 * (l + 1))
                def forward_x(ky):
                    if ky >= 2:
                        spectrum_done(pe, l, ky - 1)
                    for bp in range(BP):
                        ins = mm(banks[4 + ky % 2][:, P * bp:P * (bp + 1)], abuf[:, ky, P * bp:P * (bp + 1)],
                                 c("dft_x"), start=True, stop=True)
                    ins.then_inc(f2_mm, 1)

                def inverse_x(pair):
                    for ky in pair:
                        pe.wait_ge(z_in[ky % 8], 16 * (2 * l + ky // 8 + 1))
                    for ky in pair:
                        if ky >= 2:
                            pe.wait_ge(ys_ready, 16 * l + ky - 1)
                        mm(banks[2 + ky % 2][:, :], c("idft_x", lo=P * (ky % 2), n=P), z2[ky // 2],
                           start=True, stop=True).then_inc(i1_mm, 1)

                def pointwise(q):
                    xg, bp = q // BP, q % BP
                    mm(banks[OB[q % NO]][:, :], lcst[:, 0:P], hbuf[:, bp, 512 * xg:512 * (xg + 1)], start=True, stop=False)

                forward_x(0)
                forward_x(1)
                for ky in range(STEPS):
                    for nxt in FORWARD_X[ky]:
                        forward_x(nxt)
                    if ky < KY:
                        spectrum_done(pe, l, ky + 1)
                        if ky >= 2:
                            pe.wait_ge(zs_ready, 16 * l + ky - 1)
                        for half in range(2):
                            n = 2 * ky + half
                            pe.wait_ge(w_in[n % NW], 16 * (2 * KY // NW * l + n // NW + 1))
                            for k in range(4 * half, 4 * half + 4):
                                for q in range(4):
                                    kx = 8 * q + k
                                    ins = mm(banks[ky % 2][32 * q:32 * q + 16, 64 * k:64 * (k + 1)],
                                             spec[:, ky % NS, 2 * kx:2 * kx + 2, :].rearrange("p r b -> p (r b)"),
                                             wring[:, n % NW, C * (4 * (k % 4) + q):C * (4 * (k % 4) + q + 1)],
                                             start=True, stop=True)
                            ins.then_inc(mix_mm, 1)
                        basis_part(l, "mix", 2 * ky + 1)
                    if ky >= KY:
                        if ky == KY:
                            pe.wait_ge(lc_in, 16 * (l + 1))
                            pe.wait_ge(zs_ready, 16 * (l + 1))
                        for q in range(2 * (ky - KY), 2 * (ky - KY) + 2):
                            pointwise(q)
                    if INVERSE_X[ky]:
                        inverse_x(INVERSE_X[ky])
                for i in range(NY):
                    pe.wait_ge(y_in[i], 16 * KY // NY * (l + 1))
                for q in range(32):
                    xg, bp = q // BP, q % BP
                    if q >= 4:
                        if q >= NO:
                            pe.wait_ge(o_act, 32 * l + q - NO + 1)
                        pointwise(q)
                    for h in range(2):
                        ins = mm(banks[OB[q % NO]][:, 256 * h:256 * (h + 1)], abuf[:, 2 * xg + h, P * bp:P * (bp + 1)],
                                 c("idft_y"), start=False, stop=(h == 1))
                        if q == 0 and h == 0:
                            ins.then_inc(inverse_in, 1)
                    ins.then_inc(o_mm, 1)
                    basis_part(l, "out", q)
                    if q == 4:
                        field_transpose(l, 0)
                pe.wait_ge(bn_dve, 6 * l + 1)
                for half in (0, 64):
                    ins = mm(banks[0][half:half + 64, 0:2], c("ident", lo=64 - half, n=64), bn[:, 0:2], start=True, stop=True)
                ins.then_inc(bn_mm, 1)
                field(l, 2 * ST - 1)
                field_transpose(l, 1)

            def power_round(i):
                if i == 1:
                    pe.wait_ge(bu_out, 8)
                pe.wait_ge(pw_out, i)
                if i <= 8:
                    ins = mm(banks[7][:, 0:P], qm[i - 1], power(i - 1), start=True, stop=True)
                    if i < 8:
                        ins = mm(banks[7][:, P:2 * P], power(i - 1), qm[i - 1], start=True, stop=True)
                else:
                    k, n = ODD_POWERS[i - 9]
                    e = k.bit_length() - 1
                    lo = k - 2 ** e
                    ins = mm(banks[7][:, 0:P * n], qm[e], pm[:, lo - 1:lo - 1 + n, :].rearrange("p k n -> p (k n)"),
                             start=True, stop=True)
                ins.then_inc(pw_mm, 1)

            def text_part(n):
                if n in range(18, 26):
                    g = n - 18
                    if g == 0:
                        pe.wait_ge(ln_dve, 2)
                    elif g >= 2:
                        pe.wait_ge(tp_out, g - 1)
                    for k in range(4):
                        ins = tr(banks[6 + g % 2][0:64, P * k:P * (k + 1)], un_t[:, 4 * g + k, :], c("ident"))
                    ins.then_inc(tp_mm, 1)
                if n in range(26, 34):
                    m = n - 26
                    if m == 0:
                        pe.wait_ge(tp_out, B)
                    elif m >= 2:
                        pe.wait_ge(bu_out, m - 1)
                    for h in range(2):
                        b = 2 * m % B + h
                        ins = mm(banks[6 + m % 2][64 * h:64 * h + 64, :], c("bmat", slice(0, 64), lo=P * (2 * m // B), n=64),
                                 ut[:, S * b:S * (b + 1)], start=True, stop=True)
                    ins.then_inc(bu_mm, 1)
                if n >= SCAN_AT:
                    i = n - SCAN_AT + 1
                    if i <= POWER_ROUNDS:
                        power_round(i)
                    if i < T:
                        if i == 1:
                            pe.wait_ge(bu_out, 8)
                            pe.wait_ge(x_zero, 1)
                        else:
                            pe.wait_ge(st_out, i - 1)
                        mm(banks[6][:, :], power(0), sx4[:, :, :, i - 1], start=True, stop=True).then_inc(st_mm, 1)
                    elif i < T + 5:
                        k = i - T
                        pe.wait_ge(ke_out, k + 1)
                        mm(banks[7][:, 0:16 * (CH - 2 ** k)], power(4 + k), ends[:, :, 0:CH - 2 ** k],
                           start=True, stop=True).then_inc(ke_mm, 1)

            pe.wait_ge(tail_in, 16)
            def head2(k):
                half, xg = k // 8, k % 8
                pe.wait_ge(fc1_act, 4 * k + 4)
                for q in range(4):
                    ins = mm(banks[4 + half][32 * q:32 * q + 8, :], c("fc2", lo=7 - xg, n=8), hid[(4 * k + q) % NH],
                             start=(xg == 0), stop=(xg == 7))
                ins.then_inc(fc2_mm, 1)

            for n in range(64):
                k, q = n // 4, n % 4
                b, xg = 4 * (k // 8) + q, k % 8
                if n >= 4:
                    pe.wait_ge(fc1_act, n - 3)
                if n % 4 == 0 and n < 32:
                    pe.wait_ge(h_ready, 16 * LAYERS + 2 * xg + 2)
                mm(banks[n % 4][:, :], c("fc1", lo=P * (b % 2), n=P), hbuf[:, b // 2, 512 * xg:512 * (xg + 1)],
                   start=True, stop=True).then_inc(fc1_mm, 1)
                if n >= 4 and q == 1:
                    head2(k - 1)
                text_part(n)
            head2(15)
            pe.wait_ge(ln_dve, 4)
            for k in range(4):
                ins = tr(banks[0][0:64, P * k:P * (k + 1)], un_i[:, k, :], c("ident"))
            ins.then_inc(tpi_mm, 1)
            pe.wait_ge(tpi_out, 1)
            for ri in range(2):
                mm(banks[2 + ri][:, :], c("bmat", slice(0, 64), lo=P * ri, n=P), ut[:, B * S:B * L],
                   start=True, stop=True).then_inc(bi_mm, 1)
            pe.wait_ge(bi_out, 2)
            for i in range(6):
                d = 2 ** i
                for ri in range(2):
                    if i:
                        pe.wait_ge(ki_out, 2 * i - 1 + ri)
                    mm(banks[2 * (i % 2) + ri][:, 0:8 * (X - d)], power(i), si[:, 8 * ri:8 * ri + 8, 0:X - d],
                       start=True, stop=True).then_inc(ki_mm, 1)
            for i in range(5):
                pe.wait_ge(cy_out, i + 1)
                mm(banks[4 + i % 2][:, 0:16 * 2 ** i], power(4 + i), carry[:, :, 0:2 ** i], start=True, stop=True
                   ).then_inc(cy_mm, 1)
            pe.wait_ge(cy_out, 7)
            for j in range(T):
                if j >= 4:
                    pe.wait_ge(fx_out, j - 3)
                mm(banks[j % 4][:, :], pm[:, j, :], carry, start=True, stop=True).then_inc(fx_mm, 1)
            pe.wait_ge(fx_out, T)
            for i in range(TILES):
                if i < TT:
                    t0 = P * (i % ST)
                    parts = [(slice(0, P), [sx[:, S * (B * ri + i // ST) + t0:S * (B * ri + i // ST) + t0 + P] for ri in range(2)])]
                else:
                    parts = [(slice(64 * b2, 64 * b2 + 64), [si[:, B * ri + 2 * (i - TT) + b2, :] for ri in range(2)])
                             for b2 in range(2)]
                for rows, x in parts:
                    for ri in range(2):
                        ins = mm(banks[i // 8][rows, 64 * (i % 8):64 * (i % 8 + 1)], x[ri], c("cmat", lo=64 * ri, n=64),
                                 start=(ri == 0), stop=(ri == 1))
                if i % 8 == 7 or i == TILES - 1:
                    ins.then_inc(ao_mm, 1)
            for g in range(9):
                if g in (0, 4):
                    pe.wait_ge(ln_dve, 6 if g == 0 else 8)
                if g >= 3:
                    pe.wait_ge(tp2_out, g - 2)
                for k in range(4):
                    ins = tr(banks[5 + g % 3][0:64, P * k:P * (k + 1)], un[:, 4 * g + k, :], c("ident"))
                ins.then_inc(tp2_mm, 1)
            pe.wait_ge(tp2_out, 9)

            def cols(n):
                return u2t[:, 512 * n:512 * (n + 1)]

            for g in range(3):
                for q in range(4 if g < 2 else 1):
                    ins = mm(banks[g][32 * q:32 * q + 32, :], c("rw1", slice(0, 64)), cols(4 * g + q), start=True, stop=True)
                ins.then_inc(rh_mm, 1)
            for g in range(3):
                rows, w = slice(0, P if g < 2 else 32), 24 if g < 2 else E
                pe.wait_ge(rh_act, g + 1)
                for k in range(4):
                    ins = mm(banks[4][:, 96 * g + w * k:96 * g + w * (k + 1)], rh[g][rows, P * k:P * (k + 1)],
                             c("rw2", rows, n=w), start=True, stop=True)
                ins.then_inc(lg_mm, 1)

            def gates_to_rows():
                pe.wait_ge(gate, 3)
                for g in range(9):
                    if g >= 2:
                        pe.wait_ge(gt_out, g - 1)
                    for k in range(4):
                        ins = tr(banks[7 - g % 2][0:E, P * k:P * (k + 1)], gates[:, 4 * g + k, 1:E + 1], c("ident"))
                    ins.then_inc(gt_mm, 1)
                pe.wait_ge(gt_out, 9)

            def outputs(n):
                for t in range(4):
                    if n:
                        pe.wait_ge(gated, 4 * (n - 1) + t + 1)
                    for k in range(EP):
                        m = EP * n + k
                        mm(banks[4 + t][:, D + P * k:D + P * (k + 1)], ha[:, 512 * m + P * t:512 * m + P * (t + 1)],
                           c("ew3", lo=P * k, n=P), start=True, stop=True)
                    mm(banks[4 + t][:, 0:D], gtt[:, 512 * n + P * t:512 * n + P * (t + 1)],
                       c("eb3", slice(64, 70)), start=True, stop=True).then_inc(e3_mm, 1)

            for m in range(NM + 1):
                if m < NM:
                    if m >= 2:
                        pe.wait_ge(e1_act, m - 1)
                    mm(banks[m % 2][:, :], c("ew1", slice(0, 64), lo=P * (m % EP), n=P), cols(m // EP),
                       start=True, stop=True).then_inc(e1_mm, 1)
                if m:
                    pe.wait_ge(e1_act, m)
                    if m >= 3:
                        pe.wait_ge(e2_act, m - 2)
                    mm(banks[2 + (m - 1) % 2][:, :], c("ew2", lo=P * ((m - 1) % EP), n=P), hr[(m - 1) % 4],
                       start=True, stop=True).then_inc(e2_mm, 1)
                if m == 15:
                    gates_to_rows()
                if m > 15 and m % 3 != 0:
                    n = 2 * (m // 3 - 5) + m % 3 - 1
                    outputs(n)
            pe.wait_ge(e2_act, NM)
            outputs(8)


def spectra():
    th = 2 * np.pi / X
    x = np.arange(X)
    ky = np.arange(KY)
    kx = np.concatenate([np.arange(16), np.arange(48, 64)])
    dft_y = np.zeros((2, Y, 2, 2, KY))
    ang = th * np.outer(x, ky)
    for i in range(2):
        dft_y[i, :, i, 0] = np.cos(ang)
        dft_y[i, :, i, 1] = -np.sin(ang)
    ax = th * np.outer(x, kx)
    cs, sn = np.cos(ax), np.sin(ax)
    fwd = np.zeros((X, 2, 2, KX, 2))
    fwd[:, 0, 0, :, 0], fwd[:, 1, 0, :, 0] = cs, sn
    fwd[:, 0, 0, :, 1], fwd[:, 1, 0, :, 1] = -sn, cs
    fwd[:, :, 1, :, 0], fwd[:, :, 1, :, 1] = -fwd[:, :, 0, :, 1], fwd[:, :, 0, :, 0]
    dft_x = fwd.reshape(16, 4, 2, -1).transpose(1, 2, 0, 3).reshape(P, 128)
    inv = np.zeros((KX, 2, X, 2))
    inv[:, 0, :, 0], inv[:, 1, :, 0] = cs.T / X, -sn.T / X
    inv[:, 0, :, 1], inv[:, 1, :, 1] = sn.T / X, cs.T / X
    inv = inv.reshape(4, 8, 2, 16, 4, 2).transpose(1, 0, 2, 4, 5, 3).reshape(64, P)
    idft_y = np.zeros((4, 2, KY, 4, Y))
    wt = np.where(ky == 0, 1.0, 2.0)[:, None] / Y
    for i in range(4):
        idft_y[i, 0, :, i] = wt * np.cos(ang.T)
        idft_y[i, 1, :, i] = -wt * np.sin(ang.T)
    return dft_y.reshape(P, 64), dft_x, inv, idft_y.reshape(P, 256)


def kernel(**inputs):
    import concourse.bacc as bacc
    from concourse.bass_utils import run_bass_kernel_spmd

    a = {k: np.asarray(v) for k, v in inputs.items()}
    tk = {k[7:]: v for k, v in a.items() if k.startswith("L0_tok_")}
    tx = {k[7:]: v for k, v in a.items() if k.startswith("L0_txt_")}
    at = {k[8:]: v for k, v in a.items() if k.startswith("L0_attn_")}
    ff = {k[7:]: v for k, v in a.items() if k.startswith("L0_ffn_")}
    f4 = np.float32
    csts = {tile: np.zeros((P, w), f4) for tile, w in WIDTH.items()}

    def put(name, v, row=0, col=0):
        v = v.reshape(v.shape[0], -1)
        tile, lo, _ = AT[name]
        lo += col
        csts[tile][row:row + v.shape[0], lo:lo + v.shape[1]] = v

    dft_y, dft_x, idft_x, idft_y = spectra()
    put("ident", np.eye(P, dtype=f4))
    put("dft_y", dft_y.astype(f4)); put("dft_x", dft_x.astype(f4))
    put("idft_x", idft_x.astype(f4)); put("idft_x", idft_x.astype(f4), 64, P)
    put("idft_y", idft_y.astype(f4))
    for b2 in range(2):
        r = 64 * b2
        put("fc0", tk["fc0_w"], 3 * b2, r)
        put("fc0_b", tk["fc0_b"][:, None], r)
        put("fc1", tk["fc1_w"], r, P * b2)
        for e in range(4):
            t = 2 * e + b2
            if t < 7:
                put("cw1", tx["w1"][:, :, t].T, r, P * e)
        put("vocab", np.arange(64, dtype=f4)[:, None], r)
        put("agd", np.stack([at["A_diag"], at["G_diag"], at["dt"]], 1), r)
        put("eye2", np.eye(64, dtype=f4), r)
        for t in range(3):
            put("cw3", tx["w3"][0, :, t:t + 1], r, 2 * t + b2)
        for k in range(EP):
            e = 2 * k + b2
            put("ew1", ff["expert_w1"][e], 0, P * k + r)
            put("eb1", ff["expert_b1"][e][:, None], r, k)
            put("ew2", ff["expert_w2"][e], r, P * k + r)
            put("eb2", ff["expert_b2"][e][:, None], r, k)
            put("ew3", ff["expert_w3"][e], r, P * k + r)
    put("fc1_b", tk["fc1_b"][:, None]); put("fc2", tk["fc2_w"], 0, 7)
    put("fc2_b", np.broadcast_to(tk["fc2_b"][None], (P, 1)))
    put("cb1", tx["b1"][:, None]); put("cb2", np.tile(tx["b2"][:, None], (2, 1)))
    put("cw2", tx["w2"].transpose(1, 2, 0)); 
    put("cb3", np.broadcast_to(tx["b3"][None], (P, 1)))
    put("emb", np.concatenate([tx["emb"], tx["locality_shapes"]], 1))
    put("bytepos", np.linspace(0.0, 1.0, S, dtype=f4).reshape(ST, P).T)
    put("widths", np.broadcast_to(tx["multiscale_widths"][None], (P, SCALES)))
    put("swts", np.broadcast_to(tx["scale_weights"][None], (P, SCALES)))
    put("bmat", at["Bmat"][:, :, 0].T, 0, 0); put("bmat", at["Bmat"][:, :, 1].T, 0, P)
    put("cmat", at["Cmat"][:, :, 0].T, 64, 0); put("cmat", at["Cmat"][:, :, 1].T, 64, 64)
    put("dvec", np.broadcast_to(at["D"][None], (P, D)))
    put("rw1", ff["router_w1"]); put("rb1", np.tile(ff["router_b1"][:, None], (4, 1)))
    for q in range(4):
        put("rw2", ff["router_w2"], 32 * q, E * q)
    put("rb2", np.broadcast_to(ff["router_b2"][None], (P, E)))
    put("eb3", ff["expert_b3"], 64)
    lc = np.zeros((LAYERS, P, 131), f4)
    for b2 in range(2):
        r = slice(64 * b2, 64 * b2 + 64)
        lc[:, r, r] = tk["pw_w"].transpose(0, 2, 1)
        lc[:, r, 128], lc[:, r, 129], lc[:, r, 130] = tk["pw_b"], tk["gamma"], tk["beta"]
    wre = np.concatenate([tk["w1r"], tk["w2r"]], 3)
    wim = np.concatenate([tk["w1i"], tk["w2i"]], 3)
    ws = np.stack([wre, wim], 1).transpose(0, 5, 1, 2, 4, 3).reshape(LAYERS * KY, P, 4, 2, 4, C)
    ws = ws.transpose(0, 3, 1, 4, 2, 5).reshape(LAYERS * KY * 2, P, WC)
    xs = a["x"].reshape(BP, 2, PX, 3).transpose(0, 1, 3, 2).reshape(BP, 6, PX)
    arrays = {"xs": xs, "toks": a["x_txt"], "pos": a["fside_BS_continuous_positions"],
              "cmain": csts["main"], "ctext": csts["text"], "ctail": csts["tail"], "lconst": lc, "wspec": ws}
    arrays = {k: np.ascontiguousarray(v) for k, v in arrays.items()}
    nc = bacc.Bacc("TRN2", target_bir_lowering=False, num_devices=1)
    args = [nc.dram_tensor(k, v.shape, mybir.dt.from_np(v.dtype), kind="ExternalInput").ap() for k, v in arrays.items()]
    out = nc.dram_tensor("out", (B, L, D), F32, kind="ExternalOutput").ap()
    build_program(nc, *args, out)
    r = run_bass_kernel_spmd(nc, [arrays], core_ids=[0])
    return r.results[0]["out"]
```
